# Optimizing a Trainium2 kernel written in Bass

```python
import numpy as np
import jax
import jax.numpy as jnp

def _softmax(x, axis=-1):
    return jax.nn.softmax(x, axis=axis)

def _gelu(x):
    return jax.nn.gelu(x, approximate=True)

def _silu(x):
    return jax.nn.silu(x)

def _sigmoid(x):
    return jax.nn.sigmoid(x)

def _layernorm(x, axis=-1, eps=1e-05):
    m = jnp.mean(x, axis=axis, keepdims=True)
    v = jnp.var(x, axis=axis, keepdims=True)
    return (x - m) / jnp.sqrt(v + eps)

def _scatter_add(tgt, idx, src, axis=0):
    return tgt.at[idx].add(src)

def _segment_sum(src, seg, n):
    return jax.ops.segment_sum(src, seg, n)
kernel_name = 'mk_xattn_ffn_d1_seqx_r8_cf76dd'

def setup_inputs(seed: int=0):
    np.random.seed(seed)
    _w = jnp.asarray

    def _rec_inputs():
        import jax
        import jax.numpy as jnp
        _rk = jax.random.key(seed)
        x = -4.161e-06 + 1 * jax.random.normal(jax.random.fold_in(_rk, 1), (64, 64, 256), jnp.float32)
        _lenS = 64 - jax.random.randint(jax.random.fold_in(_rk, 7), (64,), 0, max(1, 64 // 4) + 1, jnp.int32)
        _lenS2 = 64 - jax.random.randint(jax.random.fold_in(_rk, 8), (64,), 0, max(1, 64 // 4) + 1, jnp.int32)
        _ctx_2048P = jax.random.normal(jax.random.fold_in(_rk, 11), (64, 16, 256), jnp.float32)
        _ctx_2048c = jax.random.dirichlet(jax.random.fold_in(_rk, 511), 0.3 * jnp.ones((16,), jnp.float32), (64, 64))
        _ctx_2048t = jnp.einsum('bsk,bkd->bsd', _ctx_2048c, _ctx_2048P)
        _ctx_2048t = _ctx_2048t * jax.lax.rsqrt(jnp.mean(jnp.square(_ctx_2048t)) + 1e-12) * 0.953939
        ctx_2048 = -0.000192764 + 0.999654 * (_ctx_2048t + 0.3 * jax.random.normal(jax.random.fold_in(_rk, 611), (64, 64, 256), jnp.float32))
        return (x, ctx_2048)
    x, ctx_2048 = _rec_inputs()

    def _L0_xattn_setup():
        import jax, jax.numpy as jnp
        import numpy as np
        FP8_MAX = 448.0
        EPS = 1e-05

        def _fp8_roundtrip(x):
            return x.astype(jnp.float8_e4m3fn).astype(jnp.float32)

        def _div_clamp_fp8(x, scale):
            y = jnp.clip(x.astype(jnp.float32) / scale, -FP8_MAX, FP8_MAX)
            y = y.astype(jnp.bfloat16).astype(jnp.float32)
            return _fp8_roundtrip(y)

        def _ln(x, w, b):
            mu = jnp.mean(x, axis=-1, keepdims=True)
            var = jnp.mean(jnp.square(x - mu), axis=-1, keepdims=True)
            return (x - mu) * jax.lax.rsqrt(var + EPS) * w + b

        def _fp8_linear_pertensor(x, wq, w_scale, in_scale):
            xq = _div_clamp_fp8(x, in_scale)
            return jnp.einsum('bsi,oi->bso', xq * in_scale, wq) * w_scale

        def _gqa(q, k, v):
            scale = 1.0 / np.sqrt(q.shape[-1])
            scores = jnp.einsum('bsghd,btgd->bghst', q, k) * scale
            p = jax.nn.softmax(scores, axis=-1)
            return jnp.einsum('bghst,btgd->bsghd', p, v)
        key = jax.random.key(seed)
        ks = jax.random.split(key, 8)
        B, S, SC, H, NH, G, D = (2, 256, 64, 256, 16, 8, 128)

        def qw(k, out_f, in_f):
            w = jax.random.normal(k, (out_f, in_f), jnp.float32) * 0.02
            sc = jnp.max(jnp.abs(w)) / FP8_MAX
            return (_fp8_roundtrip(w / sc), sc.astype(jnp.float32))
        wq, wq_s = qw(ks[0], NH * D, H)
        wqx, wqx_s = qw(ks[1], NH * D, H)
        wk, wk_s = qw(ks[2], G * D, H)
        wv, wv_s = qw(ks[3], G * D, H)
        wproj, wp_s = qw(ks[4], H, 2 * NH * D)
        return {'hidden_states': jax.random.normal(ks[5], (B, S, H), jnp.float32), 'cond': jax.random.normal(ks[6], (B, SC, H), jnp.float32), 'ln_w': jnp.ones((H,), jnp.float32), 'ln_b': jnp.zeros((H,), jnp.float32), 'wq': wq, 'wq_scale': wq_s, 'q_in_scale': jnp.full((H,), 0.05, jnp.float32), 'wqx': wqx, 'wqx_scale': wqx_s, 'qx_in_scale': jnp.full((H,), 0.05, jnp.float32), 'wk': wk, 'wk_scale': wk_s, 'k_in_scale': jnp.full((H,), 0.05, jnp.float32), 'wv': wv, 'wv_scale': wv_s, 'v_in_scale': jnp.full((H,), 0.05, jnp.float32), 'w_kv_x': jax.random.normal(ks[7], (2 * G * D, H), jnp.float32) * 0.02, 'qln_w': jnp.ones((D,), jnp.float32), 'qln_b': jnp.zeros((D,), jnp.float32), 'kln_w': jnp.ones((D,), jnp.float32), 'kln_b': jnp.zeros((D,), jnp.float32), 'qxln_w': jnp.ones((D,), jnp.float32), 'qxln_b': jnp.zeros((D,), jnp.float32), 'kxln_w': jnp.ones((D,), jnp.float32), 'kxln_b': jnp.zeros((D,), jnp.float32), 'wproj': wproj, 'proj_w_scale': wp_s, 'proj_in_scale': jnp.asarray(0.05, jnp.float32), 'proj_smooth': jnp.full((2 * NH * D,), 0.05, jnp.float32)}
    _L0_xattn_all = _L0_xattn_setup()
    _L0_xattn_in = {k: v for k, v in _L0_xattn_all.items() if k in ('ln_w', 'ln_b', 'wq', 'wq_scale', 'q_in_scale', 'wqx', 'wqx_scale', 'qx_in_scale', 'wk', 'wk_scale', 'k_in_scale', 'wv', 'wv_scale', 'v_in_scale', 'w_kv_x', 'qln_w', 'qln_b', 'kln_w', 'kln_b', 'qxln_w', 'qxln_b', 'kxln_w', 'kxln_b', 'wproj', 'proj_w_scale', 'proj_in_scale', 'proj_smooth')}
    del _L0_xattn_all

    def _L0_ffn_setup():
        import jax, jax.numpy as jnp
        import numpy as np
        B, S, H = (2, 256, 256)
        E, I, K = (8, 176, 2)
        SHARED_I = 176 * 2

        def _moe_forward(hidden_states, gate_w, w1, w3, w2, sw1, sw3, sw2):
            x = hidden_states.reshape(-1, H)
            T = x.shape[0]
            logits = x @ gate_w.T
            scores = jax.nn.softmax(logits, axis=-1)
            topk_w, topk_idx = jax.lax.top_k(scores, K)
            topk_w = topk_w / jnp.sum(topk_w, axis=-1, keepdims=True)
            h = jnp.einsum('th,ehi->eti', x, w1)
            g = jnp.einsum('th,ehi->eti', x, w3)
            y_all = jnp.einsum('eti,eih->eth', jax.nn.silu(h) * g, w2)
            tok = jnp.arange(T)[:, None]
            y_sel = y_all[topk_idx, tok]
            y = jnp.sum(y_sel * topk_w[..., None], axis=1)
            shared = jax.nn.silu(x @ sw1) * (x @ sw3) @ sw2
            return (y + shared).reshape(hidden_states.shape)
        key = jax.random.key(seed)
        ks = jax.random.split(key, 8)
        s = 0.02
        return {'hidden_states': jax.random.normal(ks[0], (B, S, H), jnp.float32), 'gate_w': jax.random.normal(ks[1], (E, H), jnp.float32) * s, 'w1': jax.random.normal(ks[2], (E, H, I), jnp.float32) * s, 'w3': jax.random.normal(ks[3], (E, H, I), jnp.float32) * s, 'w2': jax.random.normal(ks[4], (E, I, H), jnp.float32) * s, 'sw1': jax.random.normal(ks[5], (H, SHARED_I), jnp.float32) * s, 'sw3': jax.random.normal(ks[6], (H, SHARED_I), jnp.float32) * s, 'sw2': jax.random.normal(ks[7], (SHARED_I, H), jnp.float32) * s}
    _L0_ffn_all = _L0_ffn_setup()
    _L0_ffn_in = {k: v for k, v in _L0_ffn_all.items() if k in ('gate_w', 'w1', 'w3', 'w2', 'sw1', 'sw3', 'sw2')}
    del _L0_ffn_all
    return {'x': x, 'ctx_2048': ctx_2048, 'L0_xattn_ln_w': _L0_xattn_in['ln_w'], 'L0_xattn_ln_b': _L0_xattn_in['ln_b'], 'L0_xattn_wq': _L0_xattn_in['wq'], 'L0_xattn_wq_scale': _L0_xattn_in['wq_scale'], 'L0_xattn_q_in_scale': _L0_xattn_in['q_in_scale'], 'L0_xattn_wqx': _L0_xattn_in['wqx'], 'L0_xattn_wqx_scale': _L0_xattn_in['wqx_scale'], 'L0_xattn_qx_in_scale': _L0_xattn_in['qx_in_scale'], 'L0_xattn_wk': _L0_xattn_in['wk'], 'L0_xattn_wk_scale': _L0_xattn_in['wk_scale'], 'L0_xattn_k_in_scale': _L0_xattn_in['k_in_scale'], 'L0_xattn_wv': _L0_xattn_in['wv'], 'L0_xattn_wv_scale': _L0_xattn_in['wv_scale'], 'L0_xattn_v_in_scale': _L0_xattn_in['v_in_scale'], 'L0_xattn_w_kv_x': _L0_xattn_in['w_kv_x'], 'L0_xattn_qln_w': _L0_xattn_in['qln_w'], 'L0_xattn_qln_b': _L0_xattn_in['qln_b'], 'L0_xattn_kln_w': _L0_xattn_in['kln_w'], 'L0_xattn_kln_b': _L0_xattn_in['kln_b'], 'L0_xattn_qxln_w': _L0_xattn_in['qxln_w'], 'L0_xattn_qxln_b': _L0_xattn_in['qxln_b'], 'L0_xattn_kxln_w': _L0_xattn_in['kxln_w'], 'L0_xattn_kxln_b': _L0_xattn_in['kxln_b'], 'L0_xattn_wproj': _L0_xattn_in['wproj'], 'L0_xattn_proj_w_scale': _L0_xattn_in['proj_w_scale'], 'L0_xattn_proj_in_scale': _L0_xattn_in['proj_in_scale'], 'L0_xattn_proj_smooth': _L0_xattn_in['proj_smooth'], 'L0_ffn_gate_w': _L0_ffn_in['gate_w'], 'L0_ffn_w1': _L0_ffn_in['w1'], 'L0_ffn_w3': _L0_ffn_in['w3'], 'L0_ffn_w2': _L0_ffn_in['w2'], 'L0_ffn_sw1': _L0_ffn_in['sw1'], 'L0_ffn_sw3': _L0_ffn_in['sw3'], 'L0_ffn_sw2': _L0_ffn_in['sw2']}

def reference(x, ctx_2048, L0_xattn_ln_w, L0_xattn_ln_b, L0_xattn_wq, L0_xattn_wq_scale, L0_xattn_q_in_scale, L0_xattn_wqx, L0_xattn_wqx_scale, L0_xattn_qx_in_scale, L0_xattn_wk, L0_xattn_wk_scale, L0_xattn_k_in_scale, L0_xattn_wv, L0_xattn_wv_scale, L0_xattn_v_in_scale, L0_xattn_w_kv_x, L0_xattn_qln_w, L0_xattn_qln_b, L0_xattn_kln_w, L0_xattn_kln_b, L0_xattn_qxln_w, L0_xattn_qxln_b, L0_xattn_kxln_w, L0_xattn_kxln_b, L0_xattn_wproj, L0_xattn_proj_w_scale, L0_xattn_proj_in_scale, L0_xattn_proj_smooth, L0_ffn_gate_w, L0_ffn_w1, L0_ffn_w3, L0_ffn_w2, L0_ffn_sw1, L0_ffn_sw3, L0_ffn_sw2):
    import jax
    import jax.numpy as jnp

    def _L0_xattn_ref(hidden_states, cond, ln_w, ln_b, wq, wq_scale, q_in_scale, wqx, wqx_scale, qx_in_scale, wk, wk_scale, k_in_scale, wv, wv_scale, v_in_scale, w_kv_x, qln_w, qln_b, kln_w, kln_b, qxln_w, qxln_b, kxln_w, kxln_b, wproj, proj_w_scale, proj_in_scale, proj_smooth):
        import jax, jax.numpy as jnp
        import numpy as np
        FP8_MAX = 448.0
        EPS = 1e-05

        def _fp8_roundtrip(x):
            return x.astype(jnp.float8_e4m3fn).astype(jnp.float32)

        def _div_clamp_fp8(x, scale):
            y = jnp.clip(x.astype(jnp.float32) / scale, -FP8_MAX, FP8_MAX)
            y = y.astype(jnp.bfloat16).astype(jnp.float32)
            return _fp8_roundtrip(y)

        def _ln(x, w, b):
            mu = jnp.mean(x, axis=-1, keepdims=True)
            var = jnp.mean(jnp.square(x - mu), axis=-1, keepdims=True)
            return (x - mu) * jax.lax.rsqrt(var + EPS) * w + b

        def _fp8_linear_pertensor(x, wq, w_scale, in_scale):
            xq = _div_clamp_fp8(x, in_scale)
            return jnp.einsum('bsi,oi->bso', xq * in_scale, wq) * w_scale

        def _gqa(q, k, v):
            scale = 1.0 / np.sqrt(q.shape[-1])
            scores = jnp.einsum('bsghd,btgd->bghst', q, k) * scale
            p = jax.nn.softmax(scores, axis=-1)
            return jnp.einsum('bghst,btgd->bsghd', p, v)
        b, s, _ = hidden_states.shape
        sc = cond.shape[1]
        d = qln_w.shape[0]
        nh = wq.shape[0] // d
        g = wk.shape[0] // d
        hpg = nh // g
        ln_out = _ln(hidden_states, ln_w, ln_b)
        q = _fp8_linear_pertensor(ln_out, wq, wq_scale, q_in_scale).reshape(b, s, g, hpg, d)
        q = _ln(q, qln_w, qln_b)
        k = _fp8_linear_pertensor(ln_out, wk, wk_scale, k_in_scale).reshape(b, s, g, d)
        k = _ln(k, kln_w, kln_b)
        v = _fp8_linear_pertensor(ln_out, wv, wv_scale, v_in_scale).reshape(b, s, g, d)
        core = _gqa(q, k, v).reshape(b, s, nh * d)
        qx = _fp8_linear_pertensor(ln_out, wqx, wqx_scale, qx_in_scale).reshape(b, s, g, hpg, d)
        qx = _ln(qx, qxln_w, qxln_b)
        kvx = jnp.einsum('bsi,oi->bso', cond, w_kv_x)
        kx, vx = jnp.split(kvx, 2, axis=-1)
        kx = _ln(kx.reshape(b, sc, g, d), kxln_w, kxln_b)
        vx = vx.reshape(b, sc, g, d)
        xout = _gqa(qx, kx, vx).reshape(b, s, nh * d)
        cat = jnp.concatenate([core, xout], axis=-1)
        catq = _div_clamp_fp8(cat, proj_smooth)
        return jnp.einsum('bsi,oi->bso', catq, wproj) * (proj_in_scale * proj_w_scale)

    def _L0_ffn_ref(hidden_states, gate_w, w1, w3, w2, sw1, sw3, sw2):
        import jax, jax.numpy as jnp
        import numpy as np
        B, S, H = (2, 256, 256)
        E, I, K = (8, 176, 2)
        SHARED_I = 176 * 2

        def _moe_forward(hidden_states, gate_w, w1, w3, w2, sw1, sw3, sw2):
            x = hidden_states.reshape(-1, H)
            T = x.shape[0]
            logits = x @ gate_w.T
            scores = jax.nn.softmax(logits, axis=-1)
            topk_w, topk_idx = jax.lax.top_k(scores, K)
            topk_w = topk_w / jnp.sum(topk_w, axis=-1, keepdims=True)
            h = jnp.einsum('th,ehi->eti', x, w1)
            g = jnp.einsum('th,ehi->eti', x, w3)
            y_all = jnp.einsum('eti,eih->eth', jax.nn.silu(h) * g, w2)
            tok = jnp.arange(T)[:, None]
            y_sel = y_all[topk_idx, tok]
            y = jnp.sum(y_sel * topk_w[..., None], axis=1)
            shared = jax.nn.silu(x @ sw1) * (x @ sw3) @ sw2
            return (y + shared).reshape(hidden_states.shape)
        return _moe_forward(hidden_states, gate_w, w1, w3, w2, sw1, sw3, sw2)
    x = x + _L0_xattn_ref(_layernorm(x, axis=-1), ctx_2048, L0_xattn_ln_w, L0_xattn_ln_b, L0_xattn_wq, L0_xattn_wq_scale, L0_xattn_q_in_scale, L0_xattn_wqx, L0_xattn_wqx_scale, L0_xattn_qx_in_scale, L0_xattn_wk, L0_xattn_wk_scale, L0_xattn_k_in_scale, L0_xattn_wv, L0_xattn_wv_scale, L0_xattn_v_in_scale, L0_xattn_w_kv_x, L0_xattn_qln_w, L0_xattn_qln_b, L0_xattn_kln_w, L0_xattn_kln_b, L0_xattn_qxln_w, L0_xattn_qxln_b, L0_xattn_kxln_w, L0_xattn_kxln_b, L0_xattn_wproj, L0_xattn_proj_w_scale, L0_xattn_proj_in_scale, L0_xattn_proj_smooth)
    x = x + _L0_ffn_ref(_layernorm(x, axis=-1), L0_ffn_gate_w, L0_ffn_w1, L0_ffn_w3, L0_ffn_w2, L0_ffn_sw1, L0_ffn_sw3, L0_ffn_sw2)
    return x

_drawn_inputs = setup_inputs


def setup_inputs(seed=0):
    import zlib

    import numpy as np

    out = dict(_drawn_inputs(seed))
    spreads = {'L0_xattn_ln_w': (1.0, 0.561),
     'L0_xattn_ln_b': (0.0, 0.1),
     'L0_xattn_q_in_scale': (0.05000000074505806, 0.6),
     'L0_xattn_qx_in_scale': (0.05000000074505806, 0.6),
     'L0_xattn_k_in_scale': (0.05000000074505806, 0.6),
     'L0_xattn_v_in_scale': (0.05000000074505806, 0.6),
     'L0_xattn_qln_w': (1.0, 0.6),
     'L0_xattn_qln_b': (0.0, 0.8),
     'L0_xattn_kln_w': (1.0, 0.6),
     'L0_xattn_kln_b': (0.0, 0.8),
     'L0_xattn_qxln_w': (1.0, 0.6),
     'L0_xattn_qxln_b': (0.0, 0.8),
     'L0_xattn_kxln_w': (1.0, 0.6),
     'L0_xattn_kxln_b': (0.0, 0.8),
     'L0_xattn_proj_smooth': (0.05000000074505806, 0.2)}
    factors = {'L0_ffn_gate_w': 6.627,
     'L0_ffn_w1': 5.84,
     'L0_ffn_w3': 5.771,
     'L0_ffn_w2': 5.763,
     'L0_ffn_sw1': 2.931,
     'L0_ffn_sw3': 2.902,
     'L0_ffn_sw2': 2.9}
    for name, (base, spread) in spreads.items():
        noise = np.random.default_rng([zlib.crc32(name.encode()), seed]).standard_normal(out[name].shape)
        drawn = base * np.exp(spread * noise) if base else spread * noise
        out[name] = jnp.asarray(drawn.astype(out[name].dtype))
    for name, factor in factors.items():
        out[name] = (out[name] * factor).astype(out[name].dtype)
    return out
```

```python
from contextlib import ExitStack

import concourse.bass as bass
from concourse import mybir

F32 = mybir.dt.float32
F16 = mybir.dt.float16
BF16 = mybir.dt.bfloat16
U16 = mybir.dt.uint16
ALU = mybir.AluOpType
ACT = mybir.ActivationFunctionType
AX = mybir.AxisListType
RMAX = bass.bass_isa.ReduceOp.max

P = 128
H = 256
KC = H // P
NH, G = 16, 8
E, I, SI = 8, 176, 352
NE = E + SI // I
FI = NE * I
NU = -(-FI // 256)
NB = -(-FI // 512)
BLK = 512
TILES = 32
QUADS = 4 * TILES
EPS = 1e-5
FP8_MAX = 448.0
TOP = 1024.0
SCALE = float(P) ** -0.5
FP8_MIN_NORMAL = 2.0 ** -6
ROUND3 = 24.0

V_IN, V_LNW, V_LNB = 0, 8, 10
V_QLN, V_KLN, V_QXLN, V_KXLN = 12, 14, 16, 18
V_SMOOTH, V_WS, V_PW, V_PI = 20, 52, 56, 57
NV = 58

TQ, TK, TV, TX = range(4)
ATTN_BLOCKS = ([(TQ, 0, 512 * b, True) for b in range(4)] + [(TK, 1, 512 * b, True) for b in range(2)]
               + [(TV, 2, 512 * b, False) for b in range(2)] + [(TX, 3, 512 * b, True) for b in range(4)])
NA = len(ATTN_BLOCKS)
UNITS = {0: ((0, 1), (2,)), 1: ((3,), (4,)), 2: ((5,), (6,))}


def back(t, j, d):
    return t + (j - d) // 4, (j - d) % 4


def bass_xattn_moe(nc, x, cond, wqT, wkT, wvT, wqxT, wkvT, wprojT, w1T, w3T, w2, gateT, vecs, out):
    es = ExitStack()
    with es:
        def sb(name, shape, dt=F32):
            return es.enter_context(nc.sbuf_tensor(name, shape, dt))

        def sem(name):
            return es.enter_context(nc.semaphore(name))

        w_attn = sb("w_attn", [P, NA, 2, KC, BLK], F16)
        w_kv = sb("w_kv", [P, KC, 2048])
        w_proj = sb("w_proj", [P, 32, H], BF16)
        w_up = sb("w_up", [P, NU, 2, 2, KC, 256], F16)
        w_down = sb("w_down", [P, 2 * NU, H])
        w_gate = sb("w_gate", [P, KC, E])
        vec = sb("vec", [P, NV])
        ident = sb("ident", [P, P])
        expert_rows = sb("expert_rows", [P, 2 * NU * P])
        tri = sb("tri", [P, E, E])
        minus_half = sb("minus_half", [P, 12])
        inv_in = sb("inv_in", [P, 8])
        inv_smooth = sb("inv_smooth", [P, 32])
        ln_scale = sb("ln_scale", [P, 4])
        eps_head = sb("eps_head", [P, 4, 12])
        out_scale = sb("out_scale", [P, 1])
        absmax = sb("absmax", [P, NA + 2 * NB, KC])
        rowmax = sb("rowmax", [P, NA + 2 * NB])
        peak = sb("peak", [P, NA + 2 * NB])
        factor = sb("factor", [P, NA + 2 * NB, KC])
        headsum = sb("headsum", [P, 2, 8])
        sigma = sb("sigma", [P, NA])
        isig = sb("isig", [P, NA])
        eps_blk = sb("eps_blk", [P, NA])
        half_up = sb("half_up", [P, NB])
        both_up = sb("both_up", [P, NB])

        xin = sb("xin", [P, H])
        cin = sb("cin", [P, H])
        xres = sb("xres", [P, H])
        ln_stat = sb("ln_stat", [P, 6])
        ln_mv = sb("ln_mv", [P, 2])
        ln_r = sb("ln_r", [P, 1])
        yln = sb("yln", [P, H])
        zln = sb("zln", [P, H])
        zT = sb("zT", [P, KC, P])
        condT = sb("condT", [P, KC, P])
        xs = sb("xs", [P, 4, KC, P], BF16)
        xm = sb("xm", [P, 4, KC, P], BF16)
        xq = sb("xq", [P, 4, KC, P], BF16)

        raw = sb("raw", [P, 2, 12, P])
        stats = sb("stats", [P, 2, 12, 6])
        st_a = sb("st_a", [P, 12])
        st_b = sb("st_b", [P, 12])
        rstd = sb("rstd", [P, 2, 12])
        qkT = sb("qkT", [P, 12, P])
        vals = sb("vals", [P, 4, BLK])
        smax = sb("smax", [P, 8])
        shifted = sb("shifted", [P, 8, 64])
        ex = sb("ex", [P, 8, 64])
        rsum = sb("rsum", [P, 8])
        rinv = sb("rinv", [P, 8])
        probs = sb("probs", [P, 4, P])
        pT = sb("pT", [P, 4, 2, P])
        cat = sb("cat", [P, 8, P], BF16)
        catm = sb("catm", [P, 8, P], BF16)
        catq = sb("catq", [P, 8, P], BF16)

        x1 = sb("x1", [P, H])
        x1keep = sb("x1keep", [P, H])
        f_stat = sb("f_stat", [P, 6])
        f_mv = sb("f_mv", [P, 2])
        f_r = sb("f_r", [P, 1])
        xn = sb("xn", [P, H])
        xnT = sb("xnT", [P, KC, P])
        xnp = sb("xnp", [P, 2, KC, P], F16)
        g_col = sb("g_col", [P, 8])
        g_sh = sb("g_sh", [P, E])
        g_ex = sb("g_ex", [P, E])
        g_sc = sb("g_sc", [P, E])
        g_gt = sb("g_gt", [P, E, E])
        g_eq = sb("g_eq", [P, E, E])
        g_rank = sb("g_rank", [P, E])
        g_sel = sb("g_sel", [P, E])
        comb = sb("comb", [P, P])
        combT = sb("combT", [P, P])
        combs = sb("combs", [P, 2 * NU, P])
        th = sb("th", [P, 2, P])
        gu = sb("gu", [P, 2, P])
        act_ff = sb("act_ff", [P, 2, 2, P])
        yout = sb("yout", [P, H])

        bank = [es.enter_context(nc.psum_tensor(f"bank{i}", [P, 512], F32)) for i in range(8)]
        P_BANK, T_BANK, S_BANK, V_BANK, H_BANK, Y_BANK = (0, 1), (2, 3), 4, 5, 6, 7

        stage = [v.rearrange("p a b -> p (a b)") for v in (raw[:, 0, 0:8, :], raw[:, 1, 0:8, :], combs[:, 0:8, :])]

        s_vec, s_wkv, s_wd, s_wg = sem("vec_in"), sem("wkv_in"), sem("wdown_in"), sem("wgate_in")
        s_wp = [sem(f"wproj_in{i}") for i in range(2)]
        s_stage = [sem(f"stage_in{i}") for i in range(3)]
        prep_centred, prep_max, prep_scaled = sem("prep_centred"), sem("prep_max"), sem("prep_scaled")
        fac_step = sem("fac_step")
        peak_step = sem("peak_step")
        factor_ready = sem("factor_ready")
        high_done = sem("high_done")
        low_done = sem("low_done")
        wproj_cast = sem("wproj_cast")
        const_step = sem("const_step")
        tab_step = sem("tab_step")
        pad_zeroed = sem("pad_zeroed")
        apart = sem("apart")
        x_in, c_in, r_in, out_sent = sem("x_in"), sem("cond_in"), sem("res_in"), sem("out_sent")
        z_transposed, c_transposed = sem("z_transposed"), sem("cond_transposed")
        proj_done, qk_transposed, scores_done = sem("proj_done"), sem("qk_transposed"), sem("scores_done")
        p_transposed, pv_done, o_done = sem("p_transposed"), sem("pv_done"), sem("o_done")
        xn_transposed, gate_done, comb_transposed = sem("xn_transposed"), sem("gate_done"), sem("comb_transposed")
        spread_done, up_done, down_done = sem("spread_done"), sem("up_done"), sem("down_done")
        zT_ready, condT_ready, raw_ready, v_ready = sem("zT_ready"), sem("condT_ready"), sem("raw_ready"), sem("v_ready")
        qkT_ready, exp_done, pT_ready, cat_scaled = sem("qkT_ready"), sem("exp_done"), sem("pT_ready"), sem("cat_scaled")
        xnT_ready, gexp_done, combT_ready = sem("xnT_ready"), sem("gate_exp_done"), sem("combT_ready")
        combs_ready, tanh_done = sem("combs_ready"), sem("tanh_done")
        ln1_step, xqkv_step, xx_step = sem("ln1_step"), sem("xqkv_step"), sem("xx_step")
        stats_done, xhat_ready, soft_step, quant_step = sem("stats_done"), sem("xhat_ready"), sem("soft_step"), sem("quant_step")
        o_added, ln2_step, parts_step, gate_step = sem("o_added"), sem("ln2_step"), sem("parts_step"), sem("gate_step")
        gated, out_ready = sem("gated"), sem("out_ready")
        ln1_pow, ln2_pow, rstd_step, p_ready = sem("ln1_pow"), sem("ln2_pow"), sem("rstd_step"), sem("p_ready")
        x1_kept, act_ready = sem("x1_kept"), sem("act_ready")

        def after(eng, s, per, t, k):
            if not isinstance(t, int):
                eng.wait_ge(s, per * t + k)
            elif per * t + k > 0:
                eng.wait_ge(s, min(per * t + k, per * TILES))

        def after_apart(eng, s, per, t, k):
            after(eng, s, per, t, k)
            eng.sem_inc(apart, 1)

        def has(t, j=0):
            return not isinstance(t, int) or 0 <= 4 * t + j < QUADS

        def ffn(t):
            return not isinstance(t, int) or 0 <= t < TILES

        def run(eng, step):
            for j in (0, 1, 2, 3):
                step(-1, j)
            for t in (0, 1, 2):
                for j in range(4):
                    step(t, j)
            with eng.Fori(3, TILES - 1) as t:
                for j in range(4):
                    step(t, j)
            for t in (TILES - 1, TILES, TILES + 1):
                for j in range(4):
                    step(t, j)

        sources = (wqT, wkT, wvT, wqxT)
        items = []
        for b, (ty, w, c0, centred) in enumerate(ATTN_BLOCKS):
            items.append((sources[w][:, c0:c0 + BLK], BLK, centred, ty, b))
        for w, src in enumerate((w1T, w3T)):
            for b in range(NB):
                n = min(BLK, FI - BLK * b)
                items.append((src[:, BLK * b:BLK * b + n], n, False, None, (w, b)))
        NI = len(items)

        def parts(k, part, c):
            _, n, _, ty, d = items[k]
            if ty is not None:
                return [(w_attn[:, d, part, c, :], 0, BLK)]
            w, b = d
            return [(w_up[:, 2 * b + u, part, w, c, 0:min(256, n - 256 * u)], 256 * u, min(256, n - 256 * u))
                    for u in range(2) if n > 256 * u]

        def staged(k):
            n = items[k][1]
            return stage[k % 3][:, 0:KC * n].rearrange("p (c n) -> p c n", c=KC)

        block = es.enter_context(nc.Block())

        @block.sync
        def _(sp):
            sp.dma_start(vec[:, :], vecs).then_inc(s_vec, 16)
            for k in range(NI):
                if k >= 3:
                    sp.wait_ge(low_done, k - 2)
                sp.dma_start(staged(k), items[k][0].rearrange("(c p) n -> p c n", p=P)).then_inc(s_stage[k % 3], 16)
                if k == 2:
                    sp.dma_start(xin[:, :], x[0:P, :]).then_inc(x_in, 16)
                    sp.dma_start(cin[:, :], cond[0:P, :]).then_inc(c_in, 16)
                    sp.dma_start(xres[:, :], x[0:P, :]).then_inc(r_in, 16)
                    sp.dma_start(w_kv[:, :, :], wkvT.rearrange("(c p) n -> p c n", p=P)).then_inc(s_wkv, 16)
                if k == 12:
                    sp.dma_start(w_gate[:, :, :], gateT.rearrange("(c p) n -> p c n", p=P)).then_inc(s_wg, 16)
                    full = FI // P
                    sp.dma_start(w_down[:, 0:full, :], w2[0:full * P, :].rearrange("(c p) n -> p c n", p=P)).then_inc(s_wd, 16)
                    sp.dma_start(w_down[0:FI - full * P, full, :], w2[full * P:FI, :]).then_inc(s_wd, 16)
            for q in range(8):
                if q < 2:
                    sp.wait_ge(low_done, NI)
                else:
                    sp.wait_ge(wproj_cast, q - 1)
                sp.dma_start(stage[q % 2].rearrange("p (c n) -> p c n", n=H),
                             wprojT[512 * q:512 * q + 512, :].rearrange("(c p) n -> p c n", p=P)).then_inc(s_wp[q % 2], 16)

            def tile_loads(t):
                real = not isinstance(t, int)
                if real or t < TILES:
                    rows = x[bass.ts(t, P), :]
                    after(sp, c_transposed, 1, t - 1, 1)
                    sp.dma_start(cin[:, :], cond[bass.ts(t, P), :]).then_inc(c_in, 16)
                if real or t < TILES - 1:
                    after(sp, ln1_step, 6, t, 3)
                    sp.dma_start(xin[:, :], x[bass.ts(t + 1, P), :]).then_inc(x_in, 16)
                if real or t < TILES:
                    after(sp, o_added, 4, t - 1, 4)
                    sp.dma_start(xres[:, :], rows).then_inc(r_in, 16)
                if real or t >= 2:
                    after(sp, out_ready, 1, t - 2, 1)
                    sp.dma_start(out[bass.ts(t - 2, P), :], yout[:, :]).then_inc(out_sent, 16)

            sp.wait_ge(ln1_step, 3)
            sp.dma_start(xin[:, :], x[P:2 * P, :]).then_inc(x_in, 16)
            tile_loads(1)
            with sp.Fori(2, TILES - 1) as t:
                tile_loads(t)
            for t in (TILES - 1, TILES, TILES + 1):
                tile_loads(t)
            sp.wait_ge(out_sent, 16 * TILES)

        @block.gpsimd
        def _(pool):
            pool.memset(ident[:, :], 0.0).then_inc(const_step, 1)
            pool.memset(expert_rows[:, :], 1.0).then_inc(const_step, 1)
            pool.memset(tri[:, :, :], 1.0).then_inc(const_step, 1)
            pool.wait_ge(const_step, 3)
            pool.affine_select(out=ident[:, :], in_=ident[:, :], compare_op=ALU.not_equal, fill=1.0, base=0,
                               pattern=[[-1, P]], channel_multiplier=1).then_inc(const_step, 1)
            pool.affine_select(out=expert_rows[:, :], in_=expert_rows[:, :], compare_op=ALU.is_ge, fill=0.0, base=0,
                               pattern=[[1, 2 * NU * P]], channel_multiplier=-I).then_inc(const_step, 1)
            pool.affine_select(out=tri[:, :, :], in_=tri[:, :, :], compare_op=ALU.is_ge, fill=0.0, base=-1,
                               pattern=[[1, E], [-1, E]], channel_multiplier=0).then_inc(const_step, 1)
            pool.wait_ge(const_step, 6)
            pool.affine_select(out=expert_rows[:, :], in_=expert_rows[:, :], compare_op=ALU.is_ge, fill=0.0, base=I - 1,
                               pattern=[[-1, 2 * NU * P]], channel_multiplier=I).then_inc(const_step, 1)
            pool.memset(minus_half[:, :], -0.5).then_inc(const_step, 1)
            pool.memset(pT[:, :, :, :], 0.0).then_inc(const_step, 1)
            pool.memset(comb[:, :], 0.0).then_inc(const_step, 1)
            pool.memset(eps_head[:, :, :], P * EPS).then_inc(const_step, 1)
            pool.wait_ge(const_step, 11)
            pool.memset(comb[:, E:NE], 0.5).then_inc(const_step, 1)
            for k in range(NI):
                pool.wait_ge(peak_step, k + 1)
                pool.partition_all_reduce(peak[:, k:k + 1], rowmax[:, k:k + 1], P, RMAX).then_inc(factor_ready, 1)

            def power(s, dst, src, per, t, k):
                pool.tensor_scalar(dst, src, 1.0, EPS, ALU.mult, ALU.add).then_inc(s, 1)
                after(pool, s, per, t, k + 1)
                pool.tensor_tensor(dst, dst, minus_half[:, 0:1], ALU.pow).then_inc(s, 1)

            def step(t, j):
                if has(t + 1) and j == 2:
                    after_apart(pool, ln1_step, 6, t + 1, 5)
                    power(ln1_pow, ln_r[:, :], ln_mv[:, 1:2], 4, t + 1, 2)
                if has(t, j):
                    b = j % 2
                    me, mo = stats[:, b, :, 1], stats[:, b, :, 4]
                    after(pool, stats_done, 4, t, j + 1)
                    if True:
                        t2, j2 = back(t, j, 2)
                        after(pool, xhat_ready, 12, t2, 3 * j2 + 3)
                    k = 7 * j
                    pool.tensor_tensor(st_a[:, :], stats[:, b, :, 2], stats[:, b, :, 5], ALU.add).then_inc(rstd_step, 1)
                    pool.tensor_tensor(st_b[:, :], me, mo, ALU.subtract).then_inc(rstd_step, 1)
                    after(pool, rstd_step, 28, t, k + 1)
                    pool.tensor_tensor(st_a[:, :], st_a[:, :], eps_head[:, j, :], ALU.add).then_inc(rstd_step, 1)
                    after(pool, rstd_step, 28, t, k + 2)
                    pool.tensor_tensor(st_b[:, :], st_b[:, :], st_b[:, :], ALU.mult).then_inc(rstd_step, 1)
                    after_apart(pool, rstd_step, 28, t, k + 4)
                    pool.tensor_scalar(st_b[:, :], st_b[:, :], P / 4.0, 0.0, ALU.mult, ALU.add).then_inc(rstd_step, 1)
                    after(pool, rstd_step, 28, t, k + 5)
                    pool.tensor_tensor(st_a[:, :], st_a[:, :], st_b[:, :], ALU.add).then_inc(rstd_step, 1)
                    after(pool, rstd_step, 28, t, k + 6)
                    pool.tensor_tensor(rstd[:, b, :], st_a[:, :], minus_half[:, :], ALU.pow).then_inc(rstd_step, 1)

                def weigh(u):
                    f = t - 2
                    after(pool, gated, 14, f, 2 * u + 2)
                    after(pool, combs_ready, NB, f, u // 2 + 1)
                    if u >= 2:
                        after(pool, down_done, NU, f, u - 1)
                    else:
                        after(pool, down_done, NU, f - 1, 7)
                    pool.tensor_tensor(act_ff[:, u % 2, :, :], gu[:, :, :], combs[:, 2 * u:2 * u + 2, :],
                                       ALU.mult).then_inc(act_ready, 1)

                if ffn(t - 2) and j in UNITS:
                    for u in UNITS[j][0]:
                        weigh(u)
                t1, j1 = back(t, j, 1)
                if has(t1, j1):
                    after(pool, exp_done, 4, t1, j1 + 1)
                    after(pool, soft_step, 16, t1, 4 * j1 + 4)
                    t2, j2 = back(t, j, 2)
                    after(pool, p_transposed, 4, t2, j2 + 1)
                    pool.tensor_tensor(probs[:, :, :].rearrange("p g (b t) -> p (g b) t", b=2), ex[:, :, :],
                                       rinv[:, :].unsqueeze(2).broadcast_to([P, 8, 64]), ALU.mult).then_inc(p_ready, 1)
                if ffn(t - 2) and j in UNITS:
                    for u in UNITS[j][1]:
                        weigh(u)
                if has(t + 1) and j == 1:
                    after_apart(pool, ln1_step, 6, t + 1, 2)
                    power(ln1_pow, ln_r[:, :], ln_mv[:, 1:2], 4, t + 1, 0)
                if ffn(t - 1) and j == 2:
                    after(pool, ln2_step, 3, t - 1, 2)
                    after_apart(pool, ln2_step, 3, t - 2, 3)
                    power(ln2_pow, f_r[:, :], f_mv[:, 1:2], 2, t - 1, 0)
                if ffn(t - 1) and j == 3:
                    after(pool, o_added, 4, t - 1, 4)
                    after_apart(pool, out_ready, 1, t - 2, 1)
                    pool.tensor_copy(x1keep[:, :], x1[:, :]).then_inc(x1_kept, 1)

            run(pool, step)

        @block.scalar
        def _(act):
            act.wait_ge(pad_zeroed, 2)
            for k in range(NI):
                act.wait_ge(fac_step, 3 * k + 3)
                for c in range(KC):
                    for dst, c0, n in parts(k, 0, c):
                        last = act.activation(dst, staged(k)[:, c, c0:c0 + n], ACT.Copy, scale=factor[:, k, c:c + 1])
                last.then_inc(high_done, 1)
            for q in range(8):
                act.wait_ge(s_wp[q % 2], 16 * (q // 2 + 1))
                act.activation(w_proj[:, 4 * q:4 * q + 4, :].rearrange("p c n -> p (c n)"), stage[q % 2],
                               ACT.Copy).then_inc(wproj_cast, 1)
            act.wait_ge(wproj_cast, 8)
            act.wait_ge(tab_step, 13)
            act.wait_ge(const_step, 12)

            def step(t, j):
                b = j % 2
                t1, j1 = back(t, j, 1)
                t2, j2 = back(t, j, 2)
                cross1 = j1 >= 2

                def evac_T(blk):
                    ln = (V_KXLN if cross1 else V_KLN) if blk == 0 else (V_QXLN if cross1 else V_QLN)
                    after(act, qk_transposed, 12, t1, 3 * j1 + blk + 1)
                    if blk == 0:
                        after(act, scores_done, 4, t2, j2 + 1)
                    tb = T_BANK[blk % 2]
                    act.activation(qkT[:, 4 * blk:4 * blk + 4, :].rearrange("p a b -> p (a b)"), bank[tb][:, :],
                                   ACT.Identity, scale=ln_scale[:, (ln - V_QLN) // 2:(ln - V_QLN) // 2 + 1],
                                   bias=vec[:, ln + 1:ln + 2]).then_inc(qkT_ready, 1)

                def evac_raw(blk):
                    after(act, proj_done, 16, t, 4 * j + blk + 1)
                    after(act, qk_transposed, 12, t2, 3 * j2 + blk + 1)
                    act.activation(raw[:, b, 4 * blk:4 * blk + 4, :].rearrange("p a b -> p (a b)"),
                                   bank[P_BANK[blk % 2]][:, :], ACT.Copy).then_inc(raw_ready, 1)

                if has(t1, j1):
                    evac_T(0)
                    evac_T(1)
                if has(t, j):
                    evac_raw(0)
                if has(t1, j1):
                    evac_T(2)
                if ffn(t - 1) and j == 3:
                    after(act, xn_transposed, 1, t - 1, 1)
                    after(act, gate_done, 1, t - 2, 1)
                    after(act, parts_step, 2, t - 2, 2)
                    act.activation(xnT[:, :, :].rearrange("p c n -> p (c n)"), bank[Y_BANK][:, 0:H],
                                   ACT.Copy).then_inc(xnT_ready, 1)
                if has(t, j):
                    evac_raw(1)
                if has(t2, j2):
                    after(act, p_transposed, 4, t2, j2 + 1)
                    t3, j3 = back(t, j, 3)
                    after(act, pv_done, 8, t3, 2 * j3 + 2)
                    tb = bank[T_BANK[1]][:, :].rearrange("p (g n) -> p g n", g=4)
                    act.activation(pT[0:64, :, 0, :], tb[0:64], ACT.Copy)
                    act.activation(pT[64:128, :, 1, :], tb[64:128], ACT.Copy).then_inc(pT_ready, 1)
                if has(t, j):
                    evac_raw(2)
                    after(act, proj_done, 16, t, 4 * j + 4)
                    after(act, pv_done, 8, t - 1, 2 * j + 2)
                    sc = sigma[:, 6 + j:7 + j] if j < 2 else 1.0
                    act.activation(vals[:, j, :], bank[P_BANK[1]][:, :], ACT.Copy, scale=sc).then_inc(v_ready, 1)
                if has(t + 1) and j == 3:
                    after(act, z_transposed, 1, t + 1, 1)
                    after(act, xx_step, 6, t, 1)
                    after(act, xqkv_step, 6, t, 1)
                    for c in range(KC):
                        last = act.activation(zT[:, c, :], bank[T_BANK[0]][:, c * P:c * P + P], ACT.Identity,
                                              scale=vec[:, V_LNW + c:V_LNW + c + 1], bias=vec[:, V_LNB + c:V_LNB + c + 1])
                    last.then_inc(zT_ready, 1)
                if has(t) and j == 0:
                    after(act, c_transposed, 1, t, 1)
                    after(act, proj_done, 16, t - 1, 16)
                    act.activation(condT[:, :, :].rearrange("p c n -> p (c n)"), bank[T_BANK[0]][:, 0:H],
                                   ACT.Copy).then_inc(condT_ready, 1)

                def scale_cat(half):
                    after(act, pv_done, 8, t2, 2 * j2 + half + 1)
                    t3, j3 = back(t, j, 3)
                    after(act, quant_step, 20, t3, 5 * j3 + 5)
                    for i in range(4):
                        lc = 4 * half + i
                        last = act.activation(cat[:, lc, :], bank[V_BANK][:, i * P:i * P + P], ACT.Copy,
                                              scale=inv_smooth[:, 8 * j2 + lc:8 * j2 + lc + 1])
                    last.then_inc(cat_scaled, 1)

                def tanh(u):
                    f = t - 2
                    after(act, up_done, NU, f, u + 1)
                    after(act, gated, 14, f, 2 * u)
                    act.activation(th[:, :, :].rearrange("p c n -> p (c n)"), bank[H_BANK][:, 0:256], ACT.Tanh,
                                   scale=half_up[:, u // 2:u // 2 + 1]).then_inc(tanh_done, 1)

                if has(t2, j2):
                    scale_cat(0)
                if ffn(t - 1) and j == 3:
                    after(act, gate_step, 14, t - 1, 2)
                    act.activation(g_ex[:, :], g_sh[:, :], ACT.Exp).then_inc(gexp_done, 1)
                if ffn(t - 2) and j in UNITS:
                    for u in UNITS[j][0]:
                        tanh(u)
                if has(t1, j1):
                    after(act, soft_step, 16, t1, 4 * j1 + 2)
                    after(act, p_ready, 4, t2, j2 + 1)
                    act.activation(ex[:, :, :], shifted[:, :, :], ACT.Exp, scale=SCALE).then_inc(exp_done, 1)
                if has(t2, j2):
                    scale_cat(1)
                if ffn(t - 2) and j in UNITS:
                    for u in UNITS[j][1]:
                        tanh(u)
                if ffn(t - 1) and j == 3:
                    after(act, comb_transposed, 1, t - 1, 1)
                    act.activation(combT[:, :], bank[Y_BANK][:, 384:512], ACT.Copy).then_inc(combT_ready, 1)
                    after(act, act_ready, NU, t - 2, NU)
                    for q in range(NB):
                        n = min(4, 2 * NU - 4 * q)
                        after(act, spread_done, NB, t - 1, q + 1)
                        act.activation(combs[:, 4 * q:4 * q + n, :].rearrange("p c n -> p (c n)"),
                                       bank[(H_BANK, Y_BANK)[q % 2]][:, 0:n * P], ACT.Copy,
                                       scale=both_up[:, q:q + 1]).then_inc(combs_ready, 1)

            run(act, step)

        @block.vector
        def _(dve):
            dve.memset(w_up[:, NU - 1, :, :, :, :], 0.0).then_inc(pad_zeroed, 1)
            dve.memset(w_down[96:128, 2 * NU - 1, :], 0.0).then_inc(pad_zeroed, 1)
            dve.wait_ge(s_vec, 16)
            dve.wait_ge(pad_zeroed, 2)

            def measure(k):
                _, n, centred, ty, _ = items[k]
                w = staged(k)
                dve.wait_ge(s_stage[k % 3], 16 * (k // 3 + 1))
                hs = headsum[:, k % 2, :]
                if centred:
                    w8 = w.rearrange("p c (h d) -> p (c h) d", d=P)
                    n = 3 * sum(items[i][2] for i in range(k))
                    dve.tensor_reduce(hs, w8, AX.X, ALU.add).then_inc(prep_centred, 1)
                    dve.wait_ge(prep_centred, n + 1)
                    dve.tensor_scalar(hs, hs, -1.0 / P, None, ALU.mult).then_inc(prep_centred, 1)
                    dve.wait_ge(prep_centred, n + 2)
                    dve.tensor_tensor(w8, w8, hs.unsqueeze(2).broadcast_to([P, 8, P]), ALU.add).then_inc(prep_centred, 1)
                    dve.wait_ge(prep_centred, n + 3)
                dve.tensor_reduce(absmax[:, k, :], w, AX.X, ALU.max, apply_absolute_value=True).then_inc(prep_max, 1)
                dve.wait_ge(prep_max, k + 1)
                if ty is not None:
                    dve.tensor_tensor(absmax[:, k, :], absmax[:, k, :], vec[:, V_IN + 2 * ty:V_IN + 2 * ty + 2],
                                      ALU.mult).then_inc(prep_scaled, 1)
                    dve.wait_ge(prep_scaled, k + 1)
                dve.tensor_reduce(rowmax[:, k:k + 1], absmax[:, k, :], AX.X, ALU.max,
                                  apply_absolute_value=True).then_inc(peak_step, 1)

            def split(k):
                _, n, centred, ty, _ = items[k]
                dve.wait_ge(factor_ready, k + 1)
                dve.tensor_scalar(peak[:, k:k + 1], peak[:, k:k + 1], 1e-30, 1.0 / TOP, ALU.max, ALU.mult).then_inc(fac_step, 1)
                dve.wait_ge(fac_step, 3 * k + 1)
                dve.reciprocal(rowmax[:, k:k + 1], peak[:, k:k + 1]).then_inc(fac_step, 1)
                dve.wait_ge(fac_step, 3 * k + 2)
                if ty is None:
                    dve.tensor_copy(factor[:, k, :], rowmax[:, k:k + 1].broadcast_to([P, KC])).then_inc(fac_step, 1)
                else:
                    dve.tensor_scalar(factor[:, k, :], vec[:, V_IN + 2 * ty:V_IN + 2 * ty + 2], rowmax[:, k:k + 1],
                                      None, ALU.mult).then_inc(fac_step, 1)
                dve.wait_ge(fac_step, 3 * k + 3)

            def low(k):
                dve.wait_ge(high_done, k + 1)
                for c in range(KC):
                    his = parts(k, 0, c)
                    for (dst, c0, n), (hi, _, _) in zip(parts(k, 1, c), his):
                        last = dve.scalar_tensor_tensor(dst, staged(k)[:, c, c0:c0 + n], factor[:, k, c:c + 1], hi,
                                                        ALU.mult, ALU.subtract)
                last.then_inc(low_done, 1)

            measure(0)
            for k in range(NI):
                if k + 1 < NI:
                    measure(k + 1)
                split(k)
                low(k)

            dve.wait_ge(s_wkv, 16)
            for c in range(KC):
                w8 = w_kv[:, c, 0:1024].rearrange("p (h d) -> p h d", d=P)
                dve.tensor_reduce(headsum[:, c, :], w8, AX.X, ALU.add).then_inc(tab_step, 1)
            dve.wait_ge(tab_step, 2)
            dve.tensor_scalar(headsum[:, :, :], headsum[:, :, :], -1.0 / P, None, ALU.mult).then_inc(tab_step, 1)
            dve.wait_ge(tab_step, 3)
            for c in range(KC):
                w8 = w_kv[:, c, 0:1024].rearrange("p (h d) -> p h d", d=P)
                dve.tensor_tensor(w8, w8, headsum[:, c, :].unsqueeze(2).broadcast_to([P, 8, P]), ALU.add)\
                   .then_inc(tab_step, 1)
            for ty, (a, n) in enumerate(((0, 4), (4, 2), (6, 2), (8, 4))):
                last = dve.tensor_scalar(sigma[:, a:a + n], peak[:, a:a + n], vec[:, V_WS + ty:V_WS + ty + 1], None, ALU.mult)
            last.then_inc(tab_step, 1)
            dve.wait_ge(tab_step, 6)
            dve.reciprocal(isig[:, :], sigma[:, :]).then_inc(tab_step, 1)
            dve.wait_ge(tab_step, 7)
            dve.scalar_tensor_tensor(eps_blk[:, :], isig[:, :], P * EPS, isig[:, :], ALU.mult, ALU.mult).then_inc(tab_step, 1)
            dve.wait_ge(tab_step, 8)
            dve.wait_ge(const_step, 12)
            for j in range(4):
                if j < 2:
                    dve.tensor_copy(eps_head[:, j, 0:4], eps_blk[:, 4 + j:5 + j].broadcast_to([P, 4]))
                for h in range(2):
                    k = 2 * (j % 2) + h + (8 if j >= 2 else 0)
                    last = dve.tensor_copy(eps_head[:, j, 4 + 4 * h:8 + 4 * h], eps_blk[:, k:k + 1].broadcast_to([P, 4]))
            last.then_inc(tab_step, 1)
            dve.reciprocal(inv_in[:, :], vec[:, V_IN:V_IN + 8])
            dve.reciprocal(inv_smooth[:, :], vec[:, V_SMOOTH:V_SMOOTH + 32])
            dve.tensor_scalar(ln_scale[:, :], vec[:, V_QLN:V_QLN + 8:2], float(P) ** 0.5, None, ALU.mult).then_inc(tab_step, 1)
            dve.tensor_tensor(out_scale[:, :], vec[:, V_PW:V_PW + 1], vec[:, V_PI:V_PI + 1], ALU.mult).then_inc(tab_step, 1)
            dve.tensor_scalar(half_up[:, :], peak[:, NA:NA + NB], 0.5, None, ALU.mult).then_inc(tab_step, 1)
            dve.tensor_tensor(both_up[:, :], peak[:, NA:NA + NB], peak[:, NA + NB:NA + 2 * NB], ALU.mult).then_inc(tab_step, 1)
            dve.wait_ge(tab_step, 13)

            def norm_stats(s, per, t, k, src, stat, mv):
                dve.bn_stats(stat[:, :], src[:, :]).then_inc(s, 1)
                after_apart(dve, s, per, t, k + 1)
                dve.bn_aggr(mv[:, :], stat[:, :]).then_inc(s, 1)

            def quantise(s, t, src, mask, dst, per, k, wait_dst):
                def clip():
                    dve.tensor_scalar(src, src, FP8_MAX, -FP8_MAX, ALU.min, ALU.max).then_inc(s, 1)

                def binade():
                    after(dve, s, per, t, k + 1)
                    dve.tensor_scalar(mask.bitcast(U16), src.bitcast(U16), 0x7F80, None, ALU.bitwise_and).then_inc(s, 1)

                def magic():
                    after(dve, s, per, t, k + 2)
                    dve.tensor_scalar(mask, mask, FP8_MIN_NORMAL, ROUND3, ALU.max, ALU.mult).then_inc(s, 1)

                def push():
                    after(dve, s, per, t, k + 3)
                    dve.tensor_tensor(src, src, mask, ALU.add).then_inc(s, 1)

                def pull():
                    after(dve, s, per, t, k + 4)
                    wait_dst()
                    dve.tensor_tensor(dst, src, mask, ALU.subtract).then_inc(s, 1)
                return clip, binade, magic, push, pull

            def step(t, j):
                b = j % 2
                t1, j1 = back(t, j, 1)
                t2, j2 = back(t, j, 2)
                t3, j3 = back(t, j, 3)
                flat = "p a b -> p (a b)"

                def nothing():
                    return None

                clip = binade = magic = push = pull = nothing
                if has(t3, j3):
                    t4, j4 = back(t, j, 4)
                    clip, binade, magic, push, pull = quantise(
                        quant_step, t3, cat[:, :, :].rearrange(flat), catm[:, :, :].rearrange(flat),
                        catq[:, :, :].rearrange(flat), 20, 5 * j3,
                        lambda: after(dve, o_done, 4, t4, j4 + 1))

                def head_stats(blk):
                    if not has(t, j):
                        return
                    after(dve, raw_ready, 12, t, 3 * j + blk + 1)
                    if blk == 0:
                        after(dve, rstd_step, 28, t2, 7 * j2 + 7)
                    for h in range(4 * blk, 4 * blk + 4):
                        last = dve.bn_stats(stats[:, b, h, :], raw[:, b, h, :])
                    if blk == 2:
                        last.then_inc(stats_done, 1)

                def normalise(blk):
                    if not has(t, j):
                        return
                    if blk == 0:
                        after(dve, rstd_step, 28, t, 7 * j + 7)
                    r = raw[:, b, 4 * blk:4 * blk + 4, :]
                    dve.tensor_tensor(r, r, rstd[:, b, 4 * blk:4 * blk + 4].unsqueeze(2).broadcast_to([P, 4, P]),
                                      ALU.mult).then_inc(xhat_ready, 1)

                if has(t3, j3):
                    after(dve, cat_scaled, 8, t3, 2 * j3 + 2)
                clip()
                if has(t + 1) and j == 2:
                    after(dve, ln1_pow, 4, t + 1, 2)
                    dve.tensor_scalar(yln[:, :], xin[:, :], ln_mv[:, 0:1], ln_r[:, :], ALU.subtract, ALU.mult).then_inc(ln1_step, 1)
                binade()
                head_stats(0)
                magic()
                if has(t + 1) and j == 2:
                    after(dve, ln1_step, 6, t + 1, 3)
                    dve.bn_stats(ln_stat[:, :], yln[:, :]).then_inc(ln1_step, 1)
                head_stats(1)
                push()
                if has(t + 1) and j == 2:
                    after_apart(dve, ln1_step, 6, t + 1, 4)
                    dve.bn_aggr(ln_mv[:, :], ln_stat[:, :]).then_inc(ln1_step, 1)
                if ffn(t - 1) and j == 3:
                    after(dve, xnT_ready, 1, t - 1, 1)
                    after(dve, up_done, NU, t - 2, NU)
                    dve.tensor_copy(xnp[:, 0, :, :], xnT[:, :, :]).then_inc(parts_step, 1)
                    after(dve, parts_step, 2, t - 1, 1)
                    dve.tensor_tensor(xnp[:, 1, :, :], xnT[:, :, :], xnp[:, 0, :, :], ALU.subtract).then_inc(parts_step, 1)
                head_stats(2)
                pull()
                f = t - 1
                sc_f = g_sc[:, :].unsqueeze(1).broadcast_to([P, E, E])
                sc_e = g_sc[:, :].unsqueeze(2).broadcast_to([P, E, E])
                routing = ffn(f) and j == 3
                if routing:
                    after(dve, gate_done, 1, f, 1)
                    lg = bank[Y_BANK][:, 256:256 + E]
                    dve.tensor_reduce(g_col[:, 0:1], lg, AX.X, ALU.max).then_inc(gate_step, 1)
                    after(dve, gate_step, 14, f, 1)
                    dve.tensor_scalar(g_sh[:, :], lg, g_col[:, 0:1], None, ALU.subtract).then_inc(gate_step, 1)
                if has(t3, j3):
                    after(dve, o_done, 4, t3, j3 + 1)
                    if j3 == 0:
                        after(dve, r_in, 16, t3, 16)
                    else:
                        after(dve, o_added, 4, t3, j3)
                    if j3 == 3:
                        after(dve, x1_kept, 1, t3 - 1, 1)
                    dst = x1 if j3 == 3 else xres
                    dve.scalar_tensor_tensor(dst[:, :], bank[S_BANK][:, 0:H], out_scale[:, :], xres[:, :],
                                             ALU.mult, ALU.add).then_inc(o_added, 1)

                def gate_unit(u):
                    fu = t - 2
                    after(dve, tanh_done, NU, fu, u + 1)
                    if u == 0:
                        after(dve, act_ready, NU, fu - 1, NU)
                    else:
                        after(dve, act_ready, NU, fu, u)
                    dve.scalar_tensor_tensor(gu[:, :, :].rearrange(flat), th[:, :, :].rearrange(flat), 1.0,
                                             bank[H_BANK][:, 0:256], ALU.add, ALU.mult).then_inc(gated, 1)
                    after(dve, gated, 14, fu, 2 * u + 1)
                    dve.tensor_tensor(gu[:, :, :].rearrange(flat), gu[:, :, :].rearrange(flat),
                                      bank[H_BANK][:, 256:512], ALU.mult).then_inc(gated, 1)

                if ffn(t - 2) and j in UNITS:
                    for u in UNITS[j][0]:
                        gate_unit(u)
                if ffn(t - 1) and j == 2:
                    after(dve, o_added, 4, t - 1, 4)
                    after(dve, ln2_pow, 2, t - 2, 1)
                    norm_stats(ln2_step, 3, t - 1, 0, x1, f_stat, f_mv)
                sc = bank[S_BANK][:, :].rearrange("p (g t) -> p g t", t=64)
                if has(t1, j1):
                    after(dve, scores_done, 4, t1, j1 + 1)
                    dve.tensor_reduce(smax[:, :], sc, AX.X, ALU.max).then_inc(soft_step, 1)
                if routing:
                    after(dve, gexp_done, 1, f, 1)
                    dve.tensor_reduce(g_col[:, 1:2], g_ex[:, :], AX.X, ALU.add).then_inc(gate_step, 1)
                if has(t1, j1):
                    after(dve, soft_step, 16, t1, 4 * j1 + 1)
                    after(dve, exp_done, 4, t2, j2 + 1)
                    dve.tensor_tensor(shifted[:, :, :], sc, smax[:, :].unsqueeze(2).broadcast_to([P, 8, 64]),
                                      ALU.subtract).then_inc(soft_step, 1)
                if routing:
                    after(dve, gate_step, 14, f, 3)
                    dve.reciprocal(g_col[:, 2:3], g_col[:, 1:2]).then_inc(gate_step, 1)
                normalise(0)
                if routing:
                    after(dve, gate_step, 14, f, 4)
                    dve.tensor_scalar(g_sc[:, :], g_ex[:, :], g_col[:, 2:3], None, ALU.mult).then_inc(gate_step, 1)
                if has(t1, j1):
                    after(dve, exp_done, 4, t1, j1 + 1)
                    after(dve, p_ready, 4, t2, j2 + 1)
                    dve.tensor_reduce(rsum[:, :], ex[:, :, :], AX.X, ALU.add).then_inc(soft_step, 1)
                if routing:
                    after(dve, gate_step, 14, f, 5)
                    dve.tensor_tensor(g_gt[:, :, :], sc_f, sc_e, ALU.is_gt).then_inc(gate_step, 1)
                    dve.tensor_tensor(g_eq[:, :, :], sc_f, sc_e, ALU.is_equal).then_inc(gate_step, 1)
                normalise(1)
                if has(t1, j1):
                    after(dve, soft_step, 16, t1, 4 * j1 + 3)
                    dve.reciprocal(rinv[:, :], rsum[:, :]).then_inc(soft_step, 1)
                if routing:
                    after(dve, gate_step, 14, f, 7)
                    dve.tensor_tensor(g_eq[:, :, :], g_eq[:, :, :], tri[:, :, :], ALU.mult).then_inc(gate_step, 1)
                normalise(2)
                if routing:
                    after(dve, gate_step, 14, f, 8)
                    dve.tensor_tensor(g_gt[:, :, :], g_gt[:, :, :], g_eq[:, :, :], ALU.add).then_inc(gate_step, 1)
                if ffn(t - 2) and j in UNITS:
                    for u in UNITS[j][1]:
                        gate_unit(u)
                if ffn(t - 1) and j == 2:
                    after(dve, ln2_pow, 2, t - 1, 2)
                    after(dve, xn_transposed, 1, t - 2, 1)
                    dve.tensor_scalar(xn[:, :], x1[:, :], f_mv[:, 0:1], f_r[:, :], ALU.subtract, ALU.mult).then_inc(ln2_step, 1)
                if ffn(t - 2) and j == 2:
                    after(dve, down_done, NU, t - 2, NU)
                    after(dve, x1_kept, 1, t - 2, 1)
                    after(dve, out_sent, 16, t - 3, 16)
                    dve.tensor_tensor(yout[:, :], bank[Y_BANK][:, 0:H], x1keep[:, :], ALU.add).then_inc(out_ready, 1)
                if has(t + 1) and j == 1:
                    after(dve, x_in, 16, t + 1, 16)
                    after(dve, ln1_pow, 4, t, 3)
                    after(dve, ln1_step, 6, t, 6)
                    norm_stats(ln1_step, 6, t + 1, 0, xin, ln_stat, ln_mv)
                if has(t + 1) and j == 2:
                    after(dve, ln1_pow, 4, t + 1, 4)
                    after(dve, z_transposed, 1, t, 1)
                    dve.tensor_scalar(zln[:, :], yln[:, :], ln_mv[:, 0:1], ln_r[:, :], ALU.subtract, ALU.mult).then_inc(ln1_step, 1)

                def scaled_input(ty):
                    for c in range(KC):
                        last = dve.tensor_scalar(xs[:, ty, c, :], zT[:, c, :], inv_in[:, 2 * ty + c:2 * ty + c + 1], None, ALU.mult)
                    return last

                if has(t + 1) and j == 3:
                    after(dve, zT_ready, 1, t + 1, 1)
                    for ty in (TQ, TK, TV):
                        last = scaled_input(ty)
                    last.then_inc(xqkv_step, 1)
                    whole = "p a b c -> p (a b c)"
                    after(dve, xqkv_step, 6, t + 1, 1)
                    for go in quantise(xqkv_step, t + 1, xs[:, 0:3].rearrange(whole), xm[:, 0:3].rearrange(whole),
                                       xq[:, 0:3].rearrange(whole), 6, 1,
                                       lambda: after(dve, proj_done, 16, t, 8)):
                        go()
                if routing:
                    after(dve, gate_step, 14, f, 9)
                    dve.tensor_reduce(g_rank[:, :], g_gt[:, :, :], AX.X, ALU.add).then_inc(gate_step, 1)
                    after(dve, gate_step, 14, f, 10)
                    dve.scalar_tensor_tensor(g_sel[:, :], g_rank[:, :], 1.5, g_sc[:, :], ALU.is_lt, ALU.mult).then_inc(gate_step, 1)
                    after(dve, gate_step, 14, f, 11)
                    dve.tensor_reduce(g_col[:, 3:4], g_sel[:, :], AX.X, ALU.add).then_inc(gate_step, 1)
                    after(dve, gate_step, 14, f, 12)
                    dve.reciprocal(g_col[:, 4:5], g_col[:, 3:4]).then_inc(gate_step, 1)
                    after(dve, gate_step, 14, f, 13)
                    after(dve, comb_transposed, 1, f - 1, 1)
                    dve.tensor_scalar(comb[:, 0:E], g_sel[:, :], g_col[:, 4:5], 0.5, ALU.mult, ALU.mult).then_inc(gate_step, 1)
                if has(t) and j == 0:
                    after(dve, zT_ready, 1, t, 1)
                    scaled_input(TX).then_inc(xx_step, 1)
                    whole = "p b c -> p (b c)"
                    after(dve, xx_step, 6, t, 1)
                    for go in quantise(xx_step, t, xs[:, 3].rearrange(whole), xm[:, 3].rearrange(whole),
                                       xq[:, 3].rearrange(whole), 6, 1,
                                       lambda: after(dve, proj_done, 16, t - 1, 16)):
                        go()

            run(dve, step)

        @block.tensor
        def _(pe):
            pe.wait_ge(const_step, 12)
            pe.wait_ge(tab_step, 13)
            pe.wait_ge(low_done, NI)
            pe.wait_ge(high_done, NI)
            pe.wait_ge(wproj_cast, 8)
            pe.wait_ge(s_wd, 32)
            pe.wait_ge(s_wg, 16)

            def transposes(dst, src, n):
                for i in range(n):
                    last = nc.tensor.transpose(bank[dst][:, i * P:i * P + P], src(i), ident[:, :])
                return last

            def step(t, j):
                b = j % 2
                t1, j1 = back(t, j, 1)
                t2, j2 = back(t, j, 2)
                t3, j3 = back(t, j, 3)
                cross = j >= 2

                def transpose_qk(blk):
                    after(pe, xhat_ready, 12, t1, 3 * j1 + blk + 1)
                    if blk == 0:
                        after(pe, qkT_ready, 12, t2, 3 * j2 + 3)
                        if has(t) and j == 0:
                            after(pe, zT_ready, 1, t, 1)
                        if has(t) and j == 1:
                            after(pe, condT_ready, 1, t, 1)
                    elif blk == 1:
                        after(pe, pT_ready, 4, t3, j3 + 1)
                    else:
                        after(pe, qkT_ready, 12, t1, 3 * j1 + 1)
                    tb = bank[T_BANK[blk % 2]]
                    by_head = tb[:, :].rearrange("p (g b h s) -> p g h b s", g=2, b=2, h=2)
                    for i in range(4):
                        dst = tb[:, i * P:i * P + P] if blk == 0 else by_head[:, i // 2, i % 2]
                        last = nc.tensor.transpose(dst, raw[:, 1 - b, 4 * blk + i, :], ident[:, :])
                    last.then_inc(qk_transposed, 1)

                def project(blk):
                    if blk == 0:
                        after(pe, raw_ready, 12, t1, 3 * j1 + 3)
                        if j == 0:
                            after(pe, xqkv_step, 6, t, 6)
                        if j == 2:
                            after(pe, condT_ready, 1, t, 1)
                            after(pe, xx_step, 6, t, 6)
                    elif blk == 1:
                        after(pe, v_ready, 4, t1, j1 + 1)
                    else:
                        after(pe, raw_ready, 12, t, 3 * j + blk - 1)
                    dst = bank[P_BANK[blk % 2]][:, :]
                    if cross and blk in (0, 3):
                        c0 = (1024 if blk == 3 else 0) + 512 * (j % 2)
                        for c in range(KC):
                            last = nc.tensor.matmul(dst, condT[:, c, :], w_kv[:, c, c0:c0 + BLK],
                                                    start=(c == 0), stop=(c == KC - 1))
                    else:
                        h = j % 2
                        ty, w = {0: (TK, 4 + h), 3: (TV, 6 + h)}.get(blk, (None, None))
                        if ty is None:
                            ty, w = (TX, 8 + 2 * h + blk - 1) if cross else (TQ, 2 * h + blk - 1)
                        for c in range(KC):
                            for part in range(2):
                                last = nc.tensor.matmul(dst, xq[:, ty, c, :], w_attn[:, w, part, c, :],
                                                        start=(c == 0 and part == 0), stop=(c == KC - 1 and part == 1))
                    last.then_inc(proj_done, 1)

                if has(t1, j1):
                    transpose_qk(0)
                    transpose_qk(1)
                if has(t, j):
                    project(0)
                if has(t1, j1):
                    transpose_qk(2)
                if ffn(t - 1) and j == 3:
                    after(pe, ln2_step, 3, t - 1, 3)
                    after(pe, out_ready, 1, t - 2, 1)
                    transposes(Y_BANK, lambda i: xn[:, i * P:i * P + P], 2).then_inc(xn_transposed, 1)
                if has(t, j):
                    project(1)
                if has(t2, j2):
                    after(pe, p_ready, 4, t2, j2 + 1)
                    after(pe, qkT_ready, 12, t1, 3 * j1 + 2)
                    transposes(T_BANK[1], lambda i: probs[:, i, :], 4).then_inc(p_transposed, 1)
                if has(t, j):
                    project(2)
                    project(3)
                if has(t + 1) and j == 3:
                    after(pe, ln1_step, 6, t + 1, 6)
                    after(pe, qkT_ready, 12, t1, 3 * j1 + 3)
                    transposes(T_BANK[0], lambda i: zln[:, i * P:i * P + P], 2).then_inc(z_transposed, 1)
                if has(t) and j == 0:
                    after(pe, c_in, 16, t, 16)
                    after(pe, qkT_ready, 12, t1, 3 * j1 + 3)
                    after(pe, zT_ready, 1, t, 1)
                    transposes(T_BANK[0], lambda i: cin[:, i * P:i * P + P], 2).then_inc(c_transposed, 1)
                if ffn(t - 1) and j == 3:
                    after(pe, xnT_ready, 1, t - 1, 1)
                    for c in range(KC):
                        last = nc.tensor.matmul(bank[Y_BANK][:, 256:256 + E], xnT[:, c, :], w_gate[:, c, :],
                                                start=(c == 0), stop=(c == KC - 1))
                    last.then_inc(gate_done, 1)
                if has(t3, j3):
                    after(pe, quant_step, 20, t3, 5 * j3 + 5)
                    after(pe, soft_step, 16, t2, 4 * j2 + 2)
                    for i in range(8):
                        last = nc.tensor.matmul(bank[S_BANK][:, 0:H], catq[:, i, :], w_proj[:, 8 * j3 + i, :],
                                                start=(i == 0), stop=(i == 7))
                    last.then_inc(o_done, 1)

                def values(half):
                    if half == 0:
                        after(pe, pT_ready, 4, t2, j2 + 1)
                        after(pe, v_ready, 4, t2, j2 + 1)
                        after(pe, cat_scaled, 8, t3, 2 * j3 + 2)
                    else:
                        after(pe, cat_scaled, 8, t2, 2 * j2 + 1)
                    for i in range(2):
                        g = 2 * half + i
                        last = nc.tensor.matmul(bank[V_BANK][:, 256 * i:256 * i + 256], vals[:, j2, g * P:g * P + P],
                                                pT[:, g, :, :].rearrange("p b (h s) -> p h b s", h=2),
                                                start=True, stop=True)
                    last.then_inc(pv_done, 1)

                def up(u):
                    fu = t - 2
                    if u == 0:
                        after(pe, combs_ready, NB, fu, 3)
                        after(pe, parts_step, 2, fu, 2)
                    else:
                        after(pe, gated, 14, fu, 2 * u)
                    for w in range(2):
                        for ch in range(2):
                            dst = bank[H_BANK][:, 256 * w + P * ch:256 * w + P * ch + P]
                            n = 0
                            for c in range(KC):
                                for wp, xp in ((0, 0), (0, 1), (1, 0)):
                                    last = nc.tensor.matmul(dst, w_up[:, u, wp, w, c, P * ch:P * ch + P], xnp[:, xp, c, :],
                                                            start=(n == 0), stop=(n == 5))
                                    n += 1
                    last.then_inc(up_done, 1)

                def down(u):
                    fu = t - 2
                    after(pe, act_ready, NU, fu, u + 1)
                    if u == 0:
                        after(pe, combs_ready, NB, fu, NB)
                    for ch in range(2):
                        last = nc.tensor.matmul(bank[Y_BANK][:, 0:H], act_ff[:, u % 2, ch, :], w_down[:, 2 * u + ch, :],
                                                start=(u == 0 and ch == 0), stop=(u == NU - 1 and ch == 1))
                    last.then_inc(down_done, 1)

                work = {0: (((up, 0), (up, 1), (down, 0)), ((up, 2), (down, 1))),
                        1: (((up, 3), (down, 2)), ((up, 4), (down, 3))),
                        2: (((up, 5), (down, 4)), ((up, 6), (down, 5), (down, 6)))}
                if has(t2, j2):
                    values(0)
                if ffn(t - 2) and j in work:
                    for go, u in work[j][0]:
                        go(u)
                if has(t1, j1):
                    after(pe, qkT_ready, 12, t1, 3 * j1 + 3)
                    after(pe, o_added, 4, t3, j3 + 1)
                    after(pe, soft_step, 16, t2, 4 * j2 + 2)
                    for g in range(4):
                        for bt in range(2):
                            last = nc.tensor.matmul(bank[S_BANK][:, P * g + 64 * bt:P * g + 64 * bt + 64],
                                                    qkT[:, 4 + 2 * g + bt, :],
                                                    qkT[:, g, 64 * bt:64 * bt + 64], start=True, stop=True)
                    last.then_inc(scores_done, 1)
                if has(t2, j2):
                    values(1)
                if ffn(t - 2) and j in work:
                    for go, u in work[j][1]:
                        go(u)
                if ffn(t - 1) and j == 3:
                    after(pe, gate_step, 14, t - 1, 14)
                    nc.tensor.transpose(bank[Y_BANK][:, 384:512], comb[:, :], ident[:, :]).then_inc(comb_transposed, 1)
                    after(pe, combT_ready, 1, t - 1, 1)
                    after(pe, gated, 14, t - 2, 14)
                    for q in range(NB):
                        if q >= 2:
                            after(pe, combs_ready, NB, t - 1, q - 1)
                        for i in range(4 * q, min(4 * q + 4, 2 * NU)):
                            last = nc.tensor.matmul(bank[(H_BANK, Y_BANK)[q % 2]][:, P * (i % 4):P * (i % 4) + P],
                                                    expert_rows[:, P * i:P * i + P], combT[:, :], start=True, stop=True)
                        last.then_inc(spread_done, 1)

            run(pe, step)


def kernel(**a):
    import numpy as np
    import concourse.bacc as bacc
    from concourse.bass_utils import run_bass_kernel_spmd

    pre = "L0_xattn_"
    ff = "L0_ffn_"
    a = {k: np.asarray(v) for k, v in a.items()}

    def turned(w):
        return np.ascontiguousarray(w.T)

    def inner(w, s):
        return np.ascontiguousarray(np.concatenate([np.transpose(w, (1, 0, 2)).reshape(H, E * I), s], axis=1))

    def column(v):
        return v.reshape(-1, P).T

    def spread(v):
        return np.broadcast_to(v.reshape(1, 1), (P, 1))

    names = ["q_in_scale", "k_in_scale", "v_in_scale", "qx_in_scale", "ln_w", "ln_b", "qln_w", "qln_b", "kln_w", "kln_b",
             "qxln_w", "qxln_b", "kxln_w", "kxln_b", "proj_smooth"]
    scalars = ["wq_scale", "wk_scale", "wv_scale", "wqx_scale", "proj_w_scale", "proj_in_scale"]
    vecs = np.ascontiguousarray(np.concatenate([column(a[pre + n]) for n in names] + [spread(a[pre + n]) for n in scalars],
                                               axis=1))
    arrays = {
        "x": a["x"].reshape(-1, H), "cond": a["ctx_2048"].reshape(-1, H),
        "wqT": turned(a[pre + "wq"]), "wkT": turned(a[pre + "wk"]), "wvT": turned(a[pre + "wv"]),
        "wqxT": turned(a[pre + "wqx"]), "wkvT": turned(a[pre + "w_kv_x"]), "wprojT": turned(a[pre + "wproj"]),
        "w1T": inner(a[ff + "w1"], a[ff + "sw1"]), "w3T": inner(a[ff + "w3"], a[ff + "sw3"]),
        "w2": np.ascontiguousarray(np.concatenate([a[ff + "w2"].reshape(E * I, H), a[ff + "sw2"]], axis=0)),
        "gateT": turned(a[ff + "gate_w"]), "vecs": vecs,
    }
    nc = bacc.Bacc("TRN2", target_bir_lowering=False, num_devices=1)
    args = [nc.dram_tensor(f"in_{n}", v.shape, mybir.dt.from_np(v.dtype), kind="ExternalInput").ap() for n, v in arrays.items()]
    out = nc.dram_tensor("out", (TILES * P, H), F32, kind="ExternalOutput").ap()
    bass_xattn_moe(nc, *args, out)
    r = run_bass_kernel_spmd(nc, [{f"in_{n}": v for n, v in arrays.items()}], core_ids=[0])
    return r.results[0]["out"].reshape(a["x"].shape)
```

```python
from contextlib import ExitStack

import concourse.bass as bass
from concourse import mybir

F32 = mybir.dt.float32
F16 = mybir.dt.float16
BF16 = mybir.dt.bfloat16
U16 = mybir.dt.uint16
ALU = mybir.AluOpType
ACT = mybir.ActivationFunctionType
AX = mybir.AxisListType
RMAX = bass.bass_isa.ReduceOp.max

P = 128
H = 256
KC = H // P
NH, G = 16, 8
E, I, SI = 8, 176, 352
NE = E + SI // I
FI = NE * I
NU = -(-FI // 256)
NB = -(-FI // 512)
BLK = 512
TILES = 32
QUADS = 4 * TILES
EPS = 1e-5
FP8_MAX = 448.0
TOP = 1024.0
SCALE = float(P) ** -0.5
FP8_MIN_NORMAL = 2.0 ** -6
ROUND3 = 24.0

V_IN, V_LNW, V_LNB = 0, 8, 10
V_QLN, V_KLN, V_QXLN, V_KXLN = 12, 14, 16, 18
V_SMOOTH, V_WS, V_PW, V_PI = 20, 52, 56, 57
NV = 58

TQ, TK, TV, TX = range(4)
ATTN_BLOCKS = ([(TQ, 0, 512 * b, True) for b in range(4)] + [(TK, 1, 512 * b, True) for b in range(2)]
               + [(TV, 2, 512 * b, False) for b in range(2)] + [(TX, 3, 512 * b, True) for b in range(4)])
NA = len(ATTN_BLOCKS)
UNITS = {(0, "mid"): 0, (0, "late"): 1, (1, "early"): 2, (1, "mid"): 3, (1, "late"): 4, (2, "early"): 5, (2, "mid"): 6}


def back(t, j, d):
    return t + (j - d) // 4, (j - d) % 4


def bass_xattn_moe(nc, x, cond, wqT, wkT, wvT, wqxT, wkvT, wprojT, w1T, w3T, w2, gateT, vecs, out):
    es = ExitStack()
    with es:
        def sb(name, shape, dt=F32):
            return es.enter_context(nc.sbuf_tensor(name, shape, dt))

        def sem(name):
            return es.enter_context(nc.semaphore(name))

        w_attn = sb("w_attn", [P, NA, 2, KC, BLK], F16)
        w_kv = sb("w_kv", [P, KC, 2048])
        w_proj = sb("w_proj", [P, 32, H], BF16)
        w_up = sb("w_up", [P, NU, 2, 2, KC, 256], F16)
        w_down = sb("w_down", [P, 2 * NU, H])
        w_gate = sb("w_gate", [P, KC, E])
        vec = sb("vec", [P, NV])
        ident = sb("ident", [P, P])
        ident16 = sb("ident16", [P, P], BF16)
        expert_rows = sb("expert_rows", [P, 2 * NU * P], BF16)
        tri = sb("tri", [P, E, E])
        minus_half = sb("minus_half", [P, 12])
        inv_in = sb("inv_in", [P, 8])
        inv_smooth = sb("inv_smooth", [P, 32])
        ln_scale = sb("ln_scale", [P, 4])
        eps_head = sb("eps_head", [P, 4, 12])
        out_scale = sb("out_scale", [P, 1])
        absmax = sb("absmax", [P, NA + 2 * NB, KC])
        rowmax = sb("rowmax", [P, NA + 2 * NB])
        peak = sb("peak", [P, NA + 2 * NB])
        factor = sb("factor", [P, NA + 2 * NB, KC])
        headsum = sb("headsum", [P, 2, 8])
        sigma = sb("sigma", [P, NA])
        isig = sb("isig", [P, NA])
        eps_blk = sb("eps_blk", [P, NA])
        half_up = sb("half_up", [P, NB])
        both_up = sb("both_up", [P, NB])

        xin = sb("xin", [P, H])
        cin = sb("cin", [P, H])
        xres = sb("xres", [P, H])
        ln_stat = sb("ln_stat", [P, 6])
        ln_mv = sb("ln_mv", [P, 2])
        ln_r = sb("ln_r", [P, 1])
        yln = sb("yln", [P, H])
        zln = sb("zln", [P, H])
        zT = sb("zT", [P, KC, P])
        condT = sb("condT", [P, KC, P])
        xs = sb("xs", [P, 4, KC, P], BF16)
        xm = sb("xm", [P, 4, KC, P], BF16)
        xq = sb("xq", [P, 4, KC, P], BF16)

        raw = sb("raw", [P, 2, 12, P])
        stats = sb("stats", [P, 2, 12, 6])
        st_a = sb("st_a", [P, 12])
        st_b = sb("st_b", [P, 12])
        rstd = sb("rstd", [P, 2, 12])
        qkT = sb("qkT", [P, 12, P])
        vals = sb("vals", [P, 4, BLK])
        smax = sb("smax", [P, 8])
        shifted = sb("shifted", [P, 8, 64])
        ex = sb("ex", [P, 8, 64])
        rsum = sb("rsum", [P, 8])
        rinv = sb("rinv", [P, 8])
        probs = sb("probs", [P, 4, P])
        pT = sb("pT", [P, 4, 2, P])
        cat = sb("cat", [P, 8, P], BF16)
        catm = sb("catm", [P, 8, P], BF16)
        catq = sb("catq", [P, 8, P], BF16)

        x1 = sb("x1", [P, H])
        x1keep = sb("x1keep", [P, H])
        f_stat = sb("f_stat", [P, 6])
        f_mv = sb("f_mv", [P, 2])
        f_r = sb("f_r", [P, 1])
        xn = sb("xn", [P, H])
        xnT = sb("xnT", [P, KC, P])
        xnp = sb("xnp", [P, 2, KC, P], F16)
        g_col = sb("g_col", [P, 8])
        g_sh = sb("g_sh", [P, E])
        g_ex = sb("g_ex", [P, E])
        g_sc = sb("g_sc", [P, E])
        g_gt = sb("g_gt", [P, E, E])
        g_eq = sb("g_eq", [P, E, E])
        g_rank = sb("g_rank", [P, E])
        g_sel = sb("g_sel", [P, E])
        comb = sb("comb", [P, E])
        rest = sb("rest", [P, E])
        comb3 = sb("comb3", [P, 4, 32], BF16)
        combT = sb("combT", [P, P], BF16)
        combs = sb("combs", [P, 2 * NU, P])
        th = sb("th", [P, 2, P])
        gu = sb("gu", [P, 2, P])
        act_ff = sb("act_ff", [P, 2, 2, P])
        yout = sb("yout", [P, H])

        bank = [es.enter_context(nc.psum_tensor(f"bank{i}", [P, 512], F32)) for i in range(8)]
        P_BANK, T_BANK, S_BANK, V_BANK, H_BANK, Y_BANK = (0, 1), (2, 3), 4, 5, 6, 7

        stage = [v.rearrange("p a b -> p (a b)") for v in (raw[:, 0, 0:8, :], raw[:, 1, 0:8, :], combs[:, 0:8, :])]

        s_vec, s_wkv, s_wd, s_wg = sem("vec_in"), sem("wkv_in"), sem("wdown_in"), sem("wgate_in")
        s_wp = [sem(f"wproj_in{i}") for i in range(2)]
        s_stage = [sem(f"stage_in{i}") for i in range(3)]
        prep_centred, prep_max, prep_scaled = sem("prep_centred"), sem("prep_max"), sem("prep_scaled")
        fac_step = sem("fac_step")
        peak_step = sem("peak_step")
        factor_ready = sem("factor_ready")
        high_done = sem("high_done")
        low_done = sem("low_done")
        wproj_cast = sem("wproj_cast")
        const_step = sem("const_step")
        tab_step = sem("tab_step")
        pad_zeroed = sem("pad_zeroed")
        apart = sem("apart")
        x_in, c_in, r_in, out_sent = sem("x_in"), sem("cond_in"), sem("res_in"), sem("out_sent")
        z_transposed, c_transposed = sem("z_transposed"), sem("cond_transposed")
        proj_done, qk_transposed, scores_done = sem("proj_done"), sem("qk_transposed"), sem("scores_done")
        p_transposed, pv_done, o_done = sem("p_transposed"), sem("pv_done"), sem("o_done")
        xn_transposed, gate_done, comb_transposed = sem("xn_transposed"), sem("gate_done"), sem("comb_transposed")
        spread_done, up_done, down_done = sem("spread_done"), sem("up_done"), sem("down_done")
        zT_ready, condT_ready, raw_ready, v_ready = sem("zT_ready"), sem("condT_ready"), sem("raw_ready"), sem("v_ready")
        qkT_ready, exp_done, pT_ready, cat_scaled = sem("qkT_ready"), sem("exp_done"), sem("pT_ready"), sem("cat_scaled")
        xnT_ready, gexp_done, combT_ready = sem("xnT_ready"), sem("gate_exp_done"), sem("combT_ready")
        combs_ready, tanh_done = sem("combs_ready"), sem("tanh_done")
        ln1_step, xqkv_step, xx_step = sem("ln1_step"), sem("xqkv_step"), sem("xx_step")
        stats_done, xhat_ready, soft_step, quant_step = sem("stats_done"), sem("xhat_ready"), sem("soft_step"), sem("quant_step")
        o_added, ln2_step, parts_step, gate_step = sem("o_added"), sem("ln2_step"), sem("parts_step"), sem("gate_step")
        gated, out_ready, comb3_ready = sem("gated"), sem("out_ready"), sem("comb3_ready")
        ln1_pow, ln2_pow, rstd_step, p_ready = sem("ln1_pow"), sem("ln2_pow"), sem("rstd_step"), sem("p_ready")
        x1_kept, act_ready = sem("x1_kept"), sem("act_ready")

        def after(eng, s, per, t, k):
            if not isinstance(t, int):
                eng.wait_ge(s, per * t + k)
            elif per * t + k > 0:
                eng.wait_ge(s, min(per * t + k, per * TILES))

        def after_apart(eng, s, per, t, k):
            after(eng, s, per, t, k)
            eng.sem_inc(apart, 1)

        def has(t, j=0):
            return not isinstance(t, int) or 0 <= 4 * t + j < QUADS

        def ffn(t):
            return not isinstance(t, int) or 0 <= t < TILES

        def run(eng, step):
            for j in (0, 1, 2, 3):
                step(-1, j)
            for t in (0, 1, 2):
                for j in range(4):
                    step(t, j)
            with eng.Fori(3, TILES - 1) as t:
                for j in range(4):
                    step(t, j)
            for t in (TILES - 1, TILES, TILES + 1):
                for j in range(4):
                    step(t, j)

        sources = (wqT, wkT, wvT, wqxT)
        items = []
        for b, (ty, w, c0, centred) in enumerate(ATTN_BLOCKS):
            items.append((sources[w][:, c0:c0 + BLK], BLK, centred, ty, b))
        for w, src in enumerate((w1T, w3T)):
            for b in range(NB):
                n = min(BLK, FI - BLK * b)
                items.append((src[:, BLK * b:BLK * b + n], n, False, None, (w, b)))
        NI = len(items)

        def parts(k, part, c):
            _, n, _, ty, d = items[k]
            if ty is not None:
                return [(w_attn[:, d, part, c, :], 0, BLK)]
            w, b = d
            return [(w_up[:, 2 * b + u, part, w, c, 0:min(256, n - 256 * u)], 256 * u, min(256, n - 256 * u))
                    for u in range(2) if n > 256 * u]

        def staged(k):
            n = items[k][1]
            return stage[k % 3][:, 0:KC * n].rearrange("p (c n) -> p c n", c=KC)

        block = es.enter_context(nc.Block())

        @block.sync
        def _(sp):
            sp.dma_start(vec[:, :], vecs).then_inc(s_vec, 16)
            for k in range(NI):
                if k >= 3:
                    sp.wait_ge(low_done, k - 2)
                sp.dma_start(staged(k), items[k][0].rearrange("(c p) n -> p c n", p=P)).then_inc(s_stage[k % 3], 16)
                if k == 2:
                    sp.dma_start(xin[:, :], x[0:P, :]).then_inc(x_in, 16)
                    sp.dma_start(cin[:, :], cond[0:P, :]).then_inc(c_in, 16)
                    sp.dma_start(xres[:, :], x[0:P, :]).then_inc(r_in, 16)
                    sp.dma_start(w_kv[:, :, :], wkvT.rearrange("(c p) n -> p c n", p=P)).then_inc(s_wkv, 16)
                if k == 12:
                    sp.dma_start(w_gate[:, :, :], gateT.rearrange("(c p) n -> p c n", p=P)).then_inc(s_wg, 16)
                    full = FI // P
                    sp.dma_start(w_down[:, 0:full, :], w2[0:full * P, :].rearrange("(c p) n -> p c n", p=P)).then_inc(s_wd, 16)
                    sp.dma_start(w_down[0:FI - full * P, full, :], w2[full * P:FI, :]).then_inc(s_wd, 16)
            for q in range(8):
                if q < 2:
                    sp.wait_ge(low_done, NI)
                else:
                    sp.wait_ge(wproj_cast, q - 1)
                sp.dma_start(stage[q % 2].rearrange("p (c n) -> p c n", n=H),
                             wprojT[512 * q:512 * q + 512, :].rearrange("(c p) n -> p c n", p=P)).then_inc(s_wp[q % 2], 16)

            def tile_loads(t):
                real = not isinstance(t, int)
                if real or t < TILES:
                    rows = x[bass.ts(t, P), :]
                    after(sp, c_transposed, 1, t - 1, 1)
                    sp.dma_start(cin[:, :], cond[bass.ts(t, P), :]).then_inc(c_in, 16)
                if real or t < TILES - 1:
                    after(sp, ln1_step, 6, t, 3)
                    sp.dma_start(xin[:, :], x[bass.ts(t + 1, P), :]).then_inc(x_in, 16)
                if real or t < TILES:
                    after(sp, o_added, 4, t - 1, 4)
                    sp.dma_start(xres[:, :], rows).then_inc(r_in, 16)
                if real or t >= 2:
                    after(sp, out_ready, 1, t - 2, 1)
                    sp.dma_start(out[bass.ts(t - 2, P), :], yout[:, :]).then_inc(out_sent, 16)

            sp.wait_ge(ln1_step, 3)
            sp.dma_start(xin[:, :], x[P:2 * P, :]).then_inc(x_in, 16)
            tile_loads(1)
            with sp.Fori(2, TILES - 1) as t:
                tile_loads(t)
            for t in (TILES - 1, TILES, TILES + 1):
                tile_loads(t)
            sp.wait_ge(out_sent, 16 * TILES)

        @block.gpsimd
        def _(pool):
            done = [0]

            def made(instruction):
                instruction.then_inc(const_step, 1)
                done[0] += 1
                pool.wait_ge(const_step, done[0])

            made(pool.memset(minus_half[:, :], -0.5))
            for m in (ident, ident16):
                made(pool.memset(m[:, :], 0.0))
                made(pool.affine_select(out=m[:, :], in_=m[:, :], compare_op=ALU.not_equal, fill=1.0, base=0,
                                        pattern=[[-1, P]], channel_multiplier=1))
            made(pool.memset(tri[:, :, :], 1.0))
            made(pool.affine_select(out=tri[:, :, :], in_=tri[:, :, :], compare_op=ALU.is_ge, fill=0.0, base=-1,
                                    pattern=[[1, E], [-1, E]], channel_multiplier=0))
            made(pool.memset(comb3[:, :, :], 0.0))
            made(pool.memset(comb3[:, 0, E:NE], 0.5))
            made(pool.memset(eps_head[:, :, :], P * EPS))
            made(pool.memset(pT[:, :, :, :], 0.0))
            made(pool.memset(expert_rows[:, :], 1.0))
            for q in range(3):
                rows = expert_rows[32 * q:32 * q + 32, :]
                made(pool.affine_select(out=rows, in_=rows, compare_op=ALU.is_ge, fill=0.0, base=0,
                                        pattern=[[1, 2 * NU * P]], channel_multiplier=-I))
                made(pool.affine_select(out=rows, in_=rows, compare_op=ALU.is_ge, fill=0.0, base=I - 1,
                                        pattern=[[-1, 2 * NU * P]], channel_multiplier=I))
            for k in range(NI):
                pool.wait_ge(peak_step, k + 1)
                pool.partition_all_reduce(peak[:, k:k + 1], rowmax[:, k:k + 1], P, RMAX).then_inc(factor_ready, 1)

            def power(s, dst, src, per, t, k):
                pool.tensor_scalar(dst, src, 1.0, EPS, ALU.mult, ALU.add).then_inc(s, 1)
                after(pool, s, per, t, k + 1)
                pool.tensor_tensor(dst, dst, minus_half[:, 0:1], ALU.pow).then_inc(s, 1)

            def step(t, j):
                def weigh(place):
                    u, f = UNITS.get((j, place)), t - 2
                    if u is None or not ffn(f):
                        return
                    after(pool, gated, 14, f, 2 * u + 2)
                    after(pool, combs_ready, NB, f, u // 2 + 1)
                    if u >= 2:
                        after(pool, down_done, NU, f, u - 1)
                    else:
                        after(pool, down_done, NU, f - 1, 7)
                    pool.tensor_tensor(act_ff[:, u % 2, :, :], gu[:, :, :], combs[:, 2 * u:2 * u + 2, :],
                                       ALU.mult).then_inc(act_ready, 1)

                weigh("early")
                if ffn(t - 1) and j == 3:
                    after_apart(pool, ln2_step, 3, t - 1, 2)
                    power(ln2_pow, f_r[:, :], f_mv[:, 1:2], 2, t - 1, 0)
                if has(t, j):
                    b = j % 2
                    me, mo = stats[:, b, :, 1], stats[:, b, :, 4]
                    after(pool, stats_done, 4, t, j + 1)
                    t2, j2 = back(t, j, 2)
                    after(pool, xhat_ready, 12, t2, 3 * j2 + 3)
                    k = 7 * j
                    pool.tensor_tensor(st_a[:, :], stats[:, b, :, 2], stats[:, b, :, 5], ALU.add).then_inc(rstd_step, 1)
                    pool.tensor_tensor(st_b[:, :], me, mo, ALU.subtract).then_inc(rstd_step, 1)
                    after(pool, rstd_step, 28, t, k + 1)
                    pool.tensor_tensor(st_a[:, :], st_a[:, :], eps_head[:, j, :], ALU.add).then_inc(rstd_step, 1)
                    after(pool, rstd_step, 28, t, k + 2)
                    pool.tensor_tensor(st_b[:, :], st_b[:, :], st_b[:, :], ALU.mult).then_inc(rstd_step, 1)
                    after_apart(pool, rstd_step, 28, t, k + 4)
                    pool.tensor_scalar(st_b[:, :], st_b[:, :], P / 4.0, 0.0, ALU.mult, ALU.add).then_inc(rstd_step, 1)
                    after(pool, rstd_step, 28, t, k + 5)
                    pool.tensor_tensor(st_a[:, :], st_a[:, :], st_b[:, :], ALU.add).then_inc(rstd_step, 1)
                    after(pool, rstd_step, 28, t, k + 6)
                    pool.tensor_tensor(rstd[:, b, :], st_a[:, :], minus_half[:, :], ALU.pow).then_inc(rstd_step, 1)
                t1, j1 = back(t, j, 1)
                if has(t1, j1):
                    after(pool, exp_done, 4, t1, j1 + 1)
                    after(pool, soft_step, 16, t1, 4 * j1 + 4)
                    t2, j2 = back(t, j, 2)
                    after(pool, p_transposed, 4, t2, j2 + 1)
                    pool.tensor_tensor(probs[:, :, :].rearrange("p g (b t) -> p (g b) t", b=2), ex[:, :, :],
                                       rinv[:, :].unsqueeze(2).broadcast_to([P, 8, 64]), ALU.mult).then_inc(p_ready, 1)
                weigh("mid")
                weigh("late")
                if has(t + 1) and j == 0:
                    after_apart(pool, ln1_step, 6, t + 1, 2)
                    power(ln1_pow, ln_r[:, :], ln_mv[:, 1:2], 4, t + 1, 0)
                if has(t + 1) and j == 1:
                    after_apart(pool, ln1_step, 6, t + 1, 5)
                    power(ln1_pow, ln_r[:, :], ln_mv[:, 1:2], 4, t + 1, 2)
                if ffn(t - 1) and j == 3:
                    after(pool, o_added, 4, t - 1, 4)
                    after_apart(pool, out_ready, 1, t - 2, 1)
                    pool.tensor_copy(x1keep[:, :], x1[:, :]).then_inc(x1_kept, 1)

            run(pool, step)

        @block.scalar
        def _(act):
            act.wait_ge(pad_zeroed, 2)
            for k in range(NI):
                act.wait_ge(fac_step, 3 * k + 3)
                for c in range(KC):
                    for dst, c0, n in parts(k, 0, c):
                        last = act.activation(dst, staged(k)[:, c, c0:c0 + n], ACT.Copy, scale=factor[:, k, c:c + 1])
                last.then_inc(high_done, 1)
            for q in range(8):
                act.wait_ge(s_wp[q % 2], 16 * (q // 2 + 1))
                act.activation(w_proj[:, 4 * q:4 * q + 4, :].rearrange("p c n -> p (c n)"), stage[q % 2],
                               ACT.Copy).then_inc(wproj_cast, 1)
            act.wait_ge(wproj_cast, 8)
            act.wait_ge(tab_step, 13)
            act.wait_ge(const_step, 18)

            def step(t, j):
                b = j % 2
                t1, j1 = back(t, j, 1)
                t2, j2 = back(t, j, 2)
                cross1 = j1 >= 2

                def evac_T(blk):
                    ln = (V_KXLN if cross1 else V_KLN) if blk == 0 else (V_QXLN if cross1 else V_QLN)
                    after(act, qk_transposed, 12, t1, 3 * j1 + blk + 1)
                    if blk == 0:
                        after(act, scores_done, 4, t2, j2 + 1)
                    tb = T_BANK[blk % 2]
                    act.activation(qkT[:, 4 * blk:4 * blk + 4, :].rearrange("p a b -> p (a b)"), bank[tb][:, :],
                                   ACT.Identity, scale=ln_scale[:, (ln - V_QLN) // 2:(ln - V_QLN) // 2 + 1],
                                   bias=vec[:, ln + 1:ln + 2]).then_inc(qkT_ready, 1)

                def evac_raw(blk):
                    after(act, proj_done, 16, t, 4 * j + blk + 1)
                    after(act, qk_transposed, 12, t2, 3 * j2 + blk + 1)
                    act.activation(raw[:, b, 4 * blk:4 * blk + 4, :].rearrange("p a b -> p (a b)"),
                                   bank[P_BANK[blk % 2]][:, :], ACT.Copy).then_inc(raw_ready, 1)

                def scale_cat(half):
                    if not has(t2, j2):
                        return
                    after(act, pv_done, 8, t2, 2 * j2 + half + 1)
                    t3, j3 = back(t, j, 3)
                    after(act, quant_step, 20, t3, 5 * j3 + 5)
                    for i in range(4):
                        lc = 4 * half + i
                        last = act.activation(cat[:, lc, :], bank[V_BANK][:, i * P:i * P + P], ACT.Copy,
                                              scale=inv_smooth[:, 8 * j2 + lc:8 * j2 + lc + 1])
                    last.then_inc(cat_scaled, 1)

                def tanh(place):
                    u, f = UNITS.get((j, place)), t - 2
                    if u is None or not ffn(f):
                        return
                    after(act, up_done, NU, f, u + 1)
                    after(act, gated, 14, f, 2 * u)
                    act.activation(th[:, :, :].rearrange("p c n -> p (c n)"), bank[H_BANK][:, 0:256], ACT.Tanh,
                                   scale=half_up[:, u // 2:u // 2 + 1]).then_inc(tanh_done, 1)

                if has(t1, j1):
                    evac_T(0)
                    evac_T(1)
                if has(t, j):
                    evac_raw(0)
                if has(t1, j1):
                    evac_T(2)
                if has(t, j):
                    evac_raw(1)
                tanh("early")
                if ffn(t - 1) and j == 3:
                    after(act, xn_transposed, 1, t - 1, 1)
                    after(act, gate_done, 1, t - 2, 1)
                    after(act, parts_step, 2, t - 2, 2)
                    act.activation(xnT[:, :, :].rearrange("p c n -> p (c n)"), bank[Y_BANK][:, 0:H],
                                   ACT.Copy).then_inc(xnT_ready, 1)
                if ffn(t - 2) and j == 0:
                    after(act, comb_transposed, 1, t - 2, 1)
                    after(act, spread_done, NB, t - 3, NB)
                    act.activation(combT[:, :], bank[Y_BANK][:, 384:448].bitcast(BF16), ACT.Copy).then_inc(combT_ready, 1)
                if has(t + 1) and j == 2:
                    after(act, z_transposed, 1, t + 1, 1)
                    after(act, xx_step, 6, t, 1)
                    after(act, xqkv_step, 6, t, 1)
                    for c in range(KC):
                        last = act.activation(zT[:, c, :], bank[T_BANK[0]][:, c * P:c * P + P], ACT.Identity,
                                              scale=vec[:, V_LNW + c:V_LNW + c + 1], bias=vec[:, V_LNB + c:V_LNB + c + 1])
                    last.then_inc(zT_ready, 1)
                if has(t, j):
                    evac_raw(2)
                if has(t2, j2):
                    after(act, p_transposed, 4, t2, j2 + 1)
                    t3, j3 = back(t, j, 3)
                    after(act, pv_done, 8, t3, 2 * j3 + 2)
                    tb = bank[T_BANK[1]][:, :].rearrange("p (g n) -> p g n", g=4)
                    act.activation(pT[0:64, :, 0, :], tb[0:64], ACT.Copy)
                    act.activation(pT[64:128, :, 1, :], tb[64:128], ACT.Copy).then_inc(pT_ready, 1)
                if has(t1, j1):
                    after(act, soft_step, 16, t1, 4 * j1 + 2)
                    after(act, p_ready, 4, t2, j2 + 1)
                    act.activation(ex[:, :, :], shifted[:, :, :], ACT.Exp, scale=SCALE).then_inc(exp_done, 1)
                if has(t, j):
                    after(act, proj_done, 16, t, 4 * j + 4)
                    after(act, pv_done, 8, t - 1, 2 * j + 2)
                    sc = sigma[:, 6 + j:7 + j] if j < 2 else 1.0
                    act.activation(vals[:, j, :], bank[P_BANK[1]][:, :], ACT.Copy, scale=sc).then_inc(v_ready, 1)
                if has(t) and j == 0:
                    after(act, c_transposed, 1, t, 1)
                    after(act, proj_done, 16, t - 1, 16)
                    act.activation(condT[:, :, :].rearrange("p c n -> p (c n)"), bank[T_BANK[0]][:, 0:H],
                                   ACT.Copy).then_inc(condT_ready, 1)
                if ffn(t - 2) and j == 0:
                    after(act, act_ready, NU, t - 3, NU)
                    for q in range(NB):
                        n = min(4, 2 * NU - 4 * q)
                        after(act, spread_done, NB, t - 2, q + 1)
                        act.activation(combs[:, 4 * q:4 * q + n, :].rearrange("p c n -> p (c n)"),
                                       bank[(H_BANK, Y_BANK)[q % 2]][:, 0:n * P], ACT.Copy,
                                       scale=both_up[:, q:q + 1]).then_inc(combs_ready, 1)
                if ffn(t - 1) and j == 3:
                    after(act, gate_step, 17, t - 1, 2)
                    act.activation(g_ex[:, :], g_sh[:, :], ACT.Exp).then_inc(gexp_done, 1)
                tanh("mid")
                scale_cat(0)
                tanh("late")
                scale_cat(1)

            run(act, step)

        @block.vector
        def _(dve):
            dve.memset(w_up[:, NU - 1, :, :, :, :], 0.0).then_inc(pad_zeroed, 1)
            dve.memset(w_down[96:128, 2 * NU - 1, :], 0.0).then_inc(pad_zeroed, 1)
            dve.wait_ge(s_vec, 16)
            dve.wait_ge(pad_zeroed, 2)

            def measure(k):
                _, n, centred, ty, _ = items[k]
                w = staged(k)
                dve.wait_ge(s_stage[k % 3], 16 * (k // 3 + 1))
                hs = headsum[:, k % 2, :]
                if centred:
                    w8 = w.rearrange("p c (h d) -> p (c h) d", d=P)
                    n = 3 * sum(items[i][2] for i in range(k))
                    dve.tensor_reduce(hs, w8, AX.X, ALU.add).then_inc(prep_centred, 1)
                    dve.wait_ge(prep_centred, n + 1)
                    dve.tensor_scalar(hs, hs, -1.0 / P, None, ALU.mult).then_inc(prep_centred, 1)
                    dve.wait_ge(prep_centred, n + 2)
                    dve.tensor_tensor(w8, w8, hs.unsqueeze(2).broadcast_to([P, 8, P]), ALU.add).then_inc(prep_centred, 1)
                    dve.wait_ge(prep_centred, n + 3)
                dve.tensor_reduce(absmax[:, k, :], w, AX.X, ALU.max, apply_absolute_value=True).then_inc(prep_max, 1)
                dve.wait_ge(prep_max, k + 1)
                if ty is not None:
                    dve.tensor_tensor(absmax[:, k, :], absmax[:, k, :], vec[:, V_IN + 2 * ty:V_IN + 2 * ty + 2],
                                      ALU.mult).then_inc(prep_scaled, 1)
                    dve.wait_ge(prep_scaled, k + 1)
                dve.tensor_reduce(rowmax[:, k:k + 1], absmax[:, k, :], AX.X, ALU.max,
                                  apply_absolute_value=True).then_inc(peak_step, 1)

            def split(k):
                _, n, centred, ty, _ = items[k]
                dve.wait_ge(factor_ready, k + 1)
                dve.tensor_scalar(peak[:, k:k + 1], peak[:, k:k + 1], 1e-30, 1.0 / TOP, ALU.max, ALU.mult).then_inc(fac_step, 1)
                dve.wait_ge(fac_step, 3 * k + 1)
                dve.reciprocal(rowmax[:, k:k + 1], peak[:, k:k + 1]).then_inc(fac_step, 1)
                dve.wait_ge(fac_step, 3 * k + 2)
                if ty is None:
                    dve.tensor_copy(factor[:, k, :], rowmax[:, k:k + 1].broadcast_to([P, KC])).then_inc(fac_step, 1)
                else:
                    dve.tensor_scalar(factor[:, k, :], vec[:, V_IN + 2 * ty:V_IN + 2 * ty + 2], rowmax[:, k:k + 1],
                                      None, ALU.mult).then_inc(fac_step, 1)
                dve.wait_ge(fac_step, 3 * k + 3)

            def low(k):
                dve.wait_ge(high_done, k + 1)
                for c in range(KC):
                    his = parts(k, 0, c)
                    for (dst, c0, n), (hi, _, _) in zip(parts(k, 1, c), his):
                        last = dve.scalar_tensor_tensor(dst, staged(k)[:, c, c0:c0 + n], factor[:, k, c:c + 1], hi,
                                                        ALU.mult, ALU.subtract)
                last.then_inc(low_done, 1)

            measure(0)
            for k in range(NI):
                if k + 1 < NI:
                    measure(k + 1)
                split(k)
                low(k)

            dve.wait_ge(s_wkv, 16)
            for c in range(KC):
                w8 = w_kv[:, c, 0:1024].rearrange("p (h d) -> p h d", d=P)
                dve.tensor_reduce(headsum[:, c, :], w8, AX.X, ALU.add).then_inc(tab_step, 1)
            dve.wait_ge(tab_step, 2)
            dve.tensor_scalar(headsum[:, :, :], headsum[:, :, :], -1.0 / P, None, ALU.mult).then_inc(tab_step, 1)
            dve.wait_ge(tab_step, 3)
            for c in range(KC):
                w8 = w_kv[:, c, 0:1024].rearrange("p (h d) -> p h d", d=P)
                dve.tensor_tensor(w8, w8, headsum[:, c, :].unsqueeze(2).broadcast_to([P, 8, P]), ALU.add)\
                   .then_inc(tab_step, 1)
            for ty, (a, n) in enumerate(((0, 4), (4, 2), (6, 2), (8, 4))):
                last = dve.tensor_scalar(sigma[:, a:a + n], peak[:, a:a + n], vec[:, V_WS + ty:V_WS + ty + 1], None, ALU.mult)
            last.then_inc(tab_step, 1)
            dve.wait_ge(tab_step, 6)
            dve.reciprocal(isig[:, :], sigma[:, :]).then_inc(tab_step, 1)
            dve.wait_ge(tab_step, 7)
            dve.scalar_tensor_tensor(eps_blk[:, :], isig[:, :], P * EPS, isig[:, :], ALU.mult, ALU.mult).then_inc(tab_step, 1)
            dve.wait_ge(tab_step, 8)
            dve.wait_ge(const_step, 18)
            for j in range(4):
                if j < 2:
                    dve.tensor_copy(eps_head[:, j, 0:4], eps_blk[:, 4 + j:5 + j].broadcast_to([P, 4]))
                for h in range(2):
                    k = 2 * (j % 2) + h + (8 if j >= 2 else 0)
                    last = dve.tensor_copy(eps_head[:, j, 4 + 4 * h:8 + 4 * h], eps_blk[:, k:k + 1].broadcast_to([P, 4]))
            last.then_inc(tab_step, 1)
            dve.reciprocal(inv_in[:, :], vec[:, V_IN:V_IN + 8])
            dve.reciprocal(inv_smooth[:, :], vec[:, V_SMOOTH:V_SMOOTH + 32])
            dve.tensor_scalar(ln_scale[:, :], vec[:, V_QLN:V_QLN + 8:2], float(P) ** 0.5, None, ALU.mult).then_inc(tab_step, 1)
            dve.tensor_tensor(out_scale[:, :], vec[:, V_PW:V_PW + 1], vec[:, V_PI:V_PI + 1], ALU.mult).then_inc(tab_step, 1)
            dve.tensor_scalar(half_up[:, :], peak[:, NA:NA + NB], 0.5, None, ALU.mult).then_inc(tab_step, 1)
            dve.tensor_tensor(both_up[:, :], peak[:, NA:NA + NB], peak[:, NA + NB:NA + 2 * NB], ALU.mult).then_inc(tab_step, 1)
            dve.wait_ge(tab_step, 13)

            def norm_stats(s, per, t, k, src, stat, mv):
                dve.bn_stats(stat[:, :], src[:, :]).then_inc(s, 1)
                after_apart(dve, s, per, t, k + 1)
                dve.bn_aggr(mv[:, :], stat[:, :]).then_inc(s, 1)

            def quantise(s, t, src, mask, dst, per, k, wait_dst):
                def clip():
                    dve.tensor_scalar(src, src, FP8_MAX, -FP8_MAX, ALU.min, ALU.max).then_inc(s, 1)

                def binade():
                    after(dve, s, per, t, k + 1)
                    dve.tensor_scalar(mask.bitcast(U16), src.bitcast(U16), 0x7F80, None, ALU.bitwise_and).then_inc(s, 1)

                def magic():
                    after(dve, s, per, t, k + 2)
                    dve.tensor_scalar(mask, mask, FP8_MIN_NORMAL, ROUND3, ALU.max, ALU.mult).then_inc(s, 1)

                def push():
                    after(dve, s, per, t, k + 3)
                    dve.tensor_tensor(src, src, mask, ALU.add).then_inc(s, 1)

                def pull():
                    after(dve, s, per, t, k + 4)
                    wait_dst()
                    dve.tensor_tensor(dst, src, mask, ALU.subtract).then_inc(s, 1)
                return clip, binade, magic, push, pull

            def step(t, j):
                b = j % 2
                t1, j1 = back(t, j, 1)
                t2, j2 = back(t, j, 2)
                t3, j3 = back(t, j, 3)
                flat = "p a b -> p (a b)"

                def nothing():
                    return None

                clip = binade = magic = push = pull = nothing
                if has(t3, j3):
                    t4, j4 = back(t, j, 4)
                    clip, binade, magic, push, pull = quantise(
                        quant_step, t3, cat[:, :, :].rearrange(flat), catm[:, :, :].rearrange(flat),
                        catq[:, :, :].rearrange(flat), 20, 5 * j3,
                        lambda: after(dve, o_done, 4, t4, j4 + 1))

                def head_stats(blk):
                    if not has(t, j):
                        return
                    after(dve, raw_ready, 12, t, 3 * j + blk + 1)
                    if blk == 0:
                        after(dve, rstd_step, 28, t2, 7 * j2 + 7)
                    for h in range(4 * blk, 4 * blk + 4):
                        last = dve.bn_stats(stats[:, b, h, :], raw[:, b, h, :])
                    if blk == 2:
                        last.then_inc(stats_done, 1)

                def normalise(blk):
                    if not has(t, j):
                        return
                    if blk == 0:
                        after(dve, rstd_step, 28, t, 7 * j + 7)
                    r = raw[:, b, 4 * blk:4 * blk + 4, :]
                    dve.tensor_tensor(r, r, rstd[:, b, 4 * blk:4 * blk + 4].unsqueeze(2).broadcast_to([P, 4, P]),
                                      ALU.mult).then_inc(xhat_ready, 1)

                f = t - 1
                routing = ffn(f) and j == 3
                lg = bank[Y_BANK][:, 256:256 + E]
                sc_f = g_sc[:, :].unsqueeze(1).broadcast_to([P, E, E])
                sc_e = g_sc[:, :].unsqueeze(2).broadcast_to([P, E, E])
                sc = bank[S_BANK][:, :].rearrange("p (g t) -> p g t", t=64)

                def gate_unit(place):
                    u, fu = UNITS.get((j, place)), t - 2
                    if u is None or not ffn(fu):
                        return
                    after(dve, tanh_done, NU, fu, u + 1)
                    if u == 0:
                        after(dve, act_ready, NU, fu - 1, NU)
                    else:
                        after(dve, act_ready, NU, fu, u)
                    dve.scalar_tensor_tensor(gu[:, :, :].rearrange(flat), th[:, :, :].rearrange(flat), 1.0,
                                             bank[H_BANK][:, 0:256], ALU.add, ALU.mult).then_inc(gated, 1)
                    after(dve, gated, 14, fu, 2 * u + 1)
                    dve.tensor_tensor(gu[:, :, :].rearrange(flat), gu[:, :, :].rearrange(flat),
                                      bank[H_BANK][:, 256:512], ALU.mult).then_inc(gated, 1)

                def scaled_input(ty):
                    for c in range(KC):
                        last = dve.tensor_scalar(xs[:, ty, c, :], zT[:, c, :], inv_in[:, 2 * ty + c:2 * ty + c + 1], None, ALU.mult)
                    return last

                xclip = xbinade = xmagic = xpush = xpull = nothing
                if has(t + 1) and j == 2:
                    whole = "p a b c -> p (a b c)"
                    xclip, xbinade, xmagic, xpush, xpull = quantise(
                        xqkv_step, t + 1, xs[:, 0:3].rearrange(whole), xm[:, 0:3].rearrange(whole),
                        xq[:, 0:3].rearrange(whole), 6, 1, lambda: after(dve, proj_done, 16, t, 8))
                if has(t) and j == 0:
                    xclip, xbinade, xmagic, xpush, xpull = quantise(
                        xx_step, t, xs[:, 3].rearrange(flat), xm[:, 3].rearrange(flat),
                        xq[:, 3].rearrange(flat), 6, 1, lambda: after(dve, proj_done, 16, t - 1, 16))

                if has(t3, j3):
                    after(dve, cat_scaled, 8, t3, 2 * j3 + 2)
                clip()
                if has(t + 1) and j == 1:
                    after(dve, ln1_pow, 4, t + 1, 2)
                    dve.tensor_scalar(yln[:, :], xin[:, :], ln_mv[:, 0:1], ln_r[:, :], ALU.subtract, ALU.mult).then_inc(ln1_step, 1)
                if has(t + 1) and j == 2:
                    after(dve, ln1_pow, 4, t + 1, 4)
                    after(dve, z_transposed, 1, t, 1)
                    dve.tensor_scalar(zln[:, :], yln[:, :], ln_mv[:, 0:1], ln_r[:, :], ALU.subtract, ALU.mult).then_inc(ln1_step, 1)
                binade()
                if routing:
                    after(dve, ln2_pow, 2, f, 2)
                    after(dve, xn_transposed, 1, f - 1, 1)
                    dve.tensor_scalar(xn[:, :], x1[:, :], f_mv[:, 0:1], f_r[:, :], ALU.subtract, ALU.mult).then_inc(ln2_step, 1)
                magic()
                if has(t + 1) and j == 1:
                    after(dve, ln1_step, 6, t + 1, 3)
                    dve.bn_stats(ln_stat[:, :], yln[:, :]).then_inc(ln1_step, 1)
                push()
                if has(t + 1) and j == 1:
                    after_apart(dve, ln1_step, 6, t + 1, 4)
                    dve.bn_aggr(ln_mv[:, :], ln_stat[:, :]).then_inc(ln1_step, 1)
                pull()
                head_stats(0)
                head_stats(1)
                gate_unit("early")
                head_stats(2)
                if routing:
                    after(dve, xnT_ready, 1, f, 1)
                    after(dve, up_done, NU, f - 1, NU)
                    dve.tensor_copy(xnp[:, 0, :, :], xnT[:, :, :]).then_inc(parts_step, 1)
                if has(t1, j1):
                    after(dve, scores_done, 4, t1, j1 + 1)
                    dve.tensor_reduce(smax[:, :], sc, AX.X, ALU.max).then_inc(soft_step, 1)
                if routing:
                    after(dve, parts_step, 2, f, 1)
                    dve.tensor_tensor(xnp[:, 1, :, :], xnT[:, :, :], xnp[:, 0, :, :], ALU.subtract).then_inc(parts_step, 1)
                if has(t1, j1):
                    after(dve, soft_step, 16, t1, 4 * j1 + 1)
                    after(dve, exp_done, 4, t2, j2 + 1)
                    dve.tensor_tensor(shifted[:, :, :], sc, smax[:, :].unsqueeze(2).broadcast_to([P, 8, 64]),
                                      ALU.subtract).then_inc(soft_step, 1)
                if has(t + 1) and j == 0:
                    after(dve, x_in, 16, t + 1, 16)
                    after(dve, ln1_pow, 4, t, 3)
                    after(dve, ln1_step, 6, t, 6)
                    norm_stats(ln1_step, 6, t + 1, 0, xin, ln_stat, ln_mv)
                if has(t) and j == 0:
                    after(dve, zT_ready, 1, t, 1)
                    scaled_input(TX).then_inc(xx_step, 1)
                if has(t + 1) and j == 2:
                    after(dve, zT_ready, 1, t + 1, 1)
                    for ty in (TQ, TK, TV):
                        last = scaled_input(ty)
                    last.then_inc(xqkv_step, 1)
                if routing:
                    after(dve, gate_done, 1, f, 1)
                    dve.tensor_reduce(g_col[:, 0:1], lg, AX.X, ALU.max).then_inc(gate_step, 1)
                if has(t1, j1):
                    after(dve, exp_done, 4, t1, j1 + 1)
                    after(dve, p_ready, 4, t2, j2 + 1)
                    dve.tensor_reduce(rsum[:, :], ex[:, :, :], AX.X, ALU.add).then_inc(soft_step, 1)
                if routing:
                    after(dve, gate_step, 17, f, 1)
                    dve.tensor_scalar(g_sh[:, :], lg, g_col[:, 0:1], None, ALU.subtract).then_inc(gate_step, 1)
                if has(t + 1) and j == 2:
                    after(dve, xqkv_step, 6, t + 1, 1)
                if has(t) and j == 0:
                    after(dve, xx_step, 6, t, 1)
                xclip()
                if has(t1, j1):
                    after(dve, soft_step, 16, t1, 4 * j1 + 3)
                    dve.reciprocal(rinv[:, :], rsum[:, :]).then_inc(soft_step, 1)
                xbinade()
                gate_unit("mid")
                normalise(0)
                if routing:
                    after(dve, gexp_done, 1, f, 1)
                    dve.tensor_reduce(g_col[:, 1:2], g_ex[:, :], AX.X, ALU.add).then_inc(gate_step, 1)
                xmagic()
                normalise(1)
                if routing:
                    after(dve, gate_step, 17, f, 3)
                    dve.reciprocal(g_col[:, 2:3], g_col[:, 1:2]).then_inc(gate_step, 1)
                xpush()
                normalise(2)
                if routing:
                    after(dve, gate_step, 17, f, 4)
                    dve.tensor_scalar(g_sc[:, :], g_ex[:, :], g_col[:, 2:3], None, ALU.mult).then_inc(gate_step, 1)
                xpull()
                if has(t3, j3):
                    after(dve, o_done, 4, t3, j3 + 1)
                    if j3 == 0:
                        after(dve, r_in, 16, t3, 16)
                    else:
                        after(dve, o_added, 4, t3, j3)
                    if j3 == 3:
                        after(dve, x1_kept, 1, t3 - 1, 1)
                    dst = x1 if j3 == 3 else xres
                    dve.scalar_tensor_tensor(dst[:, :], bank[S_BANK][:, 0:H], out_scale[:, :], xres[:, :],
                                             ALU.mult, ALU.add).then_inc(o_added, 1)
                gate_unit("late")
                if ffn(f) and j == 2:
                    after(dve, o_added, 4, f, 4)
                    after(dve, ln2_pow, 2, f - 1, 1)
                    norm_stats(ln2_step, 3, f, 0, x1, f_stat, f_mv)
                if ffn(t - 2) and j == 2:
                    after(dve, down_done, NU, t - 2, NU)
                    after(dve, x1_kept, 1, t - 2, 1)
                    after(dve, out_sent, 16, t - 3, 16)
                    dve.tensor_tensor(yout[:, :], bank[Y_BANK][:, 0:H], x1keep[:, :], ALU.add).then_inc(out_ready, 1)
                if routing:
                    after(dve, gate_step, 17, f, 5)
                    dve.tensor_tensor(g_gt[:, :, :], sc_f, sc_e, ALU.is_gt).then_inc(gate_step, 1)
                    dve.tensor_tensor(g_eq[:, :, :], sc_f, sc_e, ALU.is_equal).then_inc(gate_step, 1)
                    after(dve, gate_step, 17, f, 7)
                    dve.tensor_tensor(g_eq[:, :, :], g_eq[:, :, :], tri[:, :, :], ALU.mult).then_inc(gate_step, 1)
                    after(dve, gate_step, 17, f, 8)
                    dve.tensor_tensor(g_gt[:, :, :], g_gt[:, :, :], g_eq[:, :, :], ALU.add).then_inc(gate_step, 1)
                    after(dve, gate_step, 17, f, 9)
                    dve.tensor_reduce(g_rank[:, :], g_gt[:, :, :], AX.X, ALU.add).then_inc(gate_step, 1)
                    after(dve, gate_step, 17, f, 10)
                    dve.scalar_tensor_tensor(g_sel[:, :], g_rank[:, :], 1.5, g_sc[:, :], ALU.is_lt, ALU.mult).then_inc(gate_step, 1)
                    after(dve, gate_step, 17, f, 11)
                    dve.tensor_reduce(g_col[:, 3:4], g_sel[:, :], AX.X, ALU.add).then_inc(gate_step, 1)
                    after(dve, gate_step, 17, f, 12)
                    dve.reciprocal(g_col[:, 4:5], g_col[:, 3:4]).then_inc(gate_step, 1)
                    after(dve, gate_step, 17, f, 13)
                    dve.tensor_scalar(comb[:, :], g_sel[:, :], g_col[:, 4:5], 0.5, ALU.mult, ALU.mult).then_inc(gate_step, 1)
                    after(dve, gate_step, 17, f, 14)
                    after(dve, comb_transposed, 1, f - 1, 1)
                    dve.tensor_copy(comb3[:, 0, 0:E], comb[:, :]).then_inc(gate_step, 1)
                    after(dve, gate_step, 17, f, 15)
                    dve.tensor_tensor(rest[:, :], comb[:, :], comb3[:, 0, 0:E], ALU.subtract).then_inc(gate_step, 1)
                    after(dve, gate_step, 17, f, 16)
                    dve.tensor_copy(comb3[:, 1, 0:E], rest[:, :]).then_inc(gate_step, 1)
                    after(dve, gate_step, 17, f, 17)
                    dve.tensor_tensor(comb3[:, 2, 0:E], rest[:, :], comb3[:, 1, 0:E], ALU.subtract).then_inc(comb3_ready, 1)

            run(dve, step)

        @block.tensor
        def _(pe):
            pe.wait_ge(const_step, 18)
            pe.wait_ge(tab_step, 13)
            pe.wait_ge(low_done, NI)
            pe.wait_ge(high_done, NI)
            pe.wait_ge(wproj_cast, 8)
            pe.wait_ge(s_wd, 32)
            pe.wait_ge(s_wg, 16)

            def transposes(dst, src, n):
                for i in range(n):
                    last = nc.tensor.transpose(bank[dst][:, i * P:i * P + P], src(i), ident[:, :])
                return last

            def step(t, j):
                b = j % 2
                t1, j1 = back(t, j, 1)
                t2, j2 = back(t, j, 2)
                t3, j3 = back(t, j, 3)
                cross = j >= 2

                def transpose_qk(blk):
                    after(pe, xhat_ready, 12, t1, 3 * j1 + blk + 1)
                    if blk == 0:
                        after(pe, qkT_ready, 12, t2, 3 * j2 + 3)
                        if has(t + 1) and j == 3:
                            after(pe, zT_ready, 1, t + 1, 1)
                        if has(t) and j == 1:
                            after(pe, condT_ready, 1, t, 1)
                    elif blk == 1:
                        after(pe, pT_ready, 4, t3, j3 + 1)
                    else:
                        after(pe, qkT_ready, 12, t1, 3 * j1 + 1)
                    tb = bank[T_BANK[blk % 2]]
                    by_head = tb[:, :].rearrange("p (g b h s) -> p g h b s", g=2, b=2, h=2)
                    for i in range(4):
                        dst = tb[:, i * P:i * P + P] if blk == 0 else by_head[:, i // 2, i % 2]
                        last = nc.tensor.transpose(dst, raw[:, 1 - b, 4 * blk + i, :], ident[:, :])
                    last.then_inc(qk_transposed, 1)

                def project(blk):
                    if blk == 0:
                        after(pe, raw_ready, 12, t1, 3 * j1 + 3)
                        if j == 0:
                            after(pe, xqkv_step, 6, t, 6)
                        if j == 2:
                            after(pe, condT_ready, 1, t, 1)
                            after(pe, xx_step, 6, t, 6)
                    elif blk == 1:
                        after(pe, v_ready, 4, t1, j1 + 1)
                    else:
                        after(pe, raw_ready, 12, t, 3 * j + blk - 1)
                    dst = bank[P_BANK[blk % 2]][:, :]
                    if cross and blk in (0, 3):
                        c0 = (1024 if blk == 3 else 0) + 512 * (j % 2)
                        for c in range(KC):
                            last = nc.tensor.matmul(dst, condT[:, c, :], w_kv[:, c, c0:c0 + BLK],
                                                    start=(c == 0), stop=(c == KC - 1))
                    else:
                        h = j % 2
                        ty, w = {0: (TK, 4 + h), 3: (TV, 6 + h)}.get(blk, (None, None))
                        if ty is None:
                            ty, w = (TX, 8 + 2 * h + blk - 1) if cross else (TQ, 2 * h + blk - 1)
                        for c in range(KC):
                            for part in range(2):
                                last = nc.tensor.matmul(dst, xq[:, ty, c, :], w_attn[:, w, part, c, :],
                                                        start=(c == 0 and part == 0), stop=(c == KC - 1 and part == 1))
                    last.then_inc(proj_done, 1)

                def values(half):
                    if half == 0:
                        after(pe, pT_ready, 4, t2, j2 + 1)
                        after(pe, v_ready, 4, t2, j2 + 1)
                        after(pe, cat_scaled, 8, t3, 2 * j3 + 2)
                    else:
                        after(pe, cat_scaled, 8, t2, 2 * j2 + 1)
                    for i in range(2):
                        g = 2 * half + i
                        last = nc.tensor.matmul(bank[V_BANK][:, 256 * i:256 * i + 256], vals[:, j2, g * P:g * P + P],
                                                pT[:, g, :, :].rearrange("p b (h s) -> p h b s", h=2),
                                                start=True, stop=True)
                    last.then_inc(pv_done, 1)

                def up(u):
                    fu = t - 2
                    if u == 0:
                        after(pe, combs_ready, NB, fu, 3)
                        after(pe, parts_step, 2, fu, 2)
                    else:
                        after(pe, gated, 14, fu, 2 * u)
                    for w in range(2):
                        for ch in range(2):
                            dst = bank[H_BANK][:, 256 * w + P * ch:256 * w + P * ch + P]
                            n = 0
                            for c in range(KC):
                                for wp, xp in ((0, 0), (0, 1), (1, 0)):
                                    last = nc.tensor.matmul(dst, w_up[:, u, wp, w, c, P * ch:P * ch + P], xnp[:, xp, c, :],
                                                            start=(n == 0), stop=(n == 5))
                                    n += 1
                    last.then_inc(up_done, 1)

                def down(u):
                    fu = t - 2
                    after(pe, act_ready, NU, fu, u + 1)
                    if u == 0:
                        after(pe, combs_ready, NB, fu, NB)
                    for ch in range(2):
                        last = nc.tensor.matmul(bank[Y_BANK][:, 0:H], act_ff[:, u % 2, ch, :], w_down[:, 2 * u + ch, :],
                                                start=(u == 0 and ch == 0), stop=(u == NU - 1 and ch == 1))
                    last.then_inc(down_done, 1)

                def feed(place):
                    u = UNITS.get((j, place))
                    if ffn(t - 2) and u is not None:
                        up(u)
                        if u > 0:
                            down(u - 1)

                if has(t1, j1):
                    transpose_qk(0)
                    transpose_qk(1)
                if has(t, j):
                    project(0)
                if has(t1, j1):
                    transpose_qk(2)
                if has(t, j):
                    project(1)
                feed("early")
                if ffn(t - 1) and j == 3:
                    after(pe, ln2_step, 3, t - 1, 3)
                    after(pe, out_ready, 1, t - 2, 1)
                    transposes(Y_BANK, lambda i: xn[:, i * P:i * P + P], 2).then_inc(xn_transposed, 1)
                if ffn(t - 2) and j == 0:
                    after(pe, comb3_ready, 1, t - 2, 1)
                    after(pe, xnT_ready, 1, t - 2, 1)
                    nc.tensor.transpose(bank[Y_BANK][:, 384:448].bitcast(BF16), comb3[:, :, :].rearrange("p a b -> p (a b)"),
                                        ident16[:, :]).then_inc(comb_transposed, 1)
                if has(t + 1) and j == 2:
                    after(pe, ln1_step, 6, t + 1, 6)
                    after(pe, qkT_ready, 12, t1, 3 * j1 + 3)
                    transposes(T_BANK[0], lambda i: zln[:, i * P:i * P + P], 2).then_inc(z_transposed, 1)
                if has(t, j):
                    project(2)
                if has(t1, j1):
                    after(pe, qkT_ready, 12, t1, 3 * j1 + 3)
                    t4, j4 = back(t, j, 4)
                    after(pe, o_added, 4, t4, j4 + 1)
                    for g in range(4):
                        for bt in range(2):
                            last = nc.tensor.matmul(bank[S_BANK][:, P * g + 64 * bt:P * g + 64 * bt + 64],
                                                    qkT[:, 4 + 2 * g + bt, :],
                                                    qkT[:, g, 64 * bt:64 * bt + 64], start=True, stop=True)
                    last.then_inc(scores_done, 1)
                if has(t2, j2):
                    after(pe, p_ready, 4, t2, j2 + 1)
                    after(pe, qkT_ready, 12, t1, 3 * j1 + 2)
                    transposes(T_BANK[1], lambda i: probs[:, i, :], 4).then_inc(p_transposed, 1)
                if has(t, j):
                    project(3)
                if has(t) and j == 0:
                    after(pe, c_in, 16, t, 16)
                    after(pe, qkT_ready, 12, t1, 3 * j1 + 3)
                    transposes(T_BANK[0], lambda i: cin[:, i * P:i * P + P], 2).then_inc(c_transposed, 1)
                if ffn(t - 2) and j == 0:
                    after(pe, combT_ready, 1, t - 2, 1)
                    after(pe, gated, 14, t - 3, 14)
                    for q in range(NB):
                        if q >= 2:
                            after(pe, combs_ready, NB, t - 2, q - 1)
                        for i in range(4 * q, min(4 * q + 4, 2 * NU)):
                            last = nc.tensor.matmul(bank[(H_BANK, Y_BANK)[q % 2]][:, P * (i % 4):P * (i % 4) + P],
                                                    expert_rows[:, P * i:P * i + P], combT[:, :], start=True, stop=True)
                        last.then_inc(spread_done, 1)
                if ffn(t - 1) and j == 3:
                    after(pe, xnT_ready, 1, t - 1, 1)
                    for c in range(KC):
                        last = nc.tensor.matmul(bank[Y_BANK][:, 256:256 + E], xnT[:, c, :], w_gate[:, c, :],
                                                start=(c == 0), stop=(c == KC - 1))
                    last.then_inc(gate_done, 1)
                feed("mid")
                if has(t3, j3):
                    after(pe, quant_step, 20, t3, 5 * j3 + 5)
                    after(pe, soft_step, 16, t1, 4 * j1 + 2)
                    for i in range(8):
                        last = nc.tensor.matmul(bank[S_BANK][:, 0:H], catq[:, i, :], w_proj[:, 8 * j3 + i, :],
                                                start=(i == 0), stop=(i == 7))
                    last.then_inc(o_done, 1)
                if has(t2, j2):
                    values(0)
                feed("late")
                if ffn(t - 2) and j == 2:
                    down(NU - 1)
                if has(t2, j2):
                    values(1)

            run(pe, step)


def kernel(**a):
    import numpy as np
    import concourse.bacc as bacc
    from concourse.bass_utils import run_bass_kernel_spmd

    pre = "L0_xattn_"
    ff = "L0_ffn_"
    a = {k: np.asarray(v) for k, v in a.items()}

    def turned(w):
        return np.ascontiguousarray(w.T)

    def inner(w, s):
        return np.ascontiguousarray(np.concatenate([np.transpose(w, (1, 0, 2)).reshape(H, E * I), s], axis=1))

    def column(v):
        return v.reshape(-1, P).T

    def spread(v):
        return np.broadcast_to(v.reshape(1, 1), (P, 1))

    names = ["q_in_scale", "k_in_scale", "v_in_scale", "qx_in_scale", "ln_w", "ln_b", "qln_w", "qln_b", "kln_w", "kln_b",
             "qxln_w", "qxln_b", "kxln_w", "kxln_b", "proj_smooth"]
    scalars = ["wq_scale", "wk_scale", "wv_scale", "wqx_scale", "proj_w_scale", "proj_in_scale"]
    vecs = np.ascontiguousarray(np.concatenate([column(a[pre + n]) for n in names] + [spread(a[pre + n]) for n in scalars],
                                               axis=1))
    arrays = {
        "x": a["x"].reshape(-1, H), "cond": a["ctx_2048"].reshape(-1, H),
        "wqT": turned(a[pre + "wq"]), "wkT": turned(a[pre + "wk"]), "wvT": turned(a[pre + "wv"]),
        "wqxT": turned(a[pre + "wqx"]), "wkvT": turned(a[pre + "w_kv_x"]), "wprojT": turned(a[pre + "wproj"]),
        "w1T": inner(a[ff + "w1"], a[ff + "sw1"]), "w3T": inner(a[ff + "w3"], a[ff + "sw3"]),
        "w2": np.ascontiguousarray(np.concatenate([a[ff + "w2"].reshape(E * I, H), a[ff + "sw2"]], axis=0)),
        "gateT": turned(a[ff + "gate_w"]), "vecs": vecs,
    }
    nc = bacc.Bacc("TRN2", target_bir_lowering=False, num_devices=1)
    args = [nc.dram_tensor(f"in_{n}", v.shape, mybir.dt.from_np(v.dtype), kind="ExternalInput").ap() for n, v in arrays.items()]
    out = nc.dram_tensor("out", (TILES * P, H), F32, kind="ExternalOutput").ap()
    bass_xattn_moe(nc, *args, out)
    r = run_bass_kernel_spmd(nc, [{f"in_{n}": v for n, v in arrays.items()}], core_ids=[0])
    return r.results[0]["out"].reshape(a["x"].shape)
```

```python
from contextlib import ExitStack

import concourse.bass as bass
from concourse import mybir

F32 = mybir.dt.float32
F16 = mybir.dt.float16
BF16 = mybir.dt.bfloat16
U16 = mybir.dt.uint16
ALU = mybir.AluOpType
ACT = mybir.ActivationFunctionType
AX = mybir.AxisListType
RMAX = bass.bass_isa.ReduceOp.max

P = 128
H = 256
KC = H // P
NH, G = 16, 8
E, I, SI = 8, 176, 352
NE = E + SI // I
FI = NE * I
NU = -(-FI // 256)
NB = -(-FI // 512)
BLK = 512
TILES = 32
QUADS = 4 * TILES
EPS = 1e-5
FP8_MAX = 448.0
TOP = 1024.0
SCALE = float(P) ** -0.5
FP8_MIN_NORMAL = 2.0 ** -6
ROUND3 = 24.0

V_IN, V_LNW, V_LNB = 0, 8, 10
V_QLN, V_KLN, V_QXLN, V_KXLN = 12, 14, 16, 18
V_SMOOTH, V_WS, V_PW, V_PI = 20, 52, 56, 57
NV = 58

TQ, TK, TV, TX = range(4)
ATTN_BLOCKS = ([(TQ, 0, 512 * b, True) for b in range(4)] + [(TK, 1, 512 * b, True) for b in range(2)]
               + [(TV, 2, 512 * b, False) for b in range(2)] + [(TX, 3, 512 * b, True) for b in range(4)])
NA = len(ATTN_BLOCKS)
NSELF = 8
LATER = {(0, 0): (8, 9), (0, 1): (10, 11), (0, 2): (12, 13), (0, 3): (14, 15), (1, 0): (16, 17), (1, 1): (18,), (1, 2): (19,)}
UNITS = {(0, "mid"): 0, (1, "early"): 1, (1, "mid"): 2, (1, "late"): 3, (2, "early"): 4, (2, "mid"): 5, (3, "early"): 6}


def back(t, j, d):
    return t + (j - d) // 4, (j - d) % 4


def bass_xattn_moe(nc, x, cond, wqT, wkT, wvT, wqxT, wkvT, wprojT, w1T, w3T, w2, gateT, vecs, out):
    es = ExitStack()
    with es:
        def sb(name, shape, dt=F32):
            return es.enter_context(nc.sbuf_tensor(name, shape, dt))

        def sem(name):
            return es.enter_context(nc.semaphore(name))

        w_attn = sb("w_attn", [P, NA, 2, KC, BLK], F16)
        w_kv = sb("w_kv", [P, KC, 2048])
        w_proj = sb("w_proj", [P, 32, H], BF16)
        w_up = sb("w_up", [P, NU, 2, 2, KC, 256], F16)
        w_down = sb("w_down", [P, 2 * NU, H])
        w_gate = sb("w_gate", [P, KC, E])
        vec = sb("vec", [P, NV])
        ident = sb("ident", [P, P])
        ident16 = sb("ident16", [P, P], BF16)
        expert_rows = sb("expert_rows", [P, 2 * NU * P], BF16)
        tri = sb("tri", [P, E, E])
        minus_half = sb("minus_half", [P, 12])
        inv_in = sb("inv_in", [P, 8])
        inv_smooth = sb("inv_smooth", [P, 32])
        ln_scale = sb("ln_scale", [P, 4])
        eps_head = sb("eps_head", [P, 4, 12])
        out_scale = sb("out_scale", [P, 1])
        absmax = sb("absmax", [P, NA + 2 * NB, KC])
        rowmax = sb("rowmax", [P, NA + 2 * NB])
        peak = sb("peak", [P, NA + 2 * NB])
        factor = sb("factor", [P, NA + 2 * NB, KC])
        headsum = sb("headsum", [P, 2, 8])
        sigma = sb("sigma", [P, NA])
        isig = sb("isig", [P, NA])
        eps_blk = sb("eps_blk", [P, NA])
        half_up = sb("half_up", [P, NB])
        both_up = sb("both_up", [P, NB])

        xin = sb("xin", [P, H])
        cin = sb("cin", [P, H])
        xres = sb("xres", [P, H])
        ln_stat = sb("ln_stat", [P, 6])
        ln_mv = sb("ln_mv", [P, 2])
        ln_r = sb("ln_r", [P, 1])
        yln = sb("yln", [P, H])
        zln = sb("zln", [P, H])
        zT = sb("zT", [P, KC, P])
        condT = sb("condT", [P, KC, P])
        xs = sb("xs", [P, 4, KC, P], BF16)
        xm = sb("xm", [P, 4, KC, P], BF16)
        xq = sb("xq", [P, 4, KC, P], BF16)

        raw = sb("raw", [P, 2, 12, P])
        stats = sb("stats", [P, 2, 12, 6])
        st_a = sb("st_a", [P, 12])
        st_b = sb("st_b", [P, 12])
        rstd = sb("rstd", [P, 2, 12])
        qkT = sb("qkT", [P, 12, P])
        vals = sb("vals", [P, 4, BLK])
        smax = sb("smax", [P, 8])
        shifted = sb("shifted", [P, 8, 64])
        ex = sb("ex", [P, 8, 64])
        rsum = sb("rsum", [P, 8])
        rinv = sb("rinv", [P, 8])
        probs = sb("probs", [P, 4, P])
        pT = sb("pT", [P, 4, 2, P])
        cat = sb("cat", [P, 8, P], BF16)
        catm = sb("catm", [P, 8, P], BF16)
        catq = sb("catq", [P, 8, P], BF16)

        x1 = sb("x1", [P, H])
        x1keep = sb("x1keep", [P, H])
        f_stat = sb("f_stat", [P, 6])
        f_mv = sb("f_mv", [P, 2])
        f_r = sb("f_r", [P, 1])
        xn = sb("xn", [P, H])
        xnT = sb("xnT", [P, KC, P])
        xnp = sb("xnp", [P, 2, KC, P], F16)
        g_col = sb("g_col", [P, 8])
        g_sh = sb("g_sh", [P, E])
        g_ex = sb("g_ex", [P, E])
        g_sc = sb("g_sc", [P, E])
        g_gt = sb("g_gt", [P, E, E])
        g_eq = sb("g_eq", [P, E, E])
        g_rank = sb("g_rank", [P, E])
        g_sel = sb("g_sel", [P, E])
        comb = sb("comb", [P, E])
        rest = sb("rest", [P, E])
        comb3 = sb("comb3", [P, 4, 32], BF16)
        combT = sb("combT", [P, P], BF16)
        combs = sb("combs", [P, 2 * NU, P])
        th = sb("th", [P, 2, P])
        gu = sb("gu", [P, 2, P])
        act_ff = sb("act_ff", [P, 2, 2, P])
        yout = sb("yout", [P, H])

        bank = [es.enter_context(nc.psum_tensor(f"bank{i}", [P, 512], F32)) for i in range(8)]
        P_BANK, T_BANK, S_BANK, V_BANK, H_BANK, Y_BANK = (0, 1), (2, 3), 4, 5, 6, 7

        stage = [w_down[:, 0:4, :].rearrange("p a b -> p (a b)"), sb("stage", [P, KC * BLK])[:, :],
                 combs[:, 0:8, :].rearrange("p a b -> p (a b)")]
        wp_stage = [vals[:, 2 * i:2 * i + 2, :].rearrange("p a b -> p (a b)") for i in range(2)]

        s_vec, s_wkv, s_wd, s_wg = sem("vec_in"), sem("wkv_in"), sem("wdown_in"), sem("wgate_in")
        s_wp = [sem(f"wproj_in{i}") for i in range(2)]
        s_stage = [sem(f"stage_in{i}") for i in range(3)]
        prep_centred, prep_max, prep_scaled = sem("prep_centred"), sem("prep_max"), sem("prep_scaled")
        fac_step = sem("fac_step")
        peak_step = sem("peak_step")
        factor_ready = sem("factor_ready")
        high_done = sem("high_done")
        low_done = sem("low_done")
        wproj_cast = sem("wproj_cast")
        const_step = sem("const_step")
        tab_step = sem("tab_step")
        kv_centred = sem("kv_centred")
        pad_zeroed = sem("pad_zeroed")
        apart = sem("apart")
        x_in, c_in, r_in, out_sent = sem("x_in"), sem("cond_in"), sem("res_in"), sem("out_sent")
        z_transposed, c_transposed = sem("z_transposed"), sem("cond_transposed")
        proj_done, qk_transposed, scores_done = sem("proj_done"), sem("qk_transposed"), sem("scores_done")
        p_transposed, pv_done, o_done = sem("p_transposed"), sem("pv_done"), sem("o_done")
        xn_transposed, gate_done, comb_transposed = sem("xn_transposed"), sem("gate_done"), sem("comb_transposed")
        spread_done, up_done, down_done = sem("spread_done"), sem("up_done"), sem("down_done")
        zT_ready, condT_ready, raw_ready, v_ready = sem("zT_ready"), sem("condT_ready"), sem("raw_ready"), sem("v_ready")
        qkT_ready, exp_done, pT_ready, cat_scaled = sem("qkT_ready"), sem("exp_done"), sem("pT_ready"), sem("cat_scaled")
        xnT_ready, gexp_done, combT_ready = sem("xnT_ready"), sem("gate_exp_done"), sem("combT_ready")
        combs_ready, tanh_done = sem("combs_ready"), sem("tanh_done")
        ln1_step, xqkv_step, xx_step = sem("ln1_step"), sem("xqkv_step"), sem("xx_step")
        stats_done, xhat_ready, soft_step, quant_step = sem("stats_done"), sem("xhat_ready"), sem("soft_step"), sem("quant_step")
        o_added, ln2_step, parts_step, gate_step = sem("o_added"), sem("ln2_step"), sem("parts_step"), sem("gate_step")
        gated, out_ready, comb3_ready = sem("gated"), sem("out_ready"), sem("comb3_ready")
        ln1_pow, ln2_pow, rstd_step, p_ready = sem("ln1_pow"), sem("ln2_pow"), sem("rstd_step"), sem("p_ready")
        x1_kept, act_ready = sem("x1_kept"), sem("act_ready")

        def after(eng, s, per, t, k):
            if not isinstance(t, int):
                eng.wait_ge(s, per * t + k)
            elif per * t + k > 0:
                eng.wait_ge(s, min(per * t + k, per * TILES))

        def after_apart(eng, s, per, t, k):
            after(eng, s, per, t, k)
            eng.sem_inc(apart, 1)

        def has(t, j=0):
            return not isinstance(t, int) or 0 <= 4 * t + j < QUADS

        def ffn(t):
            return not isinstance(t, int) or 0 <= t < TILES

        def run(eng, step):
            for j in (0, 1, 2, 3):
                step(-1, j)
            for t in (0, 1, 2):
                for j in range(4):
                    step(t, j)
            with eng.Fori(3, TILES - 1) as t:
                for j in range(4):
                    step(t, j)
            for t in (TILES - 1, TILES, TILES + 1):
                for j in range(4):
                    step(t, j)

        sources = (wqT, wkT, wvT, wqxT)
        items = []
        for b, (ty, w, c0, centred) in enumerate(ATTN_BLOCKS):
            items.append((sources[w][:, c0:c0 + BLK], BLK, centred, ty, b))
        for w, src in enumerate((w1T, w3T)):
            for b in range(NB):
                n = min(BLK, FI - BLK * b)
                items.append((src[:, BLK * b:BLK * b + n], n, False, None, (w, b)))
        NI = len(items)

        def parts(k, part, c):
            _, n, _, ty, d = items[k]
            if ty is not None:
                return [(w_attn[:, d, part, c, :], 0, BLK)]
            w, b = d
            return [(w_up[:, 2 * b + u, part, w, c, 0:min(256, n - 256 * u)], 256 * u, min(256, n - 256 * u))
                    for u in range(2) if n > 256 * u]

        def staged(k):
            n = items[k][1]
            return stage[k % 3][:, 0:KC * n].rearrange("p (c n) -> p c n", c=KC)

        def spread_to(q, a, b):
            return bank[Y_BANK if q == 1 else T_BANK[0]][:, P * a:P * b]

        block = es.enter_context(nc.Block())

        @block.sync
        def _(sp):
            sp.dma_start(vec[:, :], vecs).then_inc(s_vec, 16)

            def load_block(k):
                if k >= 3:
                    sp.wait_ge(low_done, k - 2)
                sp.dma_start(staged(k), items[k][0].rearrange("(c p) n -> p c n", p=P)).then_inc(s_stage[k % 3], 16)

            for k in range(NSELF):
                load_block(k)
                if k >= 2:
                    sp.wait_ge(wproj_cast, k - 1)
                sp.dma_start(wp_stage[k % 2].rearrange("p (c n) -> p c n", n=H),
                             wprojT[512 * k:512 * k + 512, :].rearrange("(c p) n -> p c n", p=P)).then_inc(s_wp[k % 2], 16)
                if k == 2:
                    sp.dma_start(xin[:, :], x[0:P, :]).then_inc(x_in, 16)
                    sp.dma_start(cin[:, :], cond[0:P, :]).then_inc(c_in, 16)
                    sp.dma_start(xres[:, :], x[0:P, :]).then_inc(r_in, 16)
            for k in (8, 9, 10):
                load_block(k)
            sp.dma_start(w_kv[:, :, :], wkvT.rearrange("(c p) n -> p c n", p=P)).then_inc(s_wkv, 16)

            def next_input(t):
                after(sp, ln1_step, 6, t, 3)
                sp.dma_start(xin[:, :], x[bass.ts(t + 1, P), :]).then_inc(x_in, 16)

            def condition(t):
                after(sp, c_transposed, 1, t - 1, 1)
                sp.dma_start(cin[:, :], cond[bass.ts(t, P), :]).then_inc(c_in, 16)

            def residual(t):
                after(sp, o_added, 4, t - 1, 4)
                sp.dma_start(xres[:, :], x[bass.ts(t, P), :]).then_inc(r_in, 16)

            def tile_loads(t):
                real = not isinstance(t, int)
                if real or t < TILES:
                    condition(t)
                if real or t < TILES - 1:
                    next_input(t)
                if real or t < TILES:
                    residual(t)
                after(sp, out_ready, 1, t - 2, 1)
                sp.dma_start(out[bass.ts(t - 2, P), :], yout[:, :]).then_inc(out_sent, 16)

            next_input(0)
            sp.dma_start(w_gate[:, :, :], gateT.rearrange("(c p) n -> p c n", p=P)).then_inc(s_wg, 16)
            for k in (11, 12):
                load_block(k)
            condition(1)
            for k in (13, 14):
                load_block(k)
            next_input(1)
            for k in range(15, NI):
                load_block(k)
            full = FI // P
            sp.wait_ge(low_done, NI - 1)
            sp.dma_start(w_down[:, 0:full, :], w2[0:full * P, :].rearrange("(c p) n -> p c n", p=P)).then_inc(s_wd, 16)
            sp.dma_start(w_down[0:FI - full * P, full, :], w2[full * P:FI, :]).then_inc(s_wd, 16)
            residual(1)
            with sp.Fori(2, TILES - 1) as t:
                tile_loads(t)
            for t in (TILES - 1, TILES, TILES + 1):
                tile_loads(t)
            sp.wait_ge(out_sent, 16 * TILES)

        @block.gpsimd
        def _(pool):
            done = [0]

            def made(instruction):
                instruction.then_inc(const_step, 1)
                done[0] += 1
                pool.wait_ge(const_step, done[0])

            made(pool.memset(minus_half[:, :], -0.5))
            for m in (ident, ident16):
                made(pool.memset(m[:, :], 0.0))
                made(pool.affine_select(out=m[:, :], in_=m[:, :], compare_op=ALU.not_equal, fill=1.0, base=0,
                                        pattern=[[-1, P]], channel_multiplier=1))
            made(pool.memset(tri[:, :, :], 1.0))
            made(pool.affine_select(out=tri[:, :, :], in_=tri[:, :, :], compare_op=ALU.is_ge, fill=0.0, base=-1,
                                    pattern=[[1, E], [-1, E]], channel_multiplier=0))
            made(pool.memset(comb3[:, :, :], 0.0))
            made(pool.memset(comb3[:, 0, E:NE], 0.5))
            made(pool.memset(eps_head[:, :, :], P * EPS))
            made(pool.memset(pT[:, :, :, :], 0.0))
            def largest(k):
                pool.wait_ge(peak_step, k + 1)
                pool.partition_all_reduce(peak[:, k:k + 1], rowmax[:, k:k + 1], P, RMAX).then_inc(factor_ready, 1)

            for k in range(NSELF):
                largest(k)
            made(pool.memset(expert_rows[:, :], 1.0))
            for q in range(3):
                rows = expert_rows[32 * q:32 * q + 32, :]
                made(pool.affine_select(out=rows, in_=rows, compare_op=ALU.is_ge, fill=0.0, base=0,
                                        pattern=[[1, 2 * NU * P]], channel_multiplier=-I))
                made(pool.affine_select(out=rows, in_=rows, compare_op=ALU.is_ge, fill=0.0, base=I - 1,
                                        pattern=[[-1, 2 * NU * P]], channel_multiplier=I))

            def power(s, dst, src, per, t, k):
                pool.tensor_scalar(dst, src, 1.0, EPS, ALU.mult, ALU.add).then_inc(s, 1)
                after(pool, s, per, t, k + 1)
                pool.tensor_tensor(dst, dst, minus_half[:, 0:1], ALU.pow).then_inc(s, 1)

            def step(t, j):
                def weigh(place):
                    u, f = UNITS.get((j, place)), t - 2
                    if u is None or not ffn(f):
                        return
                    after(pool, gated, 14, f, 2 * u + 2)
                    after(pool, combs_ready, NB, f, u // 2 + 1)
                    if u >= 2:
                        after(pool, down_done, NU, f, u - 1)
                    else:
                        after(pool, down_done, NU, f - 1, 7)
                    pool.tensor_tensor(act_ff[:, u % 2, :, :], gu[:, :, :], combs[:, 2 * u:2 * u + 2, :],
                                       ALU.mult).then_inc(act_ready, 1)

                if ffn(t - 1) and j == 3:
                    after_apart(pool, ln2_step, 3, t - 1, 2)
                    power(ln2_pow, f_r[:, :], f_mv[:, 1:2], 2, t - 1, 0)
                weigh("early")
                if has(t, j):
                    b = j % 2
                    me, mo = stats[:, b, :, 1], stats[:, b, :, 4]
                    after(pool, stats_done, 4, t, j + 1)
                    t2, j2 = back(t, j, 2)
                    after(pool, xhat_ready, 12, t2, 3 * j2 + 3)
                    k = 7 * j
                    pool.tensor_tensor(st_a[:, :], stats[:, b, :, 2], stats[:, b, :, 5], ALU.add).then_inc(rstd_step, 1)
                    pool.tensor_tensor(st_b[:, :], me, mo, ALU.subtract).then_inc(rstd_step, 1)
                    after(pool, rstd_step, 28, t, k + 1)
                    pool.tensor_tensor(st_a[:, :], st_a[:, :], eps_head[:, j, :], ALU.add).then_inc(rstd_step, 1)
                    after(pool, rstd_step, 28, t, k + 2)
                    pool.tensor_tensor(st_b[:, :], st_b[:, :], st_b[:, :], ALU.mult).then_inc(rstd_step, 1)
                    after_apart(pool, rstd_step, 28, t, k + 4)
                    pool.tensor_scalar(st_b[:, :], st_b[:, :], P / 4.0, 0.0, ALU.mult, ALU.add).then_inc(rstd_step, 1)
                    after(pool, rstd_step, 28, t, k + 5)
                    pool.tensor_tensor(st_a[:, :], st_a[:, :], st_b[:, :], ALU.add).then_inc(rstd_step, 1)
                    after(pool, rstd_step, 28, t, k + 6)
                    pool.tensor_tensor(rstd[:, b, :], st_a[:, :], minus_half[:, :], ALU.pow).then_inc(rstd_step, 1)
                t1, j1 = back(t, j, 1)
                if has(t1, j1):
                    after(pool, exp_done, 4, t1, j1 + 1)
                    after(pool, soft_step, 16, t1, 4 * j1 + 4)
                    t2, j2 = back(t, j, 2)
                    after(pool, p_transposed, 4, t2, j2 + 1)
                    pool.tensor_tensor(probs[:, :, :].rearrange("p g (b t) -> p (g b) t", b=2), ex[:, :, :],
                                       rinv[:, :].unsqueeze(2).broadcast_to([P, 8, 64]), ALU.mult).then_inc(p_ready, 1)
                weigh("mid")
                weigh("late")
                if has(t + 1) and j == 0:
                    after_apart(pool, ln1_step, 6, t + 1, 2)
                    power(ln1_pow, ln_r[:, :], ln_mv[:, 1:2], 4, t + 1, 0)
                if has(t + 1) and j == 1:
                    after_apart(pool, ln1_step, 6, t + 1, 5)
                    power(ln1_pow, ln_r[:, :], ln_mv[:, 1:2], 4, t + 1, 2)
                if ffn(t - 1) and j == 3:
                    after(pool, o_added, 4, t - 1, 4)
                    after_apart(pool, out_ready, 1, t - 2, 1)
                    pool.tensor_copy(x1keep[:, :], x1[:, :]).then_inc(x1_kept, 1)
                if isinstance(t, int):
                    for k in LATER.get((t, j), ()):
                        largest(k)

            run(pool, step)

        @block.scalar
        def _(act):
            act.wait_ge(pad_zeroed, 2)
            def high(k):
                act.wait_ge(fac_step, 3 * k + 3)
                for c in range(KC):
                    for dst, c0, n in parts(k, 0, c):
                        last = act.activation(dst, staged(k)[:, c, c0:c0 + n], ACT.Copy, scale=factor[:, k, c:c + 1])
                last.then_inc(high_done, 1)

            for k in range(NSELF):
                high(k)
                act.wait_ge(s_wp[k % 2], 16 * (k // 2 + 1))
                act.activation(w_proj[:, 4 * k:4 * k + 4, :].rearrange("p c n -> p (c n)"), wp_stage[k % 2],
                               ACT.Copy).then_inc(wproj_cast, 1)
            act.wait_ge(wproj_cast, 8)
            act.wait_ge(tab_step, 6)
            act.wait_ge(const_step, 11)

            def step(t, j):
                b = j % 2
                t1, j1 = back(t, j, 1)
                t2, j2 = back(t, j, 2)
                cross1 = j1 >= 2

                def evac_T(blk):
                    ln = (V_KXLN if cross1 else V_KLN) if blk == 0 else (V_QXLN if cross1 else V_QLN)
                    after(act, qk_transposed, 12, t1, 3 * j1 + blk + 1)
                    if blk == 0:
                        after(act, scores_done, 4, t2, j2 + 1)
                    tb = T_BANK[blk % 2]
                    act.activation(qkT[:, 4 * blk:4 * blk + 4, :].rearrange("p a b -> p (a b)"), bank[tb][:, :],
                                   ACT.Identity, scale=ln_scale[:, (ln - V_QLN) // 2:(ln - V_QLN) // 2 + 1],
                                   bias=vec[:, ln + 1:ln + 2]).then_inc(qkT_ready, 1)

                def evac_raw(blk):
                    after(act, proj_done, 16, t, 4 * j + blk + 1)
                    after(act, qk_transposed, 12, t2, 3 * j2 + blk + 1)
                    act.activation(raw[:, b, 4 * blk:4 * blk + 4, :].rearrange("p a b -> p (a b)"),
                                   bank[P_BANK[blk % 2]][:, :], ACT.Copy).then_inc(raw_ready, 1)

                def evac_values():
                    if not has(t, j):
                        return
                    after(act, proj_done, 16, t, 4 * j + 4)
                    after(act, pv_done, 8, t - 1, 2 * j + 2)
                    sc = sigma[:, 6 + j:7 + j] if j < 2 else 1.0
                    act.activation(vals[:, j, :], bank[P_BANK[1]][:, :], ACT.Copy, scale=sc).then_inc(v_ready, 1)

                def spread_out(q):
                    if q == 0:
                        after(act, act_ready, NU, t - 3, NU)
                    n = min(4, 2 * NU - 4 * q)
                    after(act, spread_done, NB, t - 2, q + 1)
                    act.activation(combs[:, 4 * q:4 * q + n, :].rearrange("p c n -> p (c n)"),
                                   spread_to(q, 0, n), ACT.Copy,
                                   scale=both_up[:, q:q + 1]).then_inc(combs_ready, 1)

                def scale_cat(half):
                    if not has(t2, j2):
                        return
                    after(act, pv_done, 8, t2, 2 * j2 + half + 1)
                    t3, j3 = back(t, j, 3)
                    after(act, quant_step, 20, t3, 5 * j3 + 5)
                    for i in range(4):
                        lc = 4 * half + i
                        last = act.activation(cat[:, lc, :], bank[V_BANK][:, i * P:i * P + P], ACT.Copy,
                                              scale=inv_smooth[:, 8 * j2 + lc:8 * j2 + lc + 1])
                    last.then_inc(cat_scaled, 1)

                def tanh(place):
                    u, f = UNITS.get((j, place)), t - 2
                    if u is None or not ffn(f):
                        return
                    after(act, up_done, NU, f, u + 1)
                    after(act, gated, 14, f, 2 * u)
                    act.activation(th[:, :, :].rearrange("p c n -> p (c n)"), bank[H_BANK][:, 0:256], ACT.Tanh,
                                   scale=half_up[:, u // 2:u // 2 + 1]).then_inc(tanh_done, 1)

                if has(t1, j1):
                    evac_T(0)
                    evac_T(1)
                if has(t, j):
                    evac_raw(0)
                if has(t1, j1):
                    evac_T(2)
                if has(t, j):
                    evac_raw(1)
                if ffn(t - 2) and j == 1:
                    spread_out(1)
                tanh("early")
                if ffn(t - 1) and j == 3:
                    after(act, xn_transposed, 1, t - 1, 1)
                    after(act, gate_done, 1, t - 2, 1)
                    after(act, parts_step, 2, t - 2, 2)
                    act.activation(xnT[:, :, :].rearrange("p c n -> p (c n)"), bank[T_BANK[0]][:, 0:H],
                                   ACT.Copy).then_inc(xnT_ready, 1)
                if has(t + 1) and j == 2:
                    after(act, z_transposed, 1, t + 1, 1)
                    after(act, xx_step, 6, t, 1)
                    after(act, xqkv_step, 6, t, 1)
                    for c in range(KC):
                        last = act.activation(zT[:, c, :], bank[T_BANK[0]][:, c * P:c * P + P], ACT.Identity,
                                              scale=vec[:, V_LNW + c:V_LNW + c + 1], bias=vec[:, V_LNB + c:V_LNB + c + 1])
                    last.then_inc(zT_ready, 1)
                if has(t, j):
                    evac_raw(2)
                if has(t2, j2):
                    after(act, p_transposed, 4, t2, j2 + 1)
                    t3, j3 = back(t, j, 3)
                    after(act, pv_done, 8, t3, 2 * j3 + 2)
                    tb = bank[T_BANK[1]][:, :].rearrange("p (g n) -> p g n", g=4)
                    act.activation(pT[0:64, :, 0, :], tb[0:64], ACT.Copy)
                    act.activation(pT[64:128, :, 1, :], tb[64:128], ACT.Copy).then_inc(pT_ready, 1)
                if has(t) and j == 0:
                    after(act, c_transposed, 1, t, 1)
                    after(act, proj_done, 16, t - 1, 16)
                    act.activation(condT[:, :, :].rearrange("p c n -> p (c n)"), bank[T_BANK[0]][:, 0:H],
                                   ACT.Copy).then_inc(condT_ready, 1)
                if j == 0:
                    scale_cat(0)
                if ffn(t - 2) and j == 0:
                    after(act, comb_transposed, 1, t - 2, 1)
                    after(act, spread_done, NB, t - 3, NB)
                    act.activation(combT[:, :], bank[T_BANK[1]][:, 0:64].bitcast(BF16), ACT.Copy).then_inc(combT_ready, 1)
                if has(t1, j1):
                    after(act, soft_step, 16, t1, 4 * j1 + 2)
                    after(act, p_ready, 4, t2, j2 + 1)
                    act.activation(ex[:, :, :], shifted[:, :, :], ACT.Exp, scale=SCALE).then_inc(exp_done, 1)
                if j > 0:
                    evac_values()

                if j > 0:
                    scale_cat(0)
                tanh("mid")
                if ffn(t - 2) and j == 0:
                    spread_out(0)
                if j == 0:
                    evac_values()
                if ffn(t - 1) and j == 3:
                    after(act, gate_step, 17, t - 1, 2)
                    act.activation(g_ex[:, :], g_sh[:, :], ACT.Exp).then_inc(gexp_done, 1)
                if ffn(t - 2) and j == 1:
                    spread_out(2)
                if ffn(t - 2) and j == 2:
                    spread_out(3)
                scale_cat(1)
                tanh("late")
                if isinstance(t, int):
                    for k in LATER.get((t, j), ()):
                        high(k)

            run(act, step)

        @block.vector
        def _(dve):
            dve.memset(w_up[:, NU - 1, :, :, :, :], 0.0).then_inc(pad_zeroed, 1)
            dve.memset(w_down[96:128, 2 * NU - 1, :], 0.0).then_inc(pad_zeroed, 1)
            dve.wait_ge(s_vec, 16)
            dve.wait_ge(pad_zeroed, 2)

            def measure(k):
                _, n, centred, ty, _ = items[k]
                w = staged(k)
                dve.wait_ge(s_stage[k % 3], 16 * (k // 3 + 1))
                hs = headsum[:, k % 2, :]
                if centred:
                    w8 = w.rearrange("p c (h d) -> p (c h) d", d=P)
                    n = 3 * sum(items[i][2] for i in range(k))
                    dve.tensor_reduce(hs, w8, AX.X, ALU.add).then_inc(prep_centred, 1)
                    dve.wait_ge(prep_centred, n + 1)
                    dve.tensor_scalar(hs, hs, -1.0 / P, None, ALU.mult).then_inc(prep_centred, 1)
                    dve.wait_ge(prep_centred, n + 2)
                    dve.tensor_tensor(w8, w8, hs.unsqueeze(2).broadcast_to([P, 8, P]), ALU.add).then_inc(prep_centred, 1)
                    dve.wait_ge(prep_centred, n + 3)
                dve.tensor_reduce(absmax[:, k, :], w, AX.X, ALU.max, apply_absolute_value=True).then_inc(prep_max, 1)
                dve.wait_ge(prep_max, k + 1)
                if ty is not None:
                    dve.tensor_tensor(absmax[:, k, :], absmax[:, k, :], vec[:, V_IN + 2 * ty:V_IN + 2 * ty + 2],
                                      ALU.mult).then_inc(prep_scaled, 1)
                    dve.wait_ge(prep_scaled, k + 1)
                dve.tensor_reduce(rowmax[:, k:k + 1], absmax[:, k, :], AX.X, ALU.max,
                                  apply_absolute_value=True).then_inc(peak_step, 1)

            def split(k):
                _, n, centred, ty, _ = items[k]
                dve.wait_ge(factor_ready, k + 1)
                dve.tensor_scalar(peak[:, k:k + 1], peak[:, k:k + 1], 1e-30, 1.0 / TOP, ALU.max, ALU.mult).then_inc(fac_step, 1)
                dve.wait_ge(fac_step, 3 * k + 1)
                dve.reciprocal(rowmax[:, k:k + 1], peak[:, k:k + 1]).then_inc(fac_step, 1)
                dve.wait_ge(fac_step, 3 * k + 2)
                if ty is None:
                    dve.tensor_copy(factor[:, k, :], rowmax[:, k:k + 1].broadcast_to([P, KC])).then_inc(fac_step, 1)
                else:
                    dve.tensor_scalar(factor[:, k, :], vec[:, V_IN + 2 * ty:V_IN + 2 * ty + 2], rowmax[:, k:k + 1],
                                      None, ALU.mult).then_inc(fac_step, 1)
                dve.wait_ge(fac_step, 3 * k + 3)

            def low(k):
                dve.wait_ge(high_done, k + 1)
                for c in range(KC):
                    his = parts(k, 0, c)
                    for (dst, c0, n), (hi, _, _) in zip(parts(k, 1, c), his):
                        last = dve.scalar_tensor_tensor(dst, staged(k)[:, c, c0:c0 + n], factor[:, k, c:c + 1], hi,
                                                        ALU.mult, ALU.subtract)
                last.then_inc(low_done, 1)

            measure(0)
            split(0)
            for k in range(NSELF):
                if k + 1 < NSELF:
                    measure(k + 1)
                low(k)
                if k + 1 < NSELF:
                    split(k + 1)

            def centre_keys():
                dve.wait_ge(s_wkv, 16)
                for c in range(KC):
                    w8 = w_kv[:, c, 0:1024].rearrange("p (h d) -> p h d", d=P)
                    dve.tensor_reduce(headsum[:, c, :], w8, AX.X, ALU.add).then_inc(kv_centred, 1)
                dve.wait_ge(kv_centred, 2)
                dve.tensor_scalar(headsum[:, :, :], headsum[:, :, :], -1.0 / P, None, ALU.mult).then_inc(kv_centred, 1)
                dve.wait_ge(kv_centred, 3)
                for c in range(KC):
                    w8 = w_kv[:, c, 0:1024].rearrange("p (h d) -> p h d", d=P)
                    dve.tensor_tensor(w8, w8, headsum[:, c, :].unsqueeze(2).broadcast_to([P, 8, P]), ALU.add)\
                       .then_inc(kv_centred, 1)

            def tables(blocks, quads, n):
                for ty, a, m in blocks:
                    last = dve.tensor_scalar(sigma[:, a:a + m], peak[:, a:a + m], vec[:, V_WS + ty:V_WS + ty + 1], None, ALU.mult)
                a, e = blocks[0][1], blocks[-1][1] + blocks[-1][2]
                last.then_inc(tab_step, 1)
                dve.wait_ge(tab_step, n + 1)
                dve.reciprocal(isig[:, a:e], sigma[:, a:e]).then_inc(tab_step, 1)
                dve.wait_ge(tab_step, n + 2)
                dve.scalar_tensor_tensor(eps_blk[:, a:e], isig[:, a:e], P * EPS, isig[:, a:e], ALU.mult, ALU.mult)\
                   .then_inc(tab_step, 1)
                dve.wait_ge(tab_step, n + 3)
                for j in quads:
                    if j < 2:
                        dve.tensor_copy(eps_head[:, j, 0:4], eps_blk[:, 4 + j:5 + j].broadcast_to([P, 4]))
                    for h in range(2):
                        k = 2 * (j % 2) + h + (8 if j >= 2 else 0)
                        last = dve.tensor_copy(eps_head[:, j, 4 + 4 * h:8 + 4 * h], eps_blk[:, k:k + 1].broadcast_to([P, 4]))
                last.then_inc(tab_step, 1)

            dve.wait_ge(const_step, 11)
            dve.reciprocal(inv_in[:, :], vec[:, V_IN:V_IN + 8])
            dve.reciprocal(inv_smooth[:, :], vec[:, V_SMOOTH:V_SMOOTH + 32])
            tables(((TQ, 0, 4), (TK, 4, 2), (TV, 6, 2)), (0, 1), 0)
            dve.tensor_scalar(ln_scale[:, :], vec[:, V_QLN:V_QLN + 8:2], float(P) ** 0.5, None, ALU.mult).then_inc(tab_step, 1)
            dve.tensor_tensor(out_scale[:, :], vec[:, V_PW:V_PW + 1], vec[:, V_PI:V_PI + 1], ALU.mult).then_inc(tab_step, 1)
            dve.wait_ge(tab_step, 6)

            def prepare_later(t, j):
                blocks = LATER.get((t, j), ())
                for k in blocks[1:]:
                    measure(k)
                for k in blocks:
                    split(k)
                for k in blocks:
                    low(k)
                if (t, j) == (0, 0):
                    centre_keys()
                if NA - 1 in blocks:
                    tables(((TX, 8, 4),), (2, 3), 6)
                if NI - 1 in blocks:
                    dve.tensor_scalar(half_up[:, :], peak[:, NA:NA + NB], 0.5, None, ALU.mult).then_inc(tab_step, 1)
                    dve.tensor_tensor(both_up[:, :], peak[:, NA:NA + NB], peak[:, NA + NB:NA + 2 * NB], ALU.mult)\
                       .then_inc(tab_step, 1)

            def norm_stats(s, per, t, k, src, stat, mv):
                dve.bn_stats(stat[:, :], src[:, :]).then_inc(s, 1)
                after_apart(dve, s, per, t, k + 1)
                dve.bn_aggr(mv[:, :], stat[:, :]).then_inc(s, 1)

            def quantise(s, t, src, mask, dst, per, k, wait_dst):
                def clip():
                    dve.tensor_scalar(src, src, FP8_MAX, -FP8_MAX, ALU.min, ALU.max).then_inc(s, 1)

                def binade():
                    after(dve, s, per, t, k + 1)
                    dve.tensor_scalar(mask.bitcast(U16), src.bitcast(U16), 0x7F80, None, ALU.bitwise_and).then_inc(s, 1)

                def magic():
                    after(dve, s, per, t, k + 2)
                    dve.tensor_scalar(mask, mask, FP8_MIN_NORMAL, ROUND3, ALU.max, ALU.mult).then_inc(s, 1)

                def push():
                    after(dve, s, per, t, k + 3)
                    dve.tensor_tensor(src, src, mask, ALU.add).then_inc(s, 1)

                def pull():
                    after(dve, s, per, t, k + 4)
                    wait_dst()
                    dve.tensor_tensor(dst, src, mask, ALU.subtract).then_inc(s, 1)
                return clip, binade, magic, push, pull

            def step(t, j):
                b = j % 2
                t1, j1 = back(t, j, 1)
                t2, j2 = back(t, j, 2)
                t3, j3 = back(t, j, 3)
                flat = "p a b -> p (a b)"

                def nothing():
                    return None

                clip = binade = magic = push = pull = nothing
                if has(t3, j3):
                    t4, j4 = back(t, j, 4)
                    clip, binade, magic, push, pull = quantise(
                        quant_step, t3, cat[:, :, :].rearrange(flat), catm[:, :, :].rearrange(flat),
                        catq[:, :, :].rearrange(flat), 20, 5 * j3,
                        lambda: after(dve, o_done, 4, t4, j4 + 1))

                def head_stats(blk):
                    if not has(t, j):
                        return
                    after(dve, raw_ready, 12, t, 3 * j + blk + 1)
                    if blk == 0:
                        after(dve, rstd_step, 28, t2, 7 * j2 + 7)
                    for h in range(4 * blk, 4 * blk + 4):
                        last = dve.bn_stats(stats[:, b, h, :], raw[:, b, h, :])
                    if blk == 2:
                        last.then_inc(stats_done, 1)

                def normalise(blk):
                    if not has(t, j):
                        return
                    if blk == 0:
                        after(dve, rstd_step, 28, t, 7 * j + 7)
                    r = raw[:, b, 4 * blk:4 * blk + 4, :]
                    dve.tensor_tensor(r, r, rstd[:, b, 4 * blk:4 * blk + 4].unsqueeze(2).broadcast_to([P, 4, P]),
                                      ALU.mult).then_inc(xhat_ready, 1)

                f = t - 1
                routing = ffn(f) and j == 3
                lg = bank[H_BANK][:, 256:256 + E]
                sc_f = g_sc[:, :].unsqueeze(1).broadcast_to([P, E, E])
                sc_e = g_sc[:, :].unsqueeze(2).broadcast_to([P, E, E])
                sc = bank[S_BANK][:, :].rearrange("p (g t) -> p g t", t=64)

                def gate_unit(place):
                    u, fu = UNITS.get((j, place)), t - 2
                    if u is None or not ffn(fu):
                        return
                    after(dve, tanh_done, NU, fu, u + 1)
                    if u == 0:
                        after(dve, act_ready, NU, fu - 1, NU)
                    else:
                        after(dve, act_ready, NU, fu, u)
                    dve.scalar_tensor_tensor(gu[:, :, :].rearrange(flat), th[:, :, :].rearrange(flat), 1.0,
                                             bank[H_BANK][:, 0:256], ALU.add, ALU.mult).then_inc(gated, 1)
                    after(dve, gated, 14, fu, 2 * u + 1)
                    dve.tensor_tensor(gu[:, :, :].rearrange(flat), gu[:, :, :].rearrange(flat),
                                      bank[H_BANK][:, 256:512], ALU.mult).then_inc(gated, 1)

                def scaled_input(ty):
                    for c in range(KC):
                        last = dve.tensor_scalar(xs[:, ty, c, :], zT[:, c, :], inv_in[:, 2 * ty + c:2 * ty + c + 1], None, ALU.mult)
                    return last

                xclip = xbinade = xmagic = xpush = xpull = nothing
                if has(t + 1) and j == 2:
                    whole = "p a b c -> p (a b c)"
                    xclip, xbinade, xmagic, xpush, xpull = quantise(
                        xqkv_step, t + 1, xs[:, 0:3].rearrange(whole), xm[:, 0:3].rearrange(whole),
                        xq[:, 0:3].rearrange(whole), 6, 1, lambda: after(dve, proj_done, 16, t, 8))
                if has(t) and j == 1:
                    xclip, xbinade, xmagic, xpush, xpull = quantise(
                        xx_step, t, xs[:, 3].rearrange(flat), xm[:, 3].rearrange(flat),
                        xq[:, 3].rearrange(flat), 6, 1, lambda: after(dve, proj_done, 16, t - 1, 16))

                due = ffn(t - 2) and j == 0

                def rank_greater():
                    if due:
                        after(dve, gate_step, 17, t - 2, 5)
                        dve.tensor_tensor(g_gt[:, :, :], sc_f, sc_e, ALU.is_gt).then_inc(gate_step, 1)

                def rank_equal():
                    if due:
                        dve.tensor_tensor(g_eq[:, :, :], sc_f, sc_e, ALU.is_equal).then_inc(gate_step, 1)

                def rank_before():
                    if due:
                        after(dve, gate_step, 17, t - 2, 7)
                        dve.tensor_tensor(g_eq[:, :, :], g_eq[:, :, :], tri[:, :, :], ALU.mult).then_inc(gate_step, 1)

                def rank_ahead():
                    if due:
                        after(dve, gate_step, 17, t - 2, 8)
                        dve.tensor_tensor(g_gt[:, :, :], g_gt[:, :, :], g_eq[:, :, :], ALU.add).then_inc(gate_step, 1)

                def rank_sum():
                    if due:
                        after(dve, gate_step, 17, t - 2, 9)
                        dve.tensor_reduce(g_rank[:, :], g_gt[:, :, :], AX.X, ALU.add).then_inc(gate_step, 1)

                def select():
                    if due:
                        after(dve, gate_step, 17, t - 2, 10)
                        dve.scalar_tensor_tensor(g_sel[:, :], g_rank[:, :], 1.5, g_sc[:, :], ALU.is_lt,
                                                 ALU.mult).then_inc(gate_step, 1)

                def select_sum():
                    if due:
                        after(dve, gate_step, 17, t - 2, 11)
                        dve.tensor_reduce(g_col[:, 3:4], g_sel[:, :], AX.X, ALU.add).then_inc(gate_step, 1)

                def select_inverse():
                    if due:
                        after(dve, gate_step, 17, t - 2, 12)
                        dve.reciprocal(g_col[:, 4:5], g_col[:, 3:4]).then_inc(gate_step, 1)

                def weights():
                    if due:
                        after(dve, gate_step, 17, t - 2, 13)
                        dve.tensor_scalar(comb[:, :], g_sel[:, :], g_col[:, 4:5], 0.5, ALU.mult, ALU.mult).then_inc(gate_step, 1)

                def weights_high():
                    if due:
                        after(dve, gate_step, 17, t - 2, 14)
                        after(dve, comb_transposed, 1, t - 3, 1)
                        dve.tensor_copy(comb3[:, 0, 0:E], comb[:, :]).then_inc(gate_step, 1)

                def weights_rest():
                    if due:
                        after(dve, gate_step, 17, t - 2, 15)
                        dve.tensor_tensor(rest[:, :], comb[:, :], comb3[:, 0, 0:E], ALU.subtract).then_inc(gate_step, 1)

                def weights_middle():
                    if due:
                        after(dve, gate_step, 17, t - 2, 16)
                        dve.tensor_copy(comb3[:, 1, 0:E], rest[:, :]).then_inc(gate_step, 1)

                def weights_low():
                    if due:
                        after(dve, gate_step, 17, t - 2, 17)
                        dve.tensor_tensor(comb3[:, 2, 0:E], rest[:, :], comb3[:, 1, 0:E], ALU.subtract).then_inc(comb3_ready, 1)

                rank_greater()
                rank_equal()
                if has(t3, j3):
                    after(dve, cat_scaled, 8, t3, 2 * j3 + 2)
                clip()
                rank_before()
                if has(t + 1) and j == 1:
                    after(dve, ln1_pow, 4, t + 1, 2)
                    dve.tensor_scalar(yln[:, :], xin[:, :], ln_mv[:, 0:1], ln_r[:, :], ALU.subtract, ALU.mult).then_inc(ln1_step, 1)
                if has(t + 1) and j == 2:
                    after(dve, ln1_pow, 4, t + 1, 4)
                    after(dve, z_transposed, 1, t, 1)
                    dve.tensor_scalar(zln[:, :], yln[:, :], ln_mv[:, 0:1], ln_r[:, :], ALU.subtract, ALU.mult).then_inc(ln1_step, 1)
                binade()
                if routing:
                    after(dve, ln2_pow, 2, f, 2)
                    after(dve, xn_transposed, 1, f - 1, 1)
                    dve.tensor_scalar(xn[:, :], x1[:, :], f_mv[:, 0:1], f_r[:, :], ALU.subtract, ALU.mult).then_inc(ln2_step, 1)
                rank_ahead()
                magic()
                rank_sum()
                if has(t + 1) and j == 1:
                    after(dve, ln1_step, 6, t + 1, 3)
                    dve.bn_stats(ln_stat[:, :], yln[:, :]).then_inc(ln1_step, 1)
                if j > 0:
                    push()
                if has(t + 1) and j == 1:
                    after_apart(dve, ln1_step, 6, t + 1, 4)
                    dve.bn_aggr(ln_mv[:, :], ln_stat[:, :]).then_inc(ln1_step, 1)
                select()
                if j > 0:
                    pull()
                head_stats(0)
                select_sum()
                head_stats(1)
                select_inverse()
                gate_unit("early")
                head_stats(2)
                weights()
                if j == 0:
                    push()
                    weights_high()
                    pull()
                weights_rest()
                if isinstance(t, int) and (t, j) in LATER:
                    measure(LATER[t, j][0])
                if routing:
                    after(dve, xnT_ready, 1, f, 1)
                    after(dve, up_done, NU, f - 1, NU)
                    dve.tensor_copy(xnp[:, 0, :, :], xnT[:, :, :]).then_inc(parts_step, 1)
                if has(t1, j1):
                    after(dve, scores_done, 4, t1, j1 + 1)
                    dve.tensor_reduce(smax[:, :], sc, AX.X, ALU.max).then_inc(soft_step, 1)
                weights_middle()
                if routing:
                    after(dve, parts_step, 2, f, 1)
                    dve.tensor_tensor(xnp[:, 1, :, :], xnT[:, :, :], xnp[:, 0, :, :], ALU.subtract).then_inc(parts_step, 1)
                if has(t1, j1):
                    after(dve, soft_step, 16, t1, 4 * j1 + 1)
                    after(dve, exp_done, 4, t2, j2 + 1)
                    dve.tensor_tensor(shifted[:, :, :], sc, smax[:, :].unsqueeze(2).broadcast_to([P, 8, 64]),
                                      ALU.subtract).then_inc(soft_step, 1)
                weights_low()
                if has(t + 1) and j == 0:
                    after(dve, x_in, 16, t + 1, 16)
                    after(dve, ln1_pow, 4, t, 3)
                    after(dve, ln1_step, 6, t, 6)
                    norm_stats(ln1_step, 6, t + 1, 0, xin, ln_stat, ln_mv)
                if j == 0:
                    normalise(0)
                    normalise(1)
                    normalise(2)
                if has(t) and j == 1:
                    after(dve, zT_ready, 1, t, 1)
                    scaled_input(TX).then_inc(xx_step, 1)
                if has(t + 1) and j == 2:
                    after(dve, zT_ready, 1, t + 1, 1)
                    for ty in (TQ, TK, TV):
                        last = scaled_input(ty)
                    last.then_inc(xqkv_step, 1)
                if routing:
                    after(dve, gate_done, 1, f, 1)
                    dve.tensor_reduce(g_col[:, 0:1], lg, AX.X, ALU.max).then_inc(gate_step, 1)
                if has(t1, j1):
                    after(dve, exp_done, 4, t1, j1 + 1)
                    after(dve, p_ready, 4, t2, j2 + 1)
                    dve.tensor_reduce(rsum[:, :], ex[:, :, :], AX.X, ALU.add).then_inc(soft_step, 1)
                if routing:
                    after(dve, gate_step, 17, f, 1)
                    dve.tensor_scalar(g_sh[:, :], lg, g_col[:, 0:1], None, ALU.subtract).then_inc(gate_step, 1)
                if has(t + 1) and j == 2:
                    after(dve, xqkv_step, 6, t + 1, 1)
                if has(t) and j == 1:
                    after(dve, xx_step, 6, t, 1)
                xclip()
                if has(t1, j1):
                    after(dve, soft_step, 16, t1, 4 * j1 + 3)
                    dve.reciprocal(rinv[:, :], rsum[:, :]).then_inc(soft_step, 1)
                xbinade()
                gate_unit("mid")
                if j > 0:
                    normalise(0)
                    xmagic()
                    normalise(1)
                    xpush()
                    normalise(2)
                if routing:
                    after(dve, gexp_done, 1, f, 1)
                    dve.tensor_reduce(g_col[:, 1:2], g_ex[:, :], AX.X, ALU.add).then_inc(gate_step, 1)
                if ffn(t - 2) and j == 3:
                    after(dve, down_done, NU, t - 2, NU)
                    after(dve, x1_kept, 1, t - 2, 1)
                    after(dve, out_sent, 16, t - 3, 16)
                    dve.tensor_tensor(yout[:, :], bank[Y_BANK][:, 0:H], x1keep[:, :], ALU.add).then_inc(out_ready, 1)
                if routing:
                    after(dve, gate_step, 17, f, 3)
                    dve.reciprocal(g_col[:, 2:3], g_col[:, 1:2]).then_inc(gate_step, 1)
                    after(dve, gate_step, 17, f, 4)
                    dve.tensor_scalar(g_sc[:, :], g_ex[:, :], g_col[:, 2:3], None, ALU.mult).then_inc(gate_step, 1)
                xpull()
                if has(t3, j3):
                    after(dve, o_done, 4, t3, j3 + 1)
                    if j3 == 0:
                        after(dve, r_in, 16, t3, 16)
                    else:
                        after(dve, o_added, 4, t3, j3)
                    if j3 == 3:
                        after(dve, x1_kept, 1, t3 - 1, 1)
                    dst = x1 if j3 == 3 else xres
                    dve.scalar_tensor_tensor(dst[:, :], bank[S_BANK][:, 0:H], out_scale[:, :], xres[:, :],
                                             ALU.mult, ALU.add).then_inc(o_added, 1)
                gate_unit("late")
                if ffn(f) and j == 2:
                    after(dve, o_added, 4, f, 4)
                    after(dve, ln2_pow, 2, f - 1, 1)
                    norm_stats(ln2_step, 3, f, 0, x1, f_stat, f_mv)

                if isinstance(t, int):
                    prepare_later(t, j)

            run(dve, step)

        @block.tensor
        def _(pe):
            pe.wait_ge(const_step, 11)
            pe.wait_ge(low_done, NSELF)
            pe.wait_ge(wproj_cast, 8)

            def transposes(dst, src, n):
                for i in range(n):
                    last = nc.tensor.transpose(bank[dst][:, i * P:i * P + P], src(i), ident[:, :])
                return last

            def step(t, j):
                b = j % 2
                t1, j1 = back(t, j, 1)
                t2, j2 = back(t, j, 2)
                t3, j3 = back(t, j, 3)
                cross = j >= 2

                def transpose_qk(blk):
                    after(pe, xhat_ready, 12, t1, 3 * j1 + blk + 1)
                    if blk == 0:
                        after(pe, qkT_ready, 12, t2, 3 * j2 + 3)
                        if has(t + 1) and j == 3:
                            after(pe, zT_ready, 1, t + 1, 1)
                        if ffn(t - 2) and j == 0:
                            after(pe, xnT_ready, 1, t - 2, 1)
                        if ffn(t - 2) and j == 1:
                            after(pe, combs_ready, NB, t - 2, 1)
                        if ffn(t - 2) and j == 2:
                            after(pe, combs_ready, NB, t - 2, 3)
                        if ffn(t - 2) and j == 3:
                            after(pe, combs_ready, NB, t - 2, 4)
                        if has(t) and j == 1:
                            after(pe, condT_ready, 1, t, 1)
                    elif blk == 1:
                        after(pe, pT_ready, 4, t3, j3 + 1)
                    else:
                        after(pe, qkT_ready, 12, t1, 3 * j1 + 1)
                    tb = bank[T_BANK[blk % 2]]
                    by_head = tb[:, :].rearrange("p (g b h s) -> p g h b s", g=2, b=2, h=2)
                    for i in range(4):
                        dst = tb[:, i * P:i * P + P] if blk == 0 else by_head[:, i // 2, i % 2]
                        last = nc.tensor.transpose(dst, raw[:, 1 - b, 4 * blk + i, :], ident[:, :])
                    last.then_inc(qk_transposed, 1)

                def project(blk):
                    if blk == 0:
                        after(pe, raw_ready, 12, t1, 3 * j1 + 3)
                        if j == 0:
                            after(pe, xqkv_step, 6, t, 6)
                        if j == 2:
                            after(pe, condT_ready, 1, t, 1)
                            after(pe, xx_step, 6, t, 6)
                    elif blk == 1:
                        after(pe, v_ready, 4, t1, j1 + 1)
                    else:
                        after(pe, raw_ready, 12, t, 3 * j + blk - 1)
                    dst = bank[P_BANK[blk % 2]][:, :]
                    if cross and blk in (0, 3):
                        c0 = (1024 if blk == 3 else 0) + 512 * (j % 2)
                        for c in range(KC):
                            last = nc.tensor.matmul(dst, condT[:, c, :], w_kv[:, c, c0:c0 + BLK],
                                                    start=(c == 0), stop=(c == KC - 1))
                    else:
                        h = j % 2
                        ty, w = {0: (TK, 4 + h), 3: (TV, 6 + h)}.get(blk, (None, None))
                        if ty is None:
                            ty, w = (TX, 8 + 2 * h + blk - 1) if cross else (TQ, 2 * h + blk - 1)
                        for c in range(KC):
                            for part in range(2):
                                last = nc.tensor.matmul(dst, xq[:, ty, c, :], w_attn[:, w, part, c, :],
                                                        start=(c == 0 and part == 0), stop=(c == KC - 1 and part == 1))
                    last.then_inc(proj_done, 1)

                def values(half):
                    if half == 0:
                        after(pe, pT_ready, 4, t2, j2 + 1)
                        after(pe, v_ready, 4, t2, j2 + 1)
                        after(pe, cat_scaled, 8, t3, 2 * j3 + 2)
                    else:
                        after(pe, cat_scaled, 8, t2, 2 * j2 + 1)
                    for i in range(2):
                        g = 2 * half + i
                        last = nc.tensor.matmul(bank[V_BANK][:, 256 * i:256 * i + 256], vals[:, j2, g * P:g * P + P],
                                                pT[:, g, :, :].rearrange("p b (h s) -> p h b s", h=2),
                                                start=True, stop=True)
                    last.then_inc(pv_done, 1)

                def up(u):
                    fu = t - 2
                    if u == 0:
                        after(pe, gate_step, 17, fu, 2)
                        after(pe, parts_step, 2, fu, 2)
                    else:
                        after(pe, gated, 14, fu, 2 * u)
                    for w in range(2):
                        for ch in range(2):
                            dst = bank[H_BANK][:, 256 * w + P * ch:256 * w + P * ch + P]
                            n = 0
                            for c in range(KC):
                                for wp, xp in ((0, 0), (0, 1), (1, 0)):
                                    last = nc.tensor.matmul(dst, w_up[:, u, wp, w, c, P * ch:P * ch + P], xnp[:, xp, c, :],
                                                            start=(n == 0), stop=(n == 5))
                                    n += 1
                    last.then_inc(up_done, 1)

                def down(u):
                    fu = t - 2
                    after(pe, act_ready, NU, fu, u + 1)
                    if u == 0:
                        after(pe, combs_ready, NB, fu, 2)
                    for ch in range(2):
                        last = nc.tensor.matmul(bank[Y_BANK][:, 0:H], act_ff[:, u % 2, ch, :], w_down[:, 2 * u + ch, :],
                                                start=(u == 0 and ch == 0), stop=(u == NU - 1 and ch == 1))
                    last.then_inc(down_done, 1)

                def spread(q):
                    if q == 0:
                        after(pe, combT_ready, 1, t - 2, 1)
                        after(pe, qkT_ready, 12, t1, 3 * j1 + 3)
                        after(pe, xnT_ready, 1, t - 2, 1)
                        if has(t):
                            after(pe, condT_ready, 1, t, 1)
                    elif q == 1:
                        after(pe, out_ready, 1, t - 3, 1)
                    elif q == 2:
                        after(pe, combs_ready, NB, t - 2, 1)
                        after(pe, qkT_ready, 12, t1, 3 * j1 + 3)
                    elif q == 3:
                        after(pe, combs_ready, NB, t - 2, 3)
                        after(pe, qkT_ready, 12, t1, 3 * j1 + 3)
                        if has(t + 1):
                            after(pe, zT_ready, 1, t + 1, 1)
                    for i in range(4 * q, min(4 * q + 4, 2 * NU)):
                        last = nc.tensor.matmul(spread_to(q, i % 4, i % 4 + 1),
                                                expert_rows[:, P * i:P * i + P], combT[:, :], start=True, stop=True)
                    last.then_inc(spread_done, 1)

                def feed(place):
                    u = UNITS.get((j, place))
                    if ffn(t - 2) and u is not None:
                        up(u)
                        if u > 0:
                            down(u - 1)

                if isinstance(t, int) and (t, j) == (0, 2):
                    pe.wait_ge(kv_centred, 5)
                    pe.wait_ge(low_done, NA)
                if isinstance(t, int) and (t, j) == (2, 1):
                    pe.wait_ge(s_wd, 32)
                if isinstance(t, int) and (t, j) == (1, 3):
                    pe.wait_ge(s_wg, 16)
                    pe.wait_ge(low_done, NI)
                    pe.wait_ge(const_step, 18)
                if has(t1, j1):
                    transpose_qk(0)
                    transpose_qk(1)
                if has(t, j):
                    project(0)
                if has(t1, j1):
                    transpose_qk(2)
                if has(t, j):
                    project(1)
                feed("early")
                if ffn(t - 1) and j == 3:
                    after(pe, ln2_step, 3, t - 1, 3)
                    after(pe, combs_ready, NB, t - 2, NB)
                    after(pe, qkT_ready, 12, t1, 3 * j1 + 3)
                    transposes(T_BANK[0], lambda i: xn[:, i * P:i * P + P], 2).then_inc(xn_transposed, 1)
                if has(t + 1) and j == 2:
                    after(pe, ln1_step, 6, t + 1, 6)
                    after(pe, qkT_ready, 12, t1, 3 * j1 + 3)
                    transposes(T_BANK[0], lambda i: zln[:, i * P:i * P + P], 2).then_inc(z_transposed, 1)
                if has(t, j):
                    project(2)
                if has(t2, j2):
                    after(pe, p_ready, 4, t2, j2 + 1)
                    after(pe, qkT_ready, 12, t1, 3 * j1 + 2)
                    transposes(T_BANK[1], lambda i: probs[:, i, :], 4).then_inc(p_transposed, 1)
                if has(t1, j1):
                    after(pe, qkT_ready, 12, t1, 3 * j1 + 3)
                    t4, j4 = back(t, j, 4)
                    after(pe, o_added, 4, t4, j4 + 1)
                    for g in range(4):
                        for bt in range(2):
                            last = nc.tensor.matmul(bank[S_BANK][:, P * g + 64 * bt:P * g + 64 * bt + 64],
                                                    qkT[:, 4 + 2 * g + bt, :],
                                                    qkT[:, g, 64 * bt:64 * bt + 64], start=True, stop=True)
                    last.then_inc(scores_done, 1)
                if has(t, j):
                    project(3)
                if has(t) and j == 0:
                    after(pe, c_in, 16, t, 16)
                    after(pe, qkT_ready, 12, t1, 3 * j1 + 3)
                    transposes(T_BANK[0], lambda i: cin[:, i * P:i * P + P], 2).then_inc(c_transposed, 1)
                if has(t2, j2):
                    values(0)
                if ffn(t - 1) and j == 3:
                    after(pe, xnT_ready, 1, t - 1, 1)
                    after(pe, gated, 14, t - 2, 14)
                    for c in range(KC):
                        last = nc.tensor.matmul(bank[H_BANK][:, 256:256 + E], xnT[:, c, :], w_gate[:, c, :],
                                                start=(c == 0), stop=(c == KC - 1))
                    last.then_inc(gate_done, 1)
                if ffn(t - 2) and j == 3:
                    down(NU - 1)
                feed("mid")
                if ffn(t - 2) and j == 0:
                    after(pe, comb3_ready, 1, t - 2, 1)
                    after(pe, pT_ready, 4, t2, j2 + 1)
                    nc.tensor.transpose(bank[T_BANK[1]][:, 0:64].bitcast(BF16), comb3[:, :, :].rearrange("p a b -> p (a b)"),
                                        ident16[:, :]).then_inc(comb_transposed, 1)
                if ffn(t - 2) and j == 1:
                    spread(2)
                if has(t2, j2) and j == 3:
                    values(1)
                if has(t3, j3):
                    after(pe, quant_step, 20, t3, 5 * j3 + 5)
                    after(pe, soft_step, 16, t1, 4 * j1 + 2)
                    for i in range(8):
                        last = nc.tensor.matmul(bank[S_BANK][:, 0:H], catq[:, i, :], w_proj[:, 8 * j3 + i, :],
                                                start=(i == 0), stop=(i == 7))
                    last.then_inc(o_done, 1)
                if ffn(t - 2) and j == 0:
                    spread(0)
                    spread(1)
                if ffn(t - 2) and j == 2:
                    spread(3)
                if has(t2, j2) and j != 3:
                    values(1)
                feed("late")

            run(pe, step)


def kernel(**a):
    import numpy as np
    import concourse.bacc as bacc
    from concourse.bass_utils import run_bass_kernel_spmd

    pre = "L0_xattn_"
    ff = "L0_ffn_"
    a = {k: np.asarray(v) for k, v in a.items()}

    def turned(w):
        return np.ascontiguousarray(w.T)

    def inner(w, s):
        return np.ascontiguousarray(np.concatenate([np.transpose(w, (1, 0, 2)).reshape(H, E * I), s], axis=1))

    def column(v):
        return v.reshape(-1, P).T

    def spread(v):
        return np.broadcast_to(v.reshape(1, 1), (P, 1))

    names = ["q_in_scale", "k_in_scale", "v_in_scale", "qx_in_scale", "ln_w", "ln_b", "qln_w", "qln_b", "kln_w", "kln_b",
             "qxln_w", "qxln_b", "kxln_w", "kxln_b", "proj_smooth"]
    scalars = ["wq_scale", "wk_scale", "wv_scale", "wqx_scale", "proj_w_scale", "proj_in_scale"]
    vecs = np.ascontiguousarray(np.concatenate([column(a[pre + n]) for n in names] + [spread(a[pre + n]) for n in scalars],
                                               axis=1))
    arrays = {
        "x": a["x"].reshape(-1, H), "cond": a["ctx_2048"].reshape(-1, H),
        "wqT": turned(a[pre + "wq"]), "wkT": turned(a[pre + "wk"]), "wvT": turned(a[pre + "wv"]),
        "wqxT": turned(a[pre + "wqx"]), "wkvT": turned(a[pre + "w_kv_x"]), "wprojT": turned(a[pre + "wproj"]),
        "w1T": inner(a[ff + "w1"], a[ff + "sw1"]), "w3T": inner(a[ff + "w3"], a[ff + "sw3"]),
        "w2": np.ascontiguousarray(np.concatenate([a[ff + "w2"].reshape(E * I, H), a[ff + "sw2"]], axis=0)),
        "gateT": turned(a[ff + "gate_w"]), "vecs": vecs,
    }
    nc = bacc.Bacc("TRN2", target_bir_lowering=False, num_devices=1)
    args = [nc.dram_tensor(f"in_{n}", v.shape, mybir.dt.from_np(v.dtype), kind="ExternalInput").ap() for n, v in arrays.items()]
    out = nc.dram_tensor("out", (TILES * P, H), F32, kind="ExternalOutput").ap()
    bass_xattn_moe(nc, *args, out)
    r = run_bass_kernel_spmd(nc, [{f"in_{n}": v for n, v in arrays.items()}], core_ids=[0])
    return r.results[0]["out"].reshape(a["x"].shape)
```
